# Optimizing a Trainium2 kernel written in Bass

```python
import numpy as np
import jax
import jax.numpy as jnp

def _softmax(x, axis=-1):
    return jax.nn.softmax(x, axis=axis)

def _gelu(x):
    return jax.nn.gelu(x, approximate=True)

def _silu(x):
    return jax.nn.silu(x)

def _sigmoid(x):
    return jax.nn.sigmoid(x)

def _layernorm(x, axis=-1, eps=1e-05):
    m = jnp.mean(x, axis=axis, keepdims=True)
    v = jnp.var(x, axis=axis, keepdims=True)
    return (x - m) / jnp.sqrt(v + eps)

def _scatter_add(tgt, idx, src, axis=0):
    return tgt.at[idx].add(src)

def _segment_sum(src, seg, n):
    return jax.ops.segment_sum(src, seg, n)
kernel_name = 'mk_adj_ffn_d2_adj_r2_a6a6d9'

def setup_inputs(seed: int=0):
    np.random.seed(seed)
    _w = jnp.asarray

    def _rec_inputs():
        import jax
        import jax.numpy as jnp
        _gk = jax.random.key(seed)
        x = -0.0002928 + 1 * jax.random.normal(jax.random.fold_in(_gk, 1), (32, 256, 128), jnp.float32)
        _a = jax.random.bernoulli(jax.random.fold_in(_gk, 2), 0.03125, (32, 256, 256))
        adj = _a.astype(jnp.int32)
        return (x, adj)
    x, adj = _rec_inputs()

    def _L0_gnn_setup():
        import jax, jax.numpy as jnp
        import numpy as np
        NEG_INF = -1000000000.0
        LEAKY_SLOPE = 0.2
        key = jax.random.key(seed)
        k1, k2, k3, k4, k5 = jax.random.split(key, 5)
        B, N, F_in, F_out = (8, 1024, 128, 128)
        x = jax.random.normal(k1, (B, N, F_in), dtype=jnp.float32)
        adj = jax.random.randint(k2, (B, N, N), 0, 2, dtype=jnp.int32)
        W = jax.random.normal(k3, (F_out, F_in), dtype=jnp.float32) * 0.05
        a_src = jax.random.normal(k4, (F_out,), dtype=jnp.float32) * 0.05
        a_dst = jax.random.normal(k5, (F_out,), dtype=jnp.float32) * 0.05
        return {'x': x, 'adj': adj, 'W': W, 'a_src': a_src, 'a_dst': a_dst}
    _L0_gnn_all = _L0_gnn_setup()
    _L0_gnn_in = {k: v for k, v in _L0_gnn_all.items() if k in ('W', 'a_src', 'a_dst')}
    del _L0_gnn_all

    def _L0_ffn_setup():
        import jax, jax.numpy as jnp
        import numpy as np
        B, S, D, E, H, K = (4, 2048, 128, 8, 256, 2)
        key = jax.random.key(seed)
        ks = jax.random.split(key, 6)
        x = jax.random.normal(ks[0], (B, S, D), jnp.float32)
        Wg = jax.random.normal(ks[1], (D, E), jnp.float32) * 0.02
        bg = jnp.zeros((E,), jnp.float32)
        W1 = jax.random.normal(ks[2], (E, D, H), jnp.float32) * 0.02
        b1 = jnp.zeros((E, H), jnp.float32)
        W2 = jax.random.normal(ks[3], (E, H, D), jnp.float32) * 0.02
        b2 = jnp.zeros((E, D), jnp.float32)
        return {'x': x, 'Wg': Wg, 'bg': bg, 'W1': W1, 'b1': b1, 'W2': W2, 'b2': b2}
    _L0_ffn_all = _L0_ffn_setup()
    _L0_ffn_in = {k: v for k, v in _L0_ffn_all.items() if k in ('Wg', 'bg', 'W1', 'b1', 'W2', 'b2')}
    del _L0_ffn_all

    def _L1_gnn_setup():
        import jax, jax.numpy as jnp
        import numpy as np
        OUT = 128
        NUM_LAYERS = 3

        def _gru_cell(inp, h, w_ih, w_hh, b_ih, b_hh):
            gi = inp @ w_ih.T + b_ih
            gh = h @ w_hh.T + b_hh
            i_r, i_z, i_n = jnp.split(gi, 3, axis=-1)
            h_r, h_z, h_n = jnp.split(gh, 3, axis=-1)
            r = jax.nn.sigmoid(i_r + h_r)
            z = jax.nn.sigmoid(i_z + h_z)
            n = jnp.tanh(i_n + r * h_n)
            return (1.0 - z) * n + z * h
        key = jax.random.key(seed)
        ks = jax.random.split(key, 8)
        B, N, D = (32, 256, 128)
        x = jax.random.normal(ks[0], (B, N, D), dtype=jnp.float32)
        adj = jax.random.randint(ks[1], (B, N, N), 0, 2, dtype=jnp.int32)
        s = 1.0 / np.sqrt(OUT)
        weight = jax.random.uniform(ks[2], (NUM_LAYERS, OUT, OUT), jnp.float32, -s, s)
        w_ih = jax.random.uniform(ks[3], (3 * OUT, OUT), jnp.float32, -s, s)
        w_hh = jax.random.uniform(ks[4], (3 * OUT, OUT), jnp.float32, -s, s)
        b_ih = jax.random.uniform(ks[5], (3 * OUT,), jnp.float32, -s, s)
        b_hh = jax.random.uniform(ks[6], (3 * OUT,), jnp.float32, -s, s)
        return {'x': x, 'adj': adj, 'weight': weight, 'w_ih': w_ih, 'w_hh': w_hh, 'b_ih': b_ih, 'b_hh': b_hh}
    _L1_gnn_all = _L1_gnn_setup()
    _L1_gnn_in = {k: v for k, v in _L1_gnn_all.items() if k in ('weight', 'w_ih', 'w_hh', 'b_ih', 'b_hh')}
    del _L1_gnn_all

    def _L1_ffn_setup():
        import jax, jax.numpy as jnp
        import numpy as np
        TOP_K = 2
        LN_EPS = 1e-05
        key = jax.random.key(seed)
        ks = jax.random.split(key, 8)
        B, S, D, E, H = (16, 512, 128, 8, 512)
        x = jax.random.normal(ks[0], (B, S, D), dtype=jnp.float32)
        Wr = jax.random.normal(ks[1], (D, E), dtype=jnp.float32) * 0.1
        br = jnp.zeros((E,), dtype=jnp.float32)
        ln_g = jnp.ones((E, D), dtype=jnp.float32)
        ln_b = jnp.zeros((E, D), dtype=jnp.float32)
        W1 = jax.random.normal(ks[2], (E, D, H), dtype=jnp.float32) * (1.0 / np.sqrt(D))
        b1 = jnp.zeros((E, H), dtype=jnp.float32)
        W2 = jax.random.normal(ks[3], (E, H, D), dtype=jnp.float32) * (1.0 / np.sqrt(H))
        b2 = jnp.zeros((E, D), dtype=jnp.float32)
        return {'x': x, 'Wr': Wr, 'br': br, 'ln_g': ln_g, 'ln_b': ln_b, 'W1': W1, 'b1': b1, 'W2': W2, 'b2': b2}
    _L1_ffn_all = _L1_ffn_setup()
    _L1_ffn_in = {k: v for k, v in _L1_ffn_all.items() if k in ('Wr', 'br', 'ln_g', 'ln_b', 'W1', 'b1', 'W2', 'b2')}
    del _L1_ffn_all
    return {'x': x, 'adj': adj, 'L0_gnn_W': _L0_gnn_in['W'], 'L0_gnn_a_src': _L0_gnn_in['a_src'], 'L0_gnn_a_dst': _L0_gnn_in['a_dst'], 'L0_ffn_Wg': _L0_ffn_in['Wg'], 'L0_ffn_bg': _L0_ffn_in['bg'], 'L0_ffn_W1': _L0_ffn_in['W1'], 'L0_ffn_b1': _L0_ffn_in['b1'], 'L0_ffn_W2': _L0_ffn_in['W2'], 'L0_ffn_b2': _L0_ffn_in['b2'], 'L1_gnn_weight': _L1_gnn_in['weight'], 'L1_gnn_w_ih': _L1_gnn_in['w_ih'], 'L1_gnn_w_hh': _L1_gnn_in['w_hh'], 'L1_gnn_b_ih': _L1_gnn_in['b_ih'], 'L1_gnn_b_hh': _L1_gnn_in['b_hh'], 'L1_ffn_Wr': _L1_ffn_in['Wr'], 'L1_ffn_br': _L1_ffn_in['br'], 'L1_ffn_ln_g': _L1_ffn_in['ln_g'], 'L1_ffn_ln_b': _L1_ffn_in['ln_b'], 'L1_ffn_W1': _L1_ffn_in['W1'], 'L1_ffn_b1': _L1_ffn_in['b1'], 'L1_ffn_W2': _L1_ffn_in['W2'], 'L1_ffn_b2': _L1_ffn_in['b2']}

def reference(x, adj, L0_gnn_W, L0_gnn_a_src, L0_gnn_a_dst, L0_ffn_Wg, L0_ffn_bg, L0_ffn_W1, L0_ffn_b1, L0_ffn_W2, L0_ffn_b2, L1_gnn_weight, L1_gnn_w_ih, L1_gnn_w_hh, L1_gnn_b_ih, L1_gnn_b_hh, L1_ffn_Wr, L1_ffn_br, L1_ffn_ln_g, L1_ffn_ln_b, L1_ffn_W1, L1_ffn_b1, L1_ffn_W2, L1_ffn_b2):
    import jax
    import jax.numpy as jnp

    def _L0_gnn_ref(x, adj, W, a_src, a_dst):
        import jax, jax.numpy as jnp
        import numpy as np
        NEG_INF = -1000000000.0
        LEAKY_SLOPE = 0.2
        h = jnp.einsum('bnf,of->bno', x, W)
        s_src = h @ a_src
        s_dst = h @ a_dst
        e = s_src[:, :, None] + s_dst[:, None, :]
        e = jax.nn.leaky_relu(e, negative_slope=LEAKY_SLOPE)
        e = jnp.where(adj == 0, jnp.float32(NEG_INF), e)
        alpha = jax.nn.softmax(e, axis=-1)
        h_prime = jnp.einsum('bij,bjo->bio', alpha, h)
        return h_prime

    def _L0_ffn_ref(x, Wg, bg, W1, b1, W2, b2):
        import jax, jax.numpy as jnp
        import numpy as np
        B, S, D, E, H, K = (4, 2048, 128, 8, 256, 2)
        Bv, Sv, Dv = x.shape
        gate_scores = x @ Wg + bg
        _, idx = jax.lax.top_k(gate_scores, K)
        mask = jax.nn.one_hot(idx, E, dtype=x.dtype).sum(axis=-2)
        xf = x.reshape(-1, Dv)
        mf = mask.reshape(-1, E)
        h = jax.nn.gelu(jnp.einsum('td,edh->teh', xf, W1) + b1[None], approximate=False)
        y = jnp.einsum('teh,ehd->ted', h, W2) + b2[None]
        out = jnp.einsum('ted,te->td', y, mf)
        return out.reshape(Bv, Sv, Dv)

    def _L1_gnn_ref(x, adj, weight, w_ih, w_hh, b_ih, b_hh):
        import jax, jax.numpy as jnp
        import numpy as np
        OUT = 128
        NUM_LAYERS = 3

        def _gru_cell(inp, h, w_ih, w_hh, b_ih, b_hh):
            gi = inp @ w_ih.T + b_ih
            gh = h @ w_hh.T + b_hh
            i_r, i_z, i_n = jnp.split(gi, 3, axis=-1)
            h_r, h_z, h_n = jnp.split(gh, 3, axis=-1)
            r = jax.nn.sigmoid(i_r + h_r)
            z = jax.nn.sigmoid(i_z + h_z)
            n = jnp.tanh(i_n + r * h_n)
            return (1.0 - z) * n + z * h
        A = (adj != 0).astype(x.dtype)
        h = x
        L = weight.shape[0]
        for i in range(L):
            m = jnp.einsum('bnd,de->bne', h, weight[i])
            aggr = jnp.einsum('bst,bsd->btd', A, m)
            h = _gru_cell(aggr, h, w_ih, w_hh, b_ih, b_hh)
        return h

    def _L1_ffn_ref(x, Wr, br, ln_g, ln_b, W1, b1, W2, b2):
        import jax, jax.numpy as jnp
        import numpy as np
        TOP_K = 2
        LN_EPS = 1e-05
        B, S, D = x.shape
        N = B * S
        xt = x.reshape(N, D)
        logits = xt @ Wr + br
        probs = jax.nn.softmax(logits, axis=-1)
        top_p, top_idx = jax.lax.top_k(probs, TOP_K)
        weights = top_p / top_p.sum(axis=-1, keepdims=True)
        mu = xt.mean(axis=-1, keepdims=True)
        var = ((xt - mu) ** 2).mean(axis=-1, keepdims=True)
        xn = (xt - mu) * jax.lax.rsqrt(var + LN_EPS)
        xe = xn[None, :, :] * ln_g[:, None, :] + ln_b[:, None, :]
        h = jax.nn.gelu(jnp.einsum('end,edh->enh', xe, W1) + b1[:, None, :], approximate=False)
        y = jnp.einsum('enh,ehd->end', h, W2) + b2[:, None, :]
        y_tok = jnp.transpose(y, (1, 0, 2))
        sel = jnp.take_along_axis(y_tok, top_idx[:, :, None], axis=1)
        out = (weights[:, :, None] * sel).sum(axis=1)
        return out.reshape(B, S, D)
    x = x + _L0_gnn_ref(_layernorm(x, axis=-1), adj, L0_gnn_W, L0_gnn_a_src, L0_gnn_a_dst)
    x = x + _L0_ffn_ref(_layernorm(x, axis=-1), L0_ffn_Wg, L0_ffn_bg, L0_ffn_W1, L0_ffn_b1, L0_ffn_W2, L0_ffn_b2)
    x = x + _L1_gnn_ref(_layernorm(x, axis=-1), adj, L1_gnn_weight, L1_gnn_w_ih, L1_gnn_w_hh, L1_gnn_b_ih, L1_gnn_b_hh)
    x = x + _L1_ffn_ref(_layernorm(x, axis=-1), L1_ffn_Wr, L1_ffn_br, L1_ffn_ln_g, L1_ffn_ln_b, L1_ffn_W1, L1_ffn_b1, L1_ffn_W2, L1_ffn_b2)
    return x

_drawn_inputs = setup_inputs


def setup_inputs(seed=0):
    import zlib

    import numpy as np

    out = dict(_drawn_inputs(seed))
    spreads = {'L0_ffn_bg': (0.0, 0.1),
     'L0_ffn_b1': (0.0, 0.1),
     'L0_ffn_b2': (0.0, 0.1),
     'L1_ffn_br': (0.0, 0.1),
     'L1_ffn_ln_g': (1.0, 0.2),
     'L1_ffn_ln_b': (0.0, 0.1),
     'L1_ffn_b1': (0.0, 0.1),
     'L1_ffn_b2': (0.0, 0.1)}
    factors = {}
    for name, (base, spread) in spreads.items():
        noise = np.random.default_rng([zlib.crc32(name.encode()), seed]).standard_normal(out[name].shape)
        drawn = base * np.exp(spread * noise) if base else spread * noise
        out[name] = jnp.asarray(drawn.astype(out[name].dtype))
    for name, factor in factors.items():
        out[name] = (out[name] * factor).astype(out[name].dtype)
    return out
```

```python
import concourse.bass as bass
from concourse import mybir
from concourse.alu_op_type import AluOpType as ALU
from contextlib import ExitStack

F32 = mybir.dt.float32
F32R = mybir.dt.float32r
BF16 = mybir.dt.bfloat16
I32 = mybir.dt.int32
U32 = mybir.dt.uint32
ACT = mybir.ActivationFunctionType
AX = mybir.AxisListType

P = 128
B, N, D = 32, 256, 128
HALVES = N // P
TILES = B * HALVES
E = 8
CH = 512
CT = CH // P
CHUNKS = TILES // CT
HID0, HID1 = 256, 512
LAYERS = 3
NEG_INF = -1e9
SLOPE = 0.2
EPS = 1e-5
U = 4

R_A, R_B1A, R_B1B, R_B2A, R_B2B, R_G, R_B, R_IH, R_HH, R_END = 0, 2, 18, 50, 58, 66, 74, 82, 85, 88
PHASES = 9


def wait(eng, sem, base, off, mul=1, add=0):
    v = base * mul + (off * mul + add)
    if not isinstance(v, int) or v > 0:
        eng.wait_ge(sem, v)


def rounds(eng, n, depth, first, step, U=U):
    for k in range(first):
        step(0, k)
    with eng.Fori(first // U, n // U) as i:
        for u in range(U):
            step(i * U, u)
    for k in range(depth):
        step(n, k)


def live(base, off, n):
    return not isinstance(base, int) or 0 <= base + off < n


UNITS = LAYERS * 4
QUADS = B // 2 // 4


def waitq(eng, sem, i, off, add=0):
    v = i * UNITS + (off + add)
    if not isinstance(v, int) or v > 0:
        eng.wait_ge(sem, v)


def waitp(eng, sem, i, off, add=0):
    v = i * 4 + (off // UNITS * 4 + off % 4 + add)
    if not isinstance(v, int) or v > 0:
        eng.wait_ge(sem, v)


def liveq(i, off):
    return not isinstance(i, int) or 0 <= i * UNITS + off < QUADS * UNITS


def unit_rounds(eng, depth, step):
    for k in range(UNITS):
        step(0, k)
    with eng.Fori(1, QUADS) as i:
        for k in range(UNITS):
            step(i, k)
    for k in range(depth):
        step(QUADS, k)


def build(nc, x, adj, gW, g_src, g_dst, f0_Wg, f0_bg, f0_W1, f0_b1, f0_W2, f0_b2,
          gr_w, gr_wih, gr_whh, gr_bih, gr_bhh, f1_Wr, f1_br, f1_g, f1_b, f1_W1, f1_b1, f1_W2, f1_b2, out):
    ctx = ExitStack()
    with ctx:
        def sb(name, shape, dt=F32):
            return ctx.enter_context(nc.sbuf_tensor(name, shape, dt))

        def sem(name):
            return ctx.enter_context(nc.semaphore(name))

        X = sb("X", [P, TILES, D])
        ADJ = sb("ADJ", [P, TILES, N], BF16)
        WHI = sb("WHI", [P, 8192], F32R)
        WLO = sb("WLO", [P, 8192], F32R)
        FA = sb("FA", [P, 8448])
        RA = sb("RA", [P, 5120], F32R)
        ident = sb("ident", [P, P])
        ones = sb("ones", [P, P])
        iota8 = sb("iota8", [P, E])
        ST = sb("ST", [P, TILES, 6])
        MEAN = sb("MEAN", [P, TILES])
        RSTD = sb("RSTD", [P, TILES])
        NT = sb("NT", [P, 2, TILES])
        GT = sb("GT", [P, TILES, E])
        MEAN2 = sb("MEAN2", [P, TILES])
        RSTD2 = sb("RSTD2", [P, TILES])
        SEL = sb("SEL", [E, E, P], F32R)
        B1F = sb("B1F", [P, E * HID1 // P])
        IF = sb("IF", [P, TILES, 2])
        T2 = sb("T2", [P, 2, TILES])
        L8 = sb("L8", [P, 2, CT, E])
        M8 = sb("M8", [P, 2, CT, 8])
        I8 = sb("I8", [P, 2, CT, 8], U32)
        ROWS = sb("ROWS", [R_END, P])
        COLS = sb("COLS", [P, R_END])
        gWr = sb("gWr", [P, D])
        WE = sb("WE", [P, D + 2])
        wdst = sb("wdst", [P, P])
        wg = sb("wg", [P, 2 * E])
        wgh = sb("wgh", [P, 2 * E], F32R)
        wgl = sb("wgl", [P, 2 * E], F32R)
        bg = sb("bg", [P, 2, E])
        brz = sb("brz", [P, 2])
        WGH = sb("WGH", [P, 12 * P], F32R)
        WGL = sb("WGL", [P, 12 * P], F32R)

        PS = [ctx.enter_context(nc.psum_tensor(f"PS{i}", [P, 512], F32)) for i in range(8)]

        x_t = x.rearrange("g (r p) d -> p (g r) d", p=P)
        out_t = out.rearrange("g (r p) d -> p (g r) d", p=P)
        adj_t = adj.rearrange("g (r p) n -> g p r n", p=P)

        def fa(off, *shape):
            n = 1
            for s in shape:
                n *= s
            v = FA[:, off:off + n]
            if len(shape) == 2:
                v = v.rearrange("p (a b) -> p a b", a=shape[0])
            elif len(shape) == 3:
                v = v.rearrange("p (a b c) -> p a b c", a=shape[0], b=shape[1])
            return v

        raw1 = fa(0, E, HID0)
        raw2 = fa(2048, 2 * E, D)
        rgw = fa(4096, 3, P)
        rih = fa(4480, 3, P)
        rhh = fa(4864, 3, P)
        gwT = fa(5248, 3, P)
        ihT = fa(5632, 3 * P)

        a_xn = fa(0, 2, HALVES, D)
        a_xT = fa(512, 2, N)
        a_h = fa(1024, 4, HALVES, D + 1)
        a_ss = fa(2056, 4, HALVES)
        a_t = fa(2080, 2, HALVES, N)
        a_em = fa(3104, 2, HALVES, N)
        a_p = fa(4128, 2, HALVES, N)
        a_pT = fa(5152, 2, HALVES, N)
        a_mx = fa(6176, 2, HALVES)
        a_rc = fa(6184, 2, HALVES)
        adjst = fa(6208, U, HALVES * N).bitcast(I32)

        f_xn = fa(0, 2, CT, D)
        f_G = fa(1024, 2, CH)
        f_M = fa(2048, 2, CH)
        f_tmp = fa(3072, 2, CH)
        f_acc = fa(4096, 2, CH)
        f_y = fa(5120, CT, D)
        RT = fa(5632, 2, TILES * E).rearrange("p a (t e) -> p a t e", e=E)
        f_g = fa(6656, CT, E)
        LG = fa(7680, TILES, E)
        xTh = RA[:, 0:1024].rearrange("p (a b) -> p a b", a=2)
        xTl = RA[:, 1024:2048].rearrange("p (a b) -> p a b", a=2)
        Gh = RA[:, 2048:3072].rearrange("p (a b) -> p a b", a=2)
        Gl = RA[:, 3072:4096].rearrange("p (a b) -> p a b", a=2)
        gTh = RA[0:E, 4096:4608]
        gTl = RA[0:E, 4608:5120]

        q_hh = WHI[:, 0:2048].rearrange("p (a b) -> p a b", a=4)
        q_A = WHI[:, 2048:6144].rearrange("p (a t n) -> p a t n", a=4, t=CT)
        q_mh = WHI[:, 6144:7168].rearrange("p (a b) -> p a b", a=2)
        q_ah = WHI[:, 7168:8192].rearrange("p (a b) -> p a b", a=2)
        q_hl = WLO[:, 0:2048].rearrange("p (a b) -> p a b", a=4)
        q_ml = WLO[:, 6144:7168].rearrange("p (a b) -> p a b", a=2)
        q_al = WLO[:, 7168:8192].rearrange("p (a b) -> p a b", a=2)
        q_h = fa(0, 4, CH)
        q_xn = fa(2048, 2, CT, D)
        q_r = fa(3072, 2, CH)
        q_z = fa(4096, 2, CH)
        q_t = fa(5120, 2, CH)
        q_n = fa(6144, 2, CH)
        q_d = fa(7168, 2, CH)
        raw1b = fa(0, E, HID1)
        raw2b = fa(4096, E * HID1 // P, D)

        s_x = [sem(f"s_x{i}") for i in range(4)]
        s_vec, s_gw, s_bg, s_wg, s_raw, s_gru = (sem(n) for n in ("s_vec", "s_gw", "s_bg", "s_wg", "s_raw", "s_gru"))
        s_const = sem("s_const")
        s_ident = sem("s_ident")
        s_prep = sem("s_prep")
        s_prepv = sem("s_prepv")
        s_hi, s_lo, s_whi, s_wlo = (sem(n) for n in ("s_hi", "s_lo", "s_whi", "s_wlo"))
        s_dve = sem("s_dve")
        s_act = sem("s_act")
        s_var, s_sqrt, s_rstd = sem("s_var"), sem("s_sqrt"), sem("s_rstd")
        s_adj = [sem(f"s_adj{i}") for i in range(U)]
        (a_norm, a_tr, a_trc, a_prod, a_hc, a_e, a_fill, a_lk, a_sel, a_max, a_exp, a_ptr, a_ptc, a_out, a_rec,
         a_res, a_bn, a_stat) = (sem("a_" + n) for n in (
            "norm", "tr", "trc", "prod", "hc", "e", "fill", "lk", "sel", "max", "exp", "ptr", "ptc", "out", "rec",
            "res", "bn", "stat"))
        C = {n: sem(f"c_{n}") for n in ("xn", "adj", "tr", "h0", "hh", "hl", "mh", "ml", "ag", "ah", "al", "gr", "gz", "gn",
                                        "r", "z", "t1", "t2", "n", "d", "zd", "h", "ft", "res")}
        s_raw1, s_bias, s_biasv, s_scaled = (sem(n) for n in ("s_raw1", "s_bias", "s_biasv", "s_scaled"))
        s_out = sem("s_out")
        R = [{n: sem(f"r{l}_{n}") for n in ("norm", "tr", "hi", "lo", "log", "lg", "max", "idx", "soft", "exp", "st", "bn")} for l in range(2)]
        F = [{n: sem(f"f{l}_{n}") for n in ("norm", "pre", "tr", "xhi", "xlo", "gtr", "gth", "gtl", "m", "mc", "h", "gelu", "ghi",
                                            "glo", "yb", "tmp", "acc", "at", "res", "bn", "st", "sel")} for l in range(2)]
        NBS = (HID0 // P, HID1 // P)
        B1 = (lambda n: COLS[:, R_B1A + n:R_B1A + n + 1], lambda n: B1F[:, n:n + 1])
        B2 = (lambda e: COLS[:, R_B2A + e:R_B2A + e + 1], lambda e: COLS[:, R_B2B + e:R_B2B + e + 1])

        tick = {"dve": 0, "act": 0}

        def own(eng, ins, which="dve"):
            s = s_dve if which == "dve" else s_act
            tick[which] += 1
            ins.then_inc(s, 1)
            eng.wait_ge(s, tick[which])

        def carried(eng):
            eng.wait_ge(s_ident, 2)

        def tile(g, r, h=HALVES):
            return bass.ds(g * h + r, 1)

        block = ctx.enter_context(nc.Block())

        @block.sync
        def _(sp):
            for i in range(4):
                sl = slice(i * TILES // 4, (i + 1) * TILES // 4)
                sp.dma_start(X[:, sl, :], x_t[:, sl, :]).then_inc(s_x[i], 16)
                if i == 0:
                    sp.dma_start(gWr[:], gW).then_inc(s_gw, 16)
                    rows = [(R_A, g_src.rearrange("(a d) -> a d", a=1)), (R_A + 1, g_dst.rearrange("(a d) -> a d", a=1)),
                            (R_B1A, f0_b1.rearrange("e (b p) -> (e b) p", p=P)), (R_B1B, f1_b1.rearrange("e (b p) -> (e b) p", p=P)),
                            (R_B2A, f0_b2), (R_B2B, f1_b2), (R_G, f1_g), (R_B, f1_b),
                            (R_IH, gr_bih.rearrange("(a p) -> a p", p=P)), (R_HH, gr_bhh.rearrange("(a p) -> a p", p=P))]
                    for r, src in rows:
                        sp.dma_start(ROWS[r:r + src.shape[0], :], src).then_inc(s_vec, 16)
                    sp.dma_start(raw1, f0_W1.rearrange("e d h -> d e h")).then_inc(s_raw, 16)
                    sp.dma_start(raw2, f0_W2.rearrange("e (b p) d -> p (e b) d", p=P)).then_inc(s_raw, 16)

            def adj_round(base, off):
                wait(sp, a_sel, base, off - U + 1)
                sp.dma_start(adjst[:, off % U, :].rearrange("p (r n) -> p r n", r=HALVES)[:, None],
                             adj_t[bass.ds(base + off, 1)].rearrange("g p r n -> p g r n")).then_inc(s_adj[off % U], 16)
            rounds(sp, B, 0, U, adj_round)


            if PHASES == 1:
                sp.wait_ge(a_res, B)
                sp.dma_start(out_t, X[:]).then_inc(s_out, 16)
                sp.wait_ge(s_out, 16)
            if PHASES == 3:
                sp.wait_ge(C["res"], B // 2)
                sp.dma_start(out_t, X[:]).then_inc(s_out, 16)
                sp.wait_ge(s_out, 16)
            if PHASES >= 4:
                sp.wait_ge(C["res"], B // 2)
                sp.dma_start(raw1b, f1_W1.rearrange("e d h -> d e h")).then_inc(s_raw1, 16)
                sp.dma_start(raw2b, f1_W2.rearrange("e (b p) d -> p (e b) d", p=P)).then_inc(s_raw1, 16)
                for c in range(CHUNKS):
                    sp.wait_ge(F[1]["res"], c + 1)
                    ts = slice(c * CT, (c + 1) * CT)
                    sp.dma_start(out_t[:, ts, :], X[:, ts, :]).then_inc(s_out, 16)
                sp.wait_ge(s_out, 16 * CHUNKS)
            if PHASES == 2:
                sp.wait_ge(F[0]["res"], CHUNKS)
                sp.dma_start(out_t, X[:]).then_inc(s_out, 16)
                sp.wait_ge(s_out, 16)

        @block.gpsimd
        def _(pool):
            pool.memset(ident[:], 0.0).then_inc(s_ident, 1)
            pool.memset(ones[:], 1.0).then_inc(s_const, 1)
            for e in range(E):
                pool.memset(iota8[:, e:e + 1], float(e)).then_inc(s_const, 1)
            pool.wait_ge(s_ident, 1)
            pool.affine_select(out=ident[:], in_=ident[:], compare_op=ALU.not_equal, fill=1.0, base=0,
                               pattern=[[-1, P]], channel_multiplier=1).then_inc(s_ident, 1)
            pool.wait_ge(s_whi, 2)
            pool.wait_ge(s_wlo, 2)
            for i in range(4):
                pool.memset(a_h[:, i, :, D:D + 1], 1.0).then_inc(s_const, 1)

            def ffn(l):
                f = F[l]

                def chunk(base, off):
                    for e in range(1, E):
                        wait(pool, f["tmp"], base, off, E, e + 1)
                        wait(pool, f["acc"], base, off, E - 1, e - 1)
                        pool.tensor_tensor(f_acc[:, off % 2], f_acc[:, off % 2], f_tmp[:, e % 2], ALU.add).then_inc(f["acc"], 1)
                rounds(pool, CHUNKS - 2, 2, 2, chunk, 2)

            if PHASES >= 2:
                ffn(0)

            def gru(i, k):
                if liveq(i, k - 3):
                    u = k - 3
                    waitq(pool, C["zd"], i, u, 1)
                    pool.tensor_tensor(q_h[:, u % 4], q_n[:, u % 2], q_d[:, u % 2], ALU.add).then_inc(C["h"], 1)
            if PHASES >= 3:
                unit_rounds(pool, 5, gru)
            if PHASES >= 4:
                ffn(1)

        @block.scalar
        def _(act):
            act.dma_start(wg[:, 0:E], f0_Wg).then_inc(s_wg, 16)
            act.dma_start(wg[:, E:], f1_Wr).then_inc(s_wg, 16)
            act.dma_start(bg[:, 0], f0_bg.rearrange("(a e) -> a e", a=1).to_broadcast([P, E])).then_inc(s_bg, 16)
            act.dma_start(bg[:, 1], f1_br.rearrange("(a e) -> a e", a=1).to_broadcast([P, E])).then_inc(s_bg, 16)
            act.dma_start(rgw, gr_w.rearrange("i d e -> d i e")).then_inc(s_gru, 16)
            act.dma_start(rih, gr_wih.rearrange("(a o) k -> o a k", o=P)).then_inc(s_gru, 16)
            act.dma_start(rhh, gr_whh.rearrange("(a o) k -> o a k", o=P)).then_inc(s_gru, 16)
            act.wait_ge(s_prep, 1)
            nc.scalar.copy(COLS[:], PS[0][:, 0:R_END]).then_inc(s_prepv, 1)
            nc.scalar.copy(WE[:, 0:D], PS[1][:, 0:D]).then_inc(s_prepv, 1)
            act.wait_ge(s_prep, 2)
            nc.scalar.copy(WE[:, D:D + 2], PS[0][:, 128:130]).then_inc(s_prepv, 1)
            act.wait_ge(s_prep, 3)
            nc.scalar.copy(gwT, PS[2][:, 0:3 * P].rearrange("p (a b) -> p a b", a=3)).then_inc(s_prepv, 1)
            nc.scalar.copy(ihT, PS[3][:, 0:3 * P]).then_inc(s_prepv, 1)
            nc.scalar.copy(WGH[:, 9 * P:], PS[4][:, 0:3 * P]).then_inc(s_hi, 1)
            for i in range(LAYERS):
                act.wait_ge(s_prep, 4 + i)
                nc.scalar.copy(WGH[:, 3 * i * P:3 * (i + 1) * P], PS[5 + i][:, 0:3 * P]).then_inc(s_hi, 1)
            act.wait_ge(s_wg, 32)
            nc.scalar.copy(wgh[:], wg[:]).then_inc(s_hi, 1)
            act.wait_ge(s_raw, 32)
            nc.scalar.copy(WHI[:, 0:2048], FA[:, 0:2048]).then_inc(s_whi, 1)
            nc.scalar.copy(WHI[:, 2048:4096], FA[:, 2048:4096]).then_inc(s_whi, 1)

            act.wait_ge(s_var, 1)
            nc.scalar.activation(NT[:, 1], NT[:, 1], ACT.Sqrt).then_inc(s_sqrt, 1)
            act.wait_ge(s_wlo, 2)

            def att_round(base, off):
                if live(base, off - 1, B):
                    g = off - 1
                    wait(act, a_tr, base, g + 1)
                    wait(act, a_prod, base, g - 1)
                    nc.scalar.copy(a_xT[:, g % 2], PS[g % 2][:, 0:N]).then_inc(a_trc, 1)
                if live(base, off - 2, B):
                    g = off - 2
                    wait(act, a_max, base, g + 1)
                    wait(act, a_ptr, base, g - 1)
                    for r in range(HALVES):
                        ins = nc.scalar.activation(a_p[:, g % 2, r], a_em[:, g % 2, r], ACT.Exp,
                                                   bias=a_mx[:, g % 2, r:r + 1])
                    ins.then_inc(a_exp, 1)
                if live(base, off - 1, B):
                    g = off - 1
                    wait(act, a_prod, base, g + 1)
                    wait(act, a_out, base, g - 3)
                    src = PS[2 + g % 2][:, 0:2 * (D + 1)].rearrange("p (r c) -> p r c", r=HALVES)
                    nc.scalar.copy(a_h[:, g % 4, :, 0:D], src[:, :, 0:D]).then_inc(a_hc, 1)
                    nc.scalar.copy(a_ss[:, g % 4], src[:, :, D]).then_inc(a_hc, 1)
                    wait(act, a_hc, base, g, 2, 2)
                    wait(act, a_sel, base, g - 1)
                    for r in range(HALVES):
                        ins = nc.scalar.activation(a_t[:, g % 2, r], PS[g % 2][:, N:2 * N], ACT.Identity,
                                                   bias=a_ss[:, g % 4, r:r + 1])
                    ins.then_inc(a_e, 1)
            rounds(act, B, 4, 8, att_round)

            def router(l):
                r = R[l]

                def chunk(base, off):
                    if live(base, off - 1, CHUNKS):
                        c = off - 1
                        wait(act, r["tr"], base, c + 1)
                        wait(act, r["log"], base, c - 1)
                        nc.scalar.copy(xTh[:, c % 2], PS[c % 2][:]).then_inc(r["hi"], 1)
                rounds(act, CHUNKS, 4, 8, chunk)

            def ffn(l):
                f, nb = F[l], NBS[l]
                NB = E * nb

                def pre_x(base, c):
                    wait(act, f["tr"], base, c + 1)
                    wait(act, f["h"], base, c - 1, NB)
                    nc.scalar.copy(xTh[:, c % 2], PS[7][:]).then_inc(f["xhi"], 1)

                def pre_g(base, c):
                    wait(act, f["gtr"], base, c + 1)
                    wait(act, f["m"], base, c, E)
                    nc.scalar.copy(gTh, PS[7][0:E, :]).then_inc(f["gth"], 1)

                def chunk(base, off, last=False):
                    for n in range(NB):
                        e, b = divmod(n, nb)
                        wait(act, f["h"], base, off, NB, n + 1)
                        wait(act, f["glo"], base, off, NB, n - 1)
                        nc.scalar.activation(f_G[:, n % 2], PS[n % 4][:], ACT.Gelu, bias=B1[l](n)).then_inc(f["gelu"], 1)
                        if b == 1:
                            wait(act, f["m"], base, off, E, e + 1)
                            wait(act, f["tmp"], base, off, E, e - 1)
                            nc.scalar.copy(f_M[:, e % 2], PS[6][:]).then_inc(f["mc"], 1)
                        if n == 3 * nb and not last:
                            pre_x(base, off + 1)
                        if n == E * nb - 1 and not last:
                            pre_g(base, off + 1)
                pre_x(0, 0)
                pre_g(0, 0)
                rounds(act, CHUNKS - 2, 1, 2, chunk, 2)
                chunk(CHUNKS - 2, 1, True)

            if PHASES >= 2:
                act.wait_ge(s_var, 2)
                nc.scalar.activation(NT[:, 1], NT[:, 1], ACT.Sqrt).then_inc(s_sqrt, 1)
                router(0)
                ffn(0)

            def gru(i, k):
                l, w = k // 4, k % 4
                if liveq(i, k - 3):
                    u = k - 3
                    waitq(act, C["t2"], i, u, 1)
                    waitq(act, C["h"], i, u, -1)
                    nc.scalar.activation(q_n[:, u % 2], q_t[:, u % 2], ACT.Tanh, bias=COLS[:, R_IH + 2:R_IH + 3]).then_inc(C["n"], 1)
                if liveq(i, k):
                    T = PS[7 * (k % 2)]
                    if l == 0:
                        waitq(act, C["tr"], i, k, 1)
                        waitp(act, C["ft"], i, k, -3)
                        nc.scalar.copy(q_h[:, w], T[:]).then_inc(C["h0"], 1)
                        waitq(act, C["gn"], i, k, -3)
                        nc.scalar.copy(q_hh[:, w], T[:]).then_inc(C["hh"], 1)
                        waitq(act, C["ag"], i, k, -1)
                        nc.scalar.copy(q_mh[:, k % 2], q_xn[:, k % 2].rearrange("p t d -> p (t d)")).then_inc(C["mh"], 1)
                    else:
                        waitq(act, C["tr"], i, k, 1)
                        waitq(act, C["ag"], i, k, -1)
                        nc.scalar.copy(q_mh[:, k % 2], T[:]).then_inc(C["mh"], 1)
                if liveq(i, k - 1):
                    u = k - 1
                    waitq(act, C["ag"], i, u, 1)
                    waitq(act, C["gn"], i, u, -1)
                    nc.scalar.copy(q_ah[:, u % 2], PS[1][:]).then_inc(C["ah"], 1)
                if liveq(i, k - 2):
                    u = k - 2
                    waitq(act, C["gr"], i, u, 1)
                    waitq(act, C["t1"], i, u, -1)
                    nc.scalar.activation(q_r[:, u % 2], PS[2][:], ACT.Sigmoid, bias=brz[:, 0:1]).then_inc(C["r"], 1)
                    waitq(act, C["gz"], i, u, 1)
                    waitq(act, C["zd"], i, u, -1)
                    nc.scalar.activation(q_z[:, u % 2], PS[3][:], ACT.Sigmoid, bias=brz[:, 1:2]).then_inc(C["z"], 1)
                if liveq(i, k - 3) and (k - 3) % UNITS < UNITS - 4:
                    u = k - 3
                    waitq(act, C["h"], i, u, 1)
                    waitq(act, C["gn"], i, u, 1)
                    nc.scalar.copy(q_hh[:, u % 4], q_h[:, u % 4]).then_inc(C["hh"], 1)

            if PHASES >= 3:
                act.wait_ge(s_var, 3)
                nc.scalar.activation(NT[:, 1], NT[:, 1], ACT.Sqrt).then_inc(s_sqrt, 1)
                unit_rounds(act, 5, gru)
            if PHASES >= 4:
                act.wait_ge(s_var, 4)
                nc.scalar.activation(NT[:, 1], NT[:, 1], ACT.Sqrt).then_inc(s_sqrt, 1)
                act.wait_ge(s_bias, 1)
                act.wait_ge(s_scaled, 1)
                nc.scalar.copy(WHI[:, 0:4096], FA[:, 0:4096]).then_inc(s_whi, 1)
                act.wait_ge(s_raw1, 32)
                nc.scalar.copy(WHI[:, 4096:8192], FA[:, 4096:8192]).then_inc(s_whi, 1)
                router(1)
                act.wait_ge(R[1]["exp"], 1)
                nc.scalar.activation(RT[:, 0], RT[:, 0], ACT.Exp).then_inc(R[1]["bn"], 1)
                act.wait_ge(s_var, 5)
                nc.scalar.activation(NT[:, 1], NT[:, 1], ACT.Sqrt).then_inc(s_sqrt, 1)
                ffn(1)

        @block.vector
        def _(dve):
            for t in range(TILES):
                if t % 16 == 0:
                    dve.wait_ge(s_x[t // 16], 16)
                ins = nc.vector.bn_stats(ST[:, t], X[:, t])
            ins.then_inc(a_stat, 1)
            dve.wait_ge(s_prepv, 3)
            nc.vector.tensor_scalar(wdst[:], ones[:], WE[:, D + 1:D + 2], None, ALU.mult).then_inc(s_lo, 1)
            dve.wait_ge(s_hi, 1)
            nc.vector.tensor_tensor(WGL[:, 9 * P:], PS[4][:, 0:3 * P], WGH[:, 9 * P:].bitcast(F32), ALU.subtract).then_inc(s_lo, 1)
            for i in range(LAYERS):
                dve.wait_ge(s_hi, 2 + i)
                nc.vector.tensor_tensor(WGL[:, 3 * i * P:3 * (i + 1) * P], PS[5 + i][:, 0:3 * P],
                                        WGH[:, 3 * i * P:3 * (i + 1) * P].bitcast(F32), ALU.subtract).then_inc(s_lo, 1)
            nc.vector.tensor_tensor(brz[:], COLS[:, R_IH:R_IH + 2], COLS[:, R_HH:R_HH + 2], ALU.add).then_inc(s_lo, 1)
            dve.wait_ge(s_hi, 2 + LAYERS)
            nc.vector.tensor_tensor(wgl[:], wg[:], wgh[:].bitcast(F32), ALU.subtract).then_inc(s_lo, 1)
            for i in range(2):
                dve.wait_ge(s_whi, 1 + i)
                nc.vector.tensor_tensor(WLO[:, 2048 * i:2048 * (i + 1)], FA[:, 2048 * i:2048 * (i + 1)],
                                        WHI[:, 2048 * i:2048 * (i + 1)].bitcast(F32), ALU.subtract).then_inc(s_wlo, 1)

            def finish_stats(k, mean, rstd):
                m0, v0, m1, v1 = (ST[:, :, i] for i in (1, 2, 4, 5))
                own(dve, nc.vector.tensor_tensor(NT[:, 1], m0, m1, ALU.subtract))
                own(dve, nc.vector.scalar_tensor_tensor(out=NT[:, 1], in0=NT[:, 1], scalar=0.25, in1=NT[:, 1], op0=ALU.mult, op1=ALU.mult))
                own(dve, nc.vector.tensor_tensor(NT[:, 0], v0, v1, ALU.add))
                own(dve, nc.vector.scalar_tensor_tensor(out=NT[:, 0], in0=NT[:, 0], scalar=1.0 / D, in1=NT[:, 1], op0=ALU.mult, op1=ALU.add))
                own(dve, nc.vector.tensor_tensor(mean[:], m0, m1, ALU.add))
                own(dve, nc.vector.tensor_scalar(mean[:], mean[:], 0.5, None, ALU.mult))
                own(dve, nc.vector.tensor_scalar(NT[:, 0], NT[:, 0], EPS, None, ALU.add))
                nc.vector.tensor_scalar(NT[:, 1], NT[:, 0], 1.0, None, ALU.mult).then_inc(s_var, 1)
                dve.wait_ge(s_sqrt, k)
                own(dve, nc.vector.reciprocal(rstd[:], NT[:, 1]))
                own(dve, nc.vector.tensor_tensor(NT[:, 1], rstd[:], rstd[:], ALU.mult))
                own(dve, nc.vector.tensor_tensor(NT[:, 1], NT[:, 1], NT[:, 0], ALU.mult))
                own(dve, nc.vector.tensor_scalar(NT[:, 1], NT[:, 1], -0.5, 1.5, ALU.mult, ALU.add))
                own(dve, nc.vector.tensor_tensor(rstd[:], rstd[:], NT[:, 1], ALU.mult))

            dve.wait_ge(a_stat, 1)
            finish_stats(1, MEAN, RSTD)
            dve.wait_ge(s_wlo, 2)

            def att_round(base, off):
                if live(base, off, B):
                    g = off
                    wait(dve, a_tr, base, g - 1)
                    for r in range(HALVES):
                        t = tile(base + g, r)
                        ins = nc.vector.tensor_scalar(a_xn[:, g % 2, r][:, None], X[:, t, :], MEAN[:, t], RSTD[:, t],
                                                      ALU.subtract, ALU.mult)
                    ins.then_inc(a_norm, 1)
                if live(base, off - 2, B):
                    g = off - 2
                    wait(dve, a_exp, base, g - 1)
                    nc.vector.memset(a_em[:, g % 2], NEG_INF).then_inc(a_fill, 1)
                    wait(dve, a_e, base, g + 1)
                    nc.vector.scalar_tensor_tensor(out=a_t[:, g % 2], in0=a_t[:, g % 2], scalar=SLOPE, in1=a_t[:, g % 2],
                                                   op0=ALU.mult, op1=ALU.max).then_inc(a_lk, 1)
                    if isinstance(base, int):
                        dve.wait_ge(s_adj[g % U], 16 * ((base + g) // U + 1))
                    else:
                        dve.wait_ge(s_adj[g % U], base * (16 // U) + 16 * (g // U + 1))
                    for r in range(HALVES):
                        nc.vector.tensor_scalar(ADJ[:, tile(base + g, r), :], adjst[:, g % U, r * N:(r + 1) * N][:, None], 0, None,
                                                ALU.not_equal)
                    carried(dve)
                    wait(dve, a_fill, base, g + 1)
                    wait(dve, a_lk, base, g + 1)
                    nc.vector.copy_predicated(a_em[:, g % 2], mask=adjst[:, g % U, :].rearrange("p (r n) -> p r n", r=HALVES),
                                              data=a_t[:, g % 2]).then_inc(a_sel, 1)
                    wait(dve, a_sel, base, g + 1)
                    nc.vector.tensor_reduce(out=a_mx[:, g % 2], in_=a_em[:, g % 2], op=ALU.max, axis=AX.X,
                                            negate=True).then_inc(a_max, 1)
                if live(base, off - 3, B):
                    g = off - 3
                    wait(dve, a_ptr, base, g + 1)
                    wait(dve, a_out, base, g - 1)
                    nc.vector.tensor_copy(a_pT[:, g % 2], PS[4 + g % 2][:].rearrange("p (r n) -> p r n", r=HALVES)).then_inc(a_ptc, 1)
                if live(base, off - 4, B):
                    g = off - 4
                    wait(dve, a_out, base, g + 1)
                    o = PS[6 + g % 2][:, 0:2 * (D + 1)].rearrange("p (r c) -> p r c", r=HALVES)
                    nc.vector.reciprocal(a_rc[:, g % 2], o[:, :, D]).then_inc(a_rec, 1)
                    wait(dve, a_rec, base, g + 1)
                    for r in range(HALVES):
                        t = tile(base + g, r)
                        ins = nc.vector.scalar_tensor_tensor(out=X[:, t, :], in0=o[:, r, 0:D][:, None], scalar=a_rc[:, g % 2, r:r + 1],
                                                             in1=X[:, t, :], op0=ALU.mult, op1=ALU.add)
                    ins.then_inc(a_res, 1)
                    wait(dve, a_res, base, g + 1)
                    for r in range(HALVES):
                        t = tile(base + g, r)
                        ins = nc.vector.bn_stats(ST[:, t, :].rearrange("p a s -> p (a s)"), X[:, t, :].rearrange("p a d -> p (a d)"))
                    ins.then_inc(a_stat, 1)
            rounds(dve, B, 4, 8, att_round)

            def normalise(out_, t, mean, rstd, src):
                return nc.vector.tensor_scalar(out_, src, mean[:, t], rstd[:, t], ALU.subtract, ALU.mult)

            def token_stats(t, src):
                return nc.vector.bn_stats(ST[:, t, :].rearrange("p a s -> p (a s)"), src)

            def router(l):
                r = R[l]

                def chunk(base, off):
                    if live(base, off, CHUNKS):
                        wait(dve, r["tr"], base, off - 1)
                        for i in range(CT):
                            t = tile(base + off, i, CT)
                            ins = normalise(f_xn[:, off % 2, i][:, None], t, MEAN, RSTD, X[:, t, :])
                        ins.then_inc(r["norm"], 1)
                        if l == 1:
                            wait(dve, r["norm"], base, off + 1)
                            for i in range(CT):
                                ins = token_stats(tile(base + off, i, CT), f_xn[:, off % 2, i])
                            ins.then_inc(r["st"], 1)
                    if live(base, off - 1, CHUNKS):
                        c = off - 1
                        wait(dve, r["hi"], base, c + 1)
                        nc.vector.tensor_tensor(xTl[:, c % 2], PS[c % 2][:], xTh[:, c % 2].bitcast(F32), ALU.subtract).then_inc(r["lo"], 1)
                    if live(base, off - 3, CHUNKS):
                        c = off - 3
                        ts = bass.ds((base + c) * CT, CT)
                        wait(dve, r["log"], base, c + 1)
                        nc.vector.tensor_tensor(L8[:, c % 2], PS[2 + c % 2][:, 0:CT * E].rearrange("p (t e) -> p t e", e=E),
                                                bg[:, l][:, None, :].to_broadcast([P, CT, E]), ALU.add).then_inc(r["lg"], 1)
                        carried(dve)
                        wait(dve, r["lg"], base, c + 1)
                        for i in range(CT):
                            ins = nc.vector.max(M8[:, c % 2, i], L8[:, c % 2, i])
                        ins.then_inc(r["max"], 1)
                        nc.vector.tensor_copy(LG[:, ts, :], L8[:, c % 2])
                        carried(dve)
                        wait(dve, r["max"], base, c + 1)
                        for i in range(CT):
                            ins = nc.vector.max_index(I8[:, c % 2, i], M8[:, c % 2, i], L8[:, c % 2, i])
                        ins.then_inc(r["idx"], 1)
                        wait(dve, r["idx"], base, c + 1)
                        nc.vector.tensor_copy(IF[:, ts, :], I8[:, c % 2, :, 0:2]).then_inc(r["soft"], 1)
                rounds(dve, CHUNKS, 4, 8, chunk)
                dve.wait_ge(r["soft"], CHUNKS)
                for k in range(2):
                    ins = nc.vector.tensor_tensor(RT[:, k], iota8[:, None, :].to_broadcast([P, TILES, E]),
                                                  IF[:, :, k:k + 1].to_broadcast([P, TILES, E]), ALU.is_equal)
                own(dve, ins)
                own(dve, nc.vector.tensor_tensor(GT[:], RT[:, 0], RT[:, 1], ALU.add))
                if l == 1:
                    own(dve, nc.vector.tensor_reduce(out=NT[:, 0], in_=LG, op=ALU.max, axis=AX.X))
                    nc.vector.tensor_tensor(RT[:, 0], LG, NT[:, 0][:, :, None].to_broadcast([P, TILES, E]), ALU.subtract).then_inc(r["exp"], 1)
                    dve.wait_ge(r["bn"], 1)
                    for src, dst, times in ((RT[:, 0], RT[:, 1], RT[:, 0]), (None, RT[:, 0], RT[:, 1])):
                        if src is None:
                            src = GT[:]
                            own(dve, nc.vector.tensor_tensor(GT[:], GT[:], times, ALU.mult))
                        own(dve, nc.vector.tensor_reduce(out=NT[:, 0], in_=src, op=ALU.add, axis=AX.X))
                        own(dve, nc.vector.reciprocal(NT[:, 1], NT[:, 0]))
                        own(dve, nc.vector.tensor_tensor(dst, src, NT[:, 1][:, :, None].to_broadcast([P, TILES, E]), ALU.mult))
                    own(dve, nc.vector.tensor_copy(GT[:], RT[:, 0]))

            def ffn(l):
                f, nb = F[l], NBS[l]
                NB = E * nb

                def pre_norm(base, c):
                    wait(dve, f["tr"], base, c)
                    for i in range(CT):
                        t = tile(base + c, i, CT)
                        ins = normalise((f_y[:, i] if l else f_xn[:, 0, i])[:, None], t, MEAN, RSTD, X[:, t, :])
                    if l:
                        ins.then_inc(f["sel"], 1)
                        wait(dve, f["sel"], base, c + 1)
                        for i in range(CT):
                            t = tile(base + c, i, CT)
                            normalise(f_xn[:, 0, i][:, None], t, MEAN2, RSTD2, f_y[:, i][:, None])
                    wait(dve, f["gtr"], base, c)
                    nc.vector.tensor_copy(f_g, GT[:, bass.ds((base + c) * CT, CT), :]).then_inc(f["norm"], 1)

                def pre_x(base, c):
                    wait(dve, f["xhi"], base, c + 1)
                    nc.vector.tensor_tensor(xTl[:, c % 2], PS[7][:], xTh[:, c % 2].bitcast(F32), ALU.subtract).then_inc(f["xlo"], 1)

                def pre_g(base, c):
                    wait(dve, f["gth"], base, c + 1)
                    nc.vector.tensor_tensor(gTl, PS[7][0:E, :], gTh.bitcast(F32), ALU.subtract).then_inc(f["gtl"], 1)

                def gated(base, off, e):
                    wait(dve, f["yb"], base, off, NB, (e + 1) * nb)
                    wait(dve, f["mc"], base, off, E, e + 1)
                    if e == 0:
                        wait(dve, f["at"], base, off - 1)
                    elif e < 3:
                        wait(dve, f["acc"], base, off, E - 1)
                    else:
                        wait(dve, f["acc"], base, off, E - 1, e - 2)
                    nc.vector.scalar_tensor_tensor(out=f_acc[:, off % 2] if e == 0 else f_tmp[:, e % 2], in0=PS[4 + e % 2][:],
                                                   scalar=B2[l](e), in1=f_M[:, e % 2], op0=ALU.add, op1=ALU.mult).then_inc(f["tmp"], 1)

                def chunk(base, off, last=False):
                    for n in range(NB):
                        wait(dve, f["gelu"], base, off, NB, n + 1)
                        wait(dve, f["yb"], base, off, NB, n - 1)
                        nc.vector.tensor_copy(Gh[:, n % 2], f_G[:, n % 2]).then_inc(f["ghi"], 1)
                        wait(dve, f["ghi"], base, off, NB, n + 1)
                        nc.vector.tensor_tensor(Gl[:, n % 2], f_G[:, n % 2], Gh[:, n % 2].bitcast(F32), ALU.subtract).then_inc(f["glo"], 1)
                        if n >= nb + 1 and (n - 1) % nb == 0:
                            gated(base, off, (n - 1) // nb - 1)
                        if n == nb and not last:
                            pre_norm(base, off + 1)
                        if n == 3 * nb and not last:
                            pre_x(base, off + 1)
                    if not last:
                        pre_g(base, off + 1)
                    gated(base, off, E - 1)
                    wait(dve, f["at"], base, off + 1)
                    ts = bass.ds((base + off) * CT, CT)
                    nc.vector.tensor_tensor(X[:, ts, :], PS[7][:].rearrange("p (t d) -> p t d", d=D), X[:, ts, :], ALU.add).then_inc(f["res"], 1)
                    if l == 0:
                        wait(dve, f["res"], base, off + 1)
                        for i in range(CT):
                            t = tile(base + off, i, CT)
                            ins = token_stats(t, X[:, t, :].rearrange("p a d -> p (a d)"))
                        ins.then_inc(f["st"], 1)
                pre_norm(0, 0)
                pre_x(0, 0)
                pre_g(0, 0)
                rounds(dve, CHUNKS - 2, 1, 2, chunk, 2)
                chunk(CHUNKS - 2, 1, True)

            if PHASES >= 2:
                dve.wait_ge(a_stat, 1 + B)
                nc.vector.tensor_copy(SEL[:], ident[0:E, 0:E][:, :, None].to_broadcast([E, E, P])).then_inc(s_lo, 1)
                finish_stats(2, MEAN, RSTD)
                router(0)
                ffn(0)

            def gru(i, k):
                if liveq(i, k) and k < 4:
                    start_pair(i, k)
                if liveq(i, k - 3):
                    u = k - 3
                    waitq(dve, C["n"], i, u, 1)
                    waitq(dve, C["h"], i, u, -1)
                    nc.vector.tensor_tensor(q_d[:, u % 2], q_h[:, u % 4], q_n[:, u % 2], ALU.subtract).then_inc(C["d"], 1)
                    waitq(dve, C["d"], i, u, 1)
                    nc.vector.tensor_tensor(q_d[:, u % 2], q_d[:, u % 2], q_z[:, u % 2], ALU.mult).then_inc(C["zd"], 1)
                if liveq(i, k):
                    T = PS[7 * (k % 2)]
                    if k // 4 == 0:
                        waitq(dve, C["hh"], i, k, 1)
                        nc.vector.tensor_tensor(q_hl[:, k % 4], T[:], q_hh[:, k % 4].bitcast(F32), ALU.subtract).then_inc(C["hl"], 1)
                        T = q_xn[:, k % 2].rearrange("p t d -> p (t d)")
                    waitq(dve, C["mh"], i, k, 1)
                    nc.vector.tensor_tensor(q_ml[:, k % 2], T[:], q_mh[:, k % 2].bitcast(F32), ALU.subtract).then_inc(C["ml"], 1)
                if liveq(i, k - 1):
                    u = k - 1
                    waitq(dve, C["ah"], i, u, 1)
                    nc.vector.tensor_tensor(q_al[:, u % 2], PS[1][:], q_ah[:, u % 2].bitcast(F32), ALU.subtract).then_inc(C["al"], 1)
                if liveq(i, k - 2):
                    u = k - 2
                    waitq(dve, C["gn"], i, u, 1)
                    waitq(dve, C["r"], i, u, 1)
                    waitq(dve, C["n"], i, u, -1)
                    nc.vector.scalar_tensor_tensor(out=q_t[:, u % 2], in0=PS[4][:], scalar=COLS[:, R_HH + 2:R_HH + 3], in1=q_r[:, u % 2],
                                                   op0=ALU.add, op1=ALU.mult).then_inc(C["t1"], 1)
                    waitq(dve, C["t1"], i, u, 1)
                    nc.vector.tensor_tensor(q_t[:, u % 2], PS[5][:], q_t[:, u % 2], ALU.add).then_inc(C["t2"], 1)
                if liveq(i, k - 3) and (k - 3) % UNITS < UNITS - 4:
                    u = k - 3
                    waitq(dve, C["hh"], i, u + 4, 1)
                    nc.vector.tensor_tensor(q_hl[:, u % 4], q_h[:, u % 4], q_hh[:, u % 4].bitcast(F32), ALU.subtract).then_inc(C["hl"], 1)
                if liveq(i, k - 4) and (k - 4) % UNITS >= UNITS - 4:
                    u = k - 4
                    waitp(dve, C["ft"], i, u, 1)
                    pair = i * 4 + (u // UNITS * 4 + u % 4)
                    ts = bass.ds(pair * CT, CT)
                    nc.vector.tensor_tensor(X[:, ts, :], PS[6][:].rearrange("p (t d) -> p t d", d=D), X[:, ts, :], ALU.add).then_inc(C["res"], 1)
                    waitp(dve, C["res"], i, u, 1)
                    for j in range(CT):
                        t = bass.ds(pair * CT + j, 1)
                        ins = token_stats(t, X[:, t, :].rearrange("p a d -> p (a d)"))
                    ins.then_inc(a_stat, 1)

            def start_pair(i, u):
                pair = i * 4 + (u // UNITS * 4 + u % 4)
                back = 1 if u % 4 >= 2 else 9
                waitq(dve, C["tr"], i, u, -back)
                waitq(dve, C["mh"], i, u, -back)
                for j in range(CT):
                    t = bass.ds(pair * CT + j, 1)
                    ins = normalise(q_xn[:, u % 2, j][:, None], t, MEAN, RSTD, X[:, t, :])
                ins.then_inc(C["xn"], 1)
                waitq(dve, C["ag"], i, u, -3)
                nc.vector.tensor_copy(q_A[:, u % 4], ADJ[:, bass.ds(pair * CT, CT), :]).then_inc(C["adj"], 1)

            if PHASES >= 3:
                dve.wait_ge(F[0]["st"], CHUNKS)
                finish_stats(3, MEAN, RSTD)
                unit_rounds(dve, 5, gru)
            if PHASES >= 4:
                dve.wait_ge(a_stat, 1 + B + B // 2)
                finish_stats(4, MEAN, RSTD)
                dve.wait_ge(s_bias, 1)
                nc.vector.tensor_tensor(B1F[:], PS[4][:, 0:E * HID1 // P], COLS[:, R_B1B:R_B1B + E * HID1 // P], ALU.add)
                for e in range(E):
                    ins = nc.vector.tensor_scalar(raw1b[:, e], raw1b[:, e], COLS[:, R_G + e:R_G + e + 1], None, ALU.mult)
                ins.then_inc(s_scaled, 1)
                dve.wait_ge(s_scaled, 1)
                for j in range(2):
                    dve.wait_ge(s_whi, 3 + j)
                    nc.vector.tensor_tensor(WLO[:, 4096 * j:4096 * (j + 1)], FA[:, 4096 * j:4096 * (j + 1)],
                                            WHI[:, 4096 * j:4096 * (j + 1)].bitcast(F32), ALU.subtract).then_inc(s_wlo, 1)
                dve.wait_ge(s_wlo, 4)
                router(1)
                dve.wait_ge(R[1]["st"], CHUNKS)
                finish_stats(5, MEAN2, RSTD2)
                ffn(1)

        @block.tensor
        def _(pe):
            pe.wait_ge(s_ident, 2)
            pe.wait_ge(s_vec, 160)
            pe.wait_ge(s_gw, 16)
            nc.tensor.transpose(PS[0][:, 0:R_END], ROWS[:], ident[0:R_END, 0:R_END])
            nc.tensor.transpose(PS[1][:, 0:P], gWr[:], ident[:]).then_inc(s_prep, 1)
            pe.wait_ge(s_prepv, 2)
            nc.tensor.matmul(PS[0][:, 128:130], gWr[:], COLS[:, 0:2], start=True, stop=True).then_inc(s_prep, 1)
            pe.wait_ge(s_gru, 48)
            for i in range(3):
                nc.tensor.transpose(PS[2][:, i * P:(i + 1) * P], rgw[:, i], ident[:])
                nc.tensor.transpose(PS[3][:, i * P:(i + 1) * P], rih[:, i], ident[:])
                ins = nc.tensor.transpose(PS[4][:, i * P:(i + 1) * P], rhh[:, i], ident[:])
            ins.then_inc(s_prep, 1)
            pe.wait_ge(s_prepv, 5)
            for i in range(LAYERS):
                nc.tensor.matmul(PS[5 + i][:, 0:3 * P], gwT[:, i], ihT, start=True, stop=True).then_inc(s_prep, 1)
            pe.wait_ge(s_lo, 6)
            pe.wait_ge(s_wlo, 2)
            pe.wait_ge(s_const, 13)

            def att_round(base, off):
                if live(base, off - 1, B):
                    g = off - 1
                    wait(pe, a_norm, base, g + 1)
                    wait(pe, a_e, base, g - 1)
                    for r in range(HALVES):
                        ins = nc.tensor.transpose(PS[g % 2][:, r * P:(r + 1) * P], a_xn[:, g % 2, r], ident[:])
                    ins.then_inc(a_tr, 1)
                if live(base, off - 3, B):
                    g = off - 3
                    wait(pe, a_exp, base, g + 1)
                    wait(pe, a_ptc, base, g - 1)
                    for j in range(HALVES):
                        for r in range(HALVES):
                            ins = nc.tensor.transpose(PS[4 + g % 2][:, j * N + r * P:j * N + (r + 1) * P],
                                                      a_p[:, g % 2, r, j * P:(j + 1) * P], ident[:])
                    ins.then_inc(a_ptr, 1)
                if live(base, off - 4, B):
                    g = off - 4
                    wait(pe, a_ptc, base, g + 1)
                    wait(pe, a_res, base, g - 1)
                    for r in range(HALVES):
                        for j in range(HALVES):
                            ins = nc.tensor.matmul(PS[6 + g % 2][:, r * (D + 1):(r + 1) * (D + 1)],
                                                   a_pT[:, g % 2, j, r * P:(r + 1) * P], a_h[:, g % 4, j],
                                                   start=(j == 0), stop=(j == HALVES - 1))
                    ins.then_inc(a_out, 1)
                if live(base, off - 1, B):
                    g = off - 1
                    wait(pe, a_trc, base, g + 1)
                    wait(pe, a_hc, base, g, 2, -2)
                    for r in range(HALVES):
                        nc.tensor.matmul(PS[2 + g % 2][:, r * (D + 1):(r + 1) * (D + 1)],
                                         a_xT[:, g % 2, r * P:(r + 1) * P], WE[:, 0:D + 1], start=True, stop=True)
                    nc.tensor.matmul(PS[g % 2][:, N:2 * N], wdst[:], a_xT[:, g % 2], start=True, stop=True).then_inc(a_prod, 1)
            rounds(pe, B, 4, 8, att_round)

            def mm3(o, lh, ll, rh, rl, start=True, stop=True):
                nc.tensor.matmul(o, lh, rh, start=start, stop=False)
                nc.tensor.matmul(o, lh, rl, start=False, stop=False)
                return nc.tensor.matmul(o, ll, rh, start=False, stop=stop)

            def router(l):
                r = R[l]

                def chunk(base, off):
                    if live(base, off - 1, CHUNKS):
                        c = off - 1
                        wait(pe, r["norm"], base, c + 1)
                        wait(pe, r["lo"], base, c - 1)
                        for i in range(CT):
                            ins = nc.tensor.transpose(PS[c % 2][:, i * P:(i + 1) * P], f_xn[:, c % 2, i], ident[:])
                        ins.then_inc(r["tr"], 1)
                    if live(base, off - 2, CHUNKS):
                        c = off - 2
                        wait(pe, r["lo"], base, c + 1)
                        wait(pe, r["lg"], base, c - 1)
                        for i in range(CT):
                            ins = mm3(PS[2 + c % 2][:, i * E:(i + 1) * E], xTh[:, c % 2, i * P:(i + 1) * P],
                                      xTl[:, c % 2, i * P:(i + 1) * P], wgh[:, l * E:(l + 1) * E], wgl[:, l * E:(l + 1) * E])
                        ins.then_inc(r["log"], 1)
                rounds(pe, CHUNKS, 4, 8, chunk)

            def ffn(l):
                f, nb = F[l], NBS[l]
                NB = E * nb
                W1o, W2o = 0, E * nb * P

                def pre_x(base, c):
                    wait(pe, f["norm"], base, c + 1)
                    wait(pe, f["res"], base, c - 1)
                    for i in range(CT):
                        ins = nc.tensor.transpose(PS[7][:, i * P:(i + 1) * P], f_xn[:, 0, i], ident[:])
                    ins.then_inc(f["tr"], 1)

                def pre_g(base, c):
                    wait(pe, f["xlo"], base, c + 1)
                    for i in range(CT):
                        ins = nc.tensor.transpose(PS[7][0:E, i * P:(i + 1) * P], f_g[:, i], ident[:])
                    ins.then_inc(f["gtr"], 1)

                def chunk(base, off, last=False):
                    for n in range(NB + 2):
                        e, b = divmod(n, nb)
                        if n < NB:
                            if n == 0:
                                wait(pe, f["xlo"], base, off + 1)
                            wait(pe, f["gelu"], base, off, NB, n - 3)
                            mm3(PS[n % 4][:], WHI[:, W1o + n * P:W1o + (n + 1) * P], WLO[:, W1o + n * P:W1o + (n + 1) * P],
                                xTh[:, off % 2], xTl[:, off % 2]).then_inc(f["h"], 1)
                            if b == 0:
                                if e == 0:
                                    wait(pe, f["gtl"], base, off + 1)
                                wait(pe, f["mc"], base, off, E, e)
                                nc.tensor.matmul(PS[6][:], SEL[:, e], gTh, start=True, stop=False)
                                nc.tensor.matmul(PS[6][:], SEL[:, e], gTl, start=False, stop=True).then_inc(f["m"], 1)
                        if n >= 2:
                            m = n - 2
                            e, b = divmod(m, nb)
                            wait(pe, f["glo"], base, off, NB, m + 1)
                            if b == 0:
                                wait(pe, f["tmp"], base, off, E, e - 1)
                            mm3(PS[4 + e % 2][:], WHI[:, W2o + m * P:W2o + (m + 1) * P], WLO[:, W2o + m * P:W2o + (m + 1) * P],
                                Gh[:, m % 2], Gl[:, m % 2], start=b == 0, stop=b == nb - 1).then_inc(f["yb"], 1)
                        if n == 2 * nb and not last:
                            pre_x(base, off + 1)
                        if n == 5 * nb and not last:
                            pre_g(base, off + 1)
                    wait(pe, f["acc"], base, off, E - 1, E - 1)
                    if not last:
                        wait(pe, f["gtl"], base, off + 2)
                    for i in range(CT):
                        ins = nc.tensor.transpose(PS[7][:, i * P:(i + 1) * P], f_acc[:, off % 2, i * P:(i + 1) * P], ident[:])
                    ins.then_inc(f["at"], 1)
                pre_x(0, 0)
                pre_g(0, 0)
                rounds(pe, CHUNKS - 2, 1, 2, chunk, 2)
                chunk(CHUNKS - 2, 1, True)

            if PHASES >= 2:
                router(0)
                ffn(0)

            def gru(i, k):
                w = k % 4
                if liveq(i, k):
                    T = PS[7 * (k % 2)]
                    if k // 4 == 0:
                        waitp(pe, C["xn"], i, k, 1)
                    else:
                        waitq(pe, C["h"], i, k, -3)
                    waitq(pe, C["ml"], i, k, -1)
                    waitq(pe, C["hl"], i, k, -1)
                    for j in range(CT):
                        src = q_xn[:, k % 2, j] if k // 4 == 0 else q_h[:, w, j * P:(j + 1) * P]
                        ins = nc.tensor.transpose(T[:, j * P:(j + 1) * P], src, ident[:])
                    ins.then_inc(C["tr"], 1)
                if liveq(i, k - 1):
                    u = k - 1
                    waitq(pe, C["ml"], i, u, 1)
                    if u // 4 % 3 == 0:
                        waitp(pe, C["adj"], i, u, 1)
                    waitq(pe, C["al"], i, u)
                    for g in range(2):
                        for j in range(HALVES):
                            t = g * HALVES + j
                            for m in (q_mh, q_ml):
                                ins = nc.tensor.matmul(PS[1][:, g * N:(g + 1) * N], m[:, u % 2, t * P:(t + 1) * P], q_A[:, u % 4, t],
                                                       start=j == 0 and m is q_mh, stop=j == 1 and m is q_ml)
                    ins.then_inc(C["ag"], 1)
                if liveq(i, k - 2):
                    u = k - 2
                    lay = u // 4 % LAYERS
                    ai, hi = (q_ah[:, u % 2], q_al[:, u % 2]), (q_hh[:, u % 4], q_hl[:, u % 4])

                    def part(bank, row, rhs, start, stop):
                        return mm3(PS[bank][:], WGH[:, row * P:(row + 1) * P], WGL[:, row * P:(row + 1) * P], *rhs, start, stop)
                    waitq(pe, C["hl"], i, u, 1)
                    waitq(pe, C["r"], i, u)
                    part(2, 9, hi, True, False)
                    waitq(pe, C["al"], i, u, 1)
                    part(2, 3 * lay, ai, False, True).then_inc(C["gr"], 1)
                    waitq(pe, C["z"], i, u)
                    part(3, 10, hi, True, False)
                    part(3, 3 * lay + 1, ai, False, True).then_inc(C["gz"], 1)
                    waitq(pe, C["t2"], i, u)
                    part(4, 11, hi, True, True)
                    part(5, 3 * lay + 2, ai, True, True).then_inc(C["gn"], 1)
                if liveq(i, k - 4) and (k - 4) % UNITS >= UNITS - 4:
                    u = k - 4
                    waitq(pe, C["h"], i, u, 1)
                    waitp(pe, C["res"], i, u)
                    for j in range(CT):
                        ins = nc.tensor.transpose(PS[6][:, j * P:(j + 1) * P], q_h[:, u % 4, j * P:(j + 1) * P], ident[:])
                    ins.then_inc(C["ft"], 1)

            if PHASES >= 3:
                unit_rounds(pe, 5, gru)
            if PHASES >= 4:
                pe.wait_ge(s_raw1, 32)
                pe.wait_ge(C["t2"], QUADS * UNITS)
                for n in range(E * HID1 // P):
                    e, b = divmod(n, HID1 // P)
                    ins = nc.tensor.matmul(PS[4][:, n:n + 1], raw1b[:, e, b * P:(b + 1) * P], COLS[:, R_B + e:R_B + e + 1], start=True, stop=True)
                ins.then_inc(s_bias, 1)
                pe.wait_ge(s_wlo, 4)
                router(1)
                ffn(1)


_INS = ['x', 'adj', 'L0_gnn_W', 'L0_gnn_a_src', 'L0_gnn_a_dst', 'L0_ffn_Wg', 'L0_ffn_bg', 'L0_ffn_W1', 'L0_ffn_b1',
        'L0_ffn_W2', 'L0_ffn_b2', 'L1_gnn_weight', 'L1_gnn_w_ih', 'L1_gnn_w_hh', 'L1_gnn_b_ih', 'L1_gnn_b_hh',
        'L1_ffn_Wr', 'L1_ffn_br', 'L1_ffn_ln_g', 'L1_ffn_ln_b', 'L1_ffn_W1', 'L1_ffn_b1', 'L1_ffn_W2', 'L1_ffn_b2']


def kernel(**inputs):
    import numpy as np
    import concourse.bacc as bacc
    from concourse.bass_utils import run_bass_kernel_spmd

    nc = bacc.Bacc("TRN2", target_bir_lowering=False, num_devices=1)
    arrays, args = {}, []
    for name in _INS:
        a = np.ascontiguousarray(inputs[name])
        arrays[f"in_{name}"] = a
        args.append(nc.dram_tensor(f"in_{name}", a.shape, mybir.dt.from_np(a.dtype), kind="ExternalInput").ap())
    args.append(nc.dram_tensor("out_x", (B, N, D), F32, kind="ExternalOutput").ap())
    build(nc, *args)
    r = run_bass_kernel_spmd(nc, [arrays], core_ids=[0])
    return r.results[0]["out_x"]
```

```python
import concourse.bass as bass
from concourse import mybir
from concourse.alu_op_type import AluOpType as ALU
from contextlib import ExitStack

F32 = mybir.dt.float32
F32R = mybir.dt.float32r
BF16 = mybir.dt.bfloat16
I32 = mybir.dt.int32
U32 = mybir.dt.uint32
ACT = mybir.ActivationFunctionType
AX = mybir.AxisListType

P = 128
B, N, D = 32, 256, 128
HALVES = N // P
TILES = B * HALVES
E = 8
CH = 512
CT = CH // P
CHUNKS = TILES // CT
HID0, HID1 = 256, 512
LAYERS = 3
NEG_INF = -1e9
SLOPE = 0.2
EPS = 1e-5
U = 4

R_A, R_B1A, R_B1B, R_B2A, R_B2B, R_G, R_B, R_IH, R_HH, R_END = 0, 2, 18, 50, 58, 66, 74, 82, 85, 88
PHASES = 9

PAIRS = 2 * TILES * P
V = 3
NBLK = (PAIRS + E * (CH - 1)) // CH
assert NBLK % V == 0
REGION = TILES * P + CH
SPARE = E * REGION
ROWS_X = SPARE + (NBLK - PAIRS // CH) * CH
RW = D + 4
C_ID, C_W = D, D + 1
NOPAIR = 65536.0


def wait(eng, sem, base, off, mul=1, add=0):
    v = base * mul + (off * mul + add)
    if not isinstance(v, int) or v > 0:
        eng.wait_ge(sem, v)


def rounds(eng, n, depth, first, step, U=U):
    for k in range(first):
        step(0, k)
    with eng.Fori(first // U, n // U) as i:
        for u in range(U):
            step(i * U, u)
    for k in range(depth):
        step(n, k)


def block_rounds(eng, depth, step):
    for k in range(2 * V):
        step(0, k)
    with eng.Fori(2, NBLK // V) as i:
        for k in range(V):
            step(i, k)
    for k in range(depth):
        step(NBLK // V, k)


def waits(eng, sem, i, off, each, add=0):
    v = i * each + (off // V * each + add)
    if not isinstance(v, int) or v > 0:
        eng.wait_ge(sem, v)


def wait2(eng, sem, base, off, mul, add=0):
    v = base * (mul // 2) + (off // 2 * mul + add)
    if not isinstance(v, int) or v > 0:
        eng.wait_ge(sem, v)


def live(base, off, n):
    return not isinstance(base, int) or 0 <= base + off < n


UNITS = LAYERS * 4
QUADS = B // 2 // 4


def waitq(eng, sem, i, off, add=0):
    v = i * UNITS + (off + add)
    if not isinstance(v, int) or v > 0:
        eng.wait_ge(sem, v)


def waitp(eng, sem, i, off, add=0):
    v = i * 4 + (off // UNITS * 4 + off % 4 + add)
    if not isinstance(v, int) or v > 0:
        eng.wait_ge(sem, v)


def liveq(i, off):
    return not isinstance(i, int) or 0 <= i * UNITS + off < QUADS * UNITS


def unit_rounds(eng, depth, step):
    for k in range(UNITS):
        step(0, k)
    with eng.Fori(1, QUADS) as i:
        for k in range(UNITS):
            step(i, k)
    for k in range(depth):
        step(QUADS, k)


def build(nc, x, adj, gW, g_src, g_dst, f0_Wg, f0_bg, f0_W1, f0_b1, f0_W2, f0_b2,
          gr_w, gr_wih, gr_whh, gr_bih, gr_bhh, f1_Wr, f1_br, f1_g, f1_b, f1_W1, f1_b1, f1_W2, f1_b2, out):
    ctx = ExitStack()
    with ctx:
        def sb(name, shape, dt=F32):
            return ctx.enter_context(nc.sbuf_tensor(name, shape, dt))

        def sem(name):
            return ctx.enter_context(nc.semaphore(name))

        X = sb("X", [P, TILES, D])
        ADJ = sb("ADJ", [P, TILES, N], BF16)
        WHI = sb("WHI", [P, 8192], F32R)
        WLO = sb("WLO", [P, 8192], F32R)
        FA = sb("FA", [P, 8448])
        RA = sb("RA", [P, 5120], F32R)
        ident = sb("ident", [P, P])
        ones = sb("ones", [P, P])
        iota8 = sb("iota8", [P, E])
        bidx = sb("bidx", [P, NBLK])
        zero = sb("zero", [P, 2 * CT])
        padr = sb("padr", [P, RW])
        ST = sb("ST", [P, TILES, 6])
        MEAN = sb("MEAN", [P, TILES])
        RSTD = sb("RSTD", [P, TILES])
        NT = sb("NT", [P, 2, TILES])
        RUN = sb("RUN", [P, E])
        RUNU = sb("RUNU", [P, E], U32)
        TBU = sb("TBU", [P, 3, NBLK], U32)
        TID = sb("TID", [P, TILES])
        TRI = sb("TRI", [P, P])
        TRIR = sb("TRIR", [P, P], BF16)
        ONER = sb("ONER", [P, P], BF16)
        OHR = sb("OHR", [P, 2, (4 * CT + 1) * E], BF16)
        BX0 = sb("BX0", [P, E, HID0 // P + 1])
        BX1 = sb("BX1", [P, E, HID1 // P + 1])
        BS = sb("BS", [P, V, HID1 // P + 1])
        ROWS = sb("ROWS", [R_END, P])
        COLS = sb("COLS", [P, R_END])
        gWr = sb("gWr", [P, D])
        WE = sb("WE", [P, D + 2])
        wdst = sb("wdst", [P, P])
        wg = sb("wg", [P, 2 * E])
        wgh = sb("wgh", [P, 2 * E], F32R)
        wgl = sb("wgl", [P, 2 * E], F32R)
        bg = sb("bg", [P, 2, E])
        brz = sb("brz", [P, 2])
        WGH = sb("WGH", [P, 12 * P], F32R)
        WGL = sb("WGL", [P, 12 * P], F32R)

        PS = [ctx.enter_context(nc.psum_tensor(f"PS{i}", [P, 512], F32)) for i in range(8)]

        x_t = x.rearrange("g (r p) d -> p (g r) d", p=P)
        out_t = out.rearrange("g (r p) d -> p (g r) d", p=P)
        adj_t = adj.rearrange("g (r p) n -> g p r n", p=P)

        def fa(off, *shape):
            n = 1
            for s in shape:
                n *= s
            v = FA[:, off:off + n]
            if len(shape) == 2:
                v = v.rearrange("p (a b) -> p a b", a=shape[0])
            elif len(shape) == 3:
                v = v.rearrange("p (a b c) -> p a b c", a=shape[0], b=shape[1])
            return v

        raw1 = fa(0, E, HID0)
        raw2 = fa(2048, 2 * E, D)
        rgw = fa(4096, 3, P)
        rih = fa(4480, 3, P)
        rhh = fa(4864, 3, P)
        gwT = fa(5248, 3, P)
        ihT = fa(5632, 3 * P)

        a_xn = fa(0, 2, HALVES, D)
        a_xT = fa(512, 2, N)
        a_h = fa(1024, 4, HALVES, D + 1)
        a_ss = fa(2056, 4, HALVES)
        a_t = fa(2080, 2, HALVES, N)
        a_em = fa(3104, 2, HALVES, N)
        a_p = fa(4128, 2, HALVES, N)
        a_pT = fa(5152, 2, HALVES, N)
        a_mx = fa(6176, 2, HALVES)
        a_rc = fa(6184, 2, HALVES)
        adjst = fa(6208, U, HALVES * N).bitcast(I32)

        f_y = fa(0, 4, CT, D)
        XR = fa(2048, 4, CT, RW).rearrange("p (s k) t w -> p s k t w", k=2)
        V6 = fa(4688, 4, CT, 6)
        V4 = fa(4784, 6, 4, CT)
        L8 = fa(4880, 2, CT, E)
        M8 = fa(4944, 2, CT, 8)
        I8 = fa(5008, 2, CT, 8).bitcast(U32)
        IF = fa(5072, 2, CT, 2)
        OH = fa(5088, 4, 2 * CT, E)
        D8 = fa(5344, 4, CT, E)
        Q8 = fa(5472, 2, CT, E)
        T64 = fa(5536, 2, 2 * CT, E)
        N4 = fa(5664, 2, 2, CT)
        PF = fa(5680, 2, 2 * CT)
        POSU = fa(5696, 2, 2 * CT).bitcast(U32)
        PU = fa(6768, 2, 2 * CT).bitcast(U32)
        W2 = fa(5712, 2, 2, CT)
        tb = fa(5728, 8, NBLK)
        t8 = fa(6048, 8, E)
        t8i = fa(6112, 2, E).bitcast(I32)
        tge = fa(6128, E, NBLK)
        tgr = fa(6448, E, NBLK)
        XB = fa(0, V, CT, RW)
        f_G = fa(1584, 2, CH)
        f_ye = fa(2608, V, CH)
        YB = fa(4144, V, CT, D)
        IDF = fa(5680, V, CT).bitcast(U32)
        IDX = fa(5692, V, CT).bitcast(U32)
        WR = fa(5704, V, CT)
        YL = fa(0, 4, CT, D).rearrange("p (s k) t d -> p s k t d", k=2)
        xTh = RA[:, 0:1536].rearrange("p (a b) -> p a b", a=V)
        xTl = RA[:, 1536:3072].rearrange("p (a b) -> p a b", a=V)
        Gh = RA[:, 3072:4096].rearrange("p (a b) -> p a b", a=2)
        Gl = RA[:, 4096:5120].rearrange("p (a b) -> p a b", a=2)
        WS = WHI[:, 0:4 * HID1 * V].rearrange("p (a b) -> p a b", a=V)

        XS = nc.dram_tensor("XS", [ROWS_X, RW], F32, kind="Internal").ap()
        YD = nc.dram_tensor("YD", [PAIRS, D], F32, kind="Internal").ap()
        WD = [nc.dram_tensor(f"WD{l}", [E, P, 4 * h], F32, kind="Internal").ap() for l, h in enumerate((HID0, HID1))]
        BD = [nc.dram_tensor(f"BD{l}", [E, P, h // P + 1], F32, kind="Internal").ap() for l, h in enumerate((HID0, HID1))]

        q_hh = WHI[:, 0:2048].rearrange("p (a b) -> p a b", a=4)
        q_A = WHI[:, 2048:6144].rearrange("p (a t n) -> p a t n", a=4, t=CT)
        q_mh = WHI[:, 6144:7168].rearrange("p (a b) -> p a b", a=2)
        q_ah = WHI[:, 7168:8192].rearrange("p (a b) -> p a b", a=2)
        q_hl = WLO[:, 0:2048].rearrange("p (a b) -> p a b", a=4)
        q_ml = WLO[:, 6144:7168].rearrange("p (a b) -> p a b", a=2)
        q_al = WLO[:, 7168:8192].rearrange("p (a b) -> p a b", a=2)
        q_h = fa(0, 4, CH)
        q_xn = fa(2048, 2, CT, D)
        q_r = fa(3072, 2, CH)
        q_z = fa(4096, 2, CH)
        q_t = fa(5120, 2, CH)
        q_n = fa(6144, 2, CH)
        q_d = fa(7168, 2, CH)
        rawb = ADJ[:].rearrange("p a b -> p (a b)").bitcast(F32)
        raw1b = rawb[:, 0:4096].rearrange("p (a b) -> p a b", a=E)
        raw2b = rawb[:, 4096:8192].rearrange("p (a b) -> p a b", b=D)

        s_x = [sem(f"s_x{i}") for i in range(4)]
        s_vec, s_wg, s_raw, s_gru = (sem(n) for n in ("s_vec", "s_wg", "s_raw", "s_gru"))
        s_const = sem("s_const")
        s_ident = sem("s_ident")
        s_prep = sem("s_prep")
        s_prepv = sem("s_prepv")
        s_hi, s_lo, s_whi, s_wlo = (sem(n) for n in ("s_hi", "s_lo", "s_whi", "s_wlo"))
        s_dve = sem("s_dve")
        s_var, s_sqrt = sem("s_var"), sem("s_sqrt")
        s_adj = [sem(f"s_adj{i}") for i in range(U)]
        (a_norm, a_tr, a_trc, a_prod, a_hc, a_e, a_fill, a_lk, a_sel, a_max, a_exp, a_ptr, a_ptc, a_out, a_rec,
         a_res, a_stat) = (sem("a_" + n) for n in (
            "norm", "tr", "trc", "prod", "hc", "e", "fill", "lk", "sel", "max", "exp", "ptr", "ptc", "out", "rec",
            "res", "stat"))
        C = {n: sem(f"c_{n}") for n in ("xn", "adj", "tr", "h0", "hh", "hl", "mh", "ml", "ag", "ah", "al", "gr", "gz", "gn",
                                        "r", "z", "t1", "t2", "n", "d", "zd", "h", "ft", "res")}
        s_raw1, s_scaled = sem("s_raw1"), sem("s_scaled")
        s_out = sem("s_out")
        R = [{n: sem(f"r{l}_{n}") for n in ("norm", "tr", "hi", "lo", "log", "lg", "max", "s2", "ohr", "pre", "pos", "rows", "s4",
                                            "posu") + ("ex", "exd", "var", "sq", "s0", "s1") * l} for l in range(2)]
        F = [{n: sem(f"f{l}_{n}") for n in ("tr", "xhi", "xlo", "h", "gelu", "g", "yb", "yev", "yt", "wsc", "ix", "ixu", "ysum",
                                            "res") + ("st",) * (1 - l)} for l in range(2)]
        d_xs, d_xb, d_ws, d_ys, d_yl = ([sem(f"d_{n}{i}") for i in range(k)] for n, k in (("xs", 2), ("xb", V), ("ws", V), ("ys", V), ("yl", 2)))
        XS_L, XB_L, WS_L, YS_L, YL_L = (16 * 2 * CT * CHUNKS // 2, 16 * NBLK // V, 32 * NBLK // V, 16 * CT * NBLK // V,
                                        32 * CHUNKS // 2)
        s_run, s_pad = sem("s_run"), sem("s_pad")
        s_wd, s_padc, s_tab, s_bx = (sem(n) for n in ("s_wd", "s_padc", "s_tab", "s_bx"))
        INIT = 16 * ((ROWS_X - SPARE) // CH)
        NBS = (HID0 // P, HID1 // P)
        BX = (BX0, BX1)

        tick = [0]

        def own(dve, ins):
            tick[0] += 1
            ins.then_inc(s_dve, 1)
            dve.wait_ge(s_dve, tick[0])

        def carried(eng):
            eng.wait_ge(*((s_x[0], 16) if eng is nc.gpsimd else (s_ident, 2)))

        def tile(g, r, h=HALVES):
            return bass.ds(g * h + r, 1)

        block = ctx.enter_context(nc.Block())

        @block.sync
        def _(sp):
            for i in range(4):
                sl = slice(i * TILES // 4, (i + 1) * TILES // 4)
                sp.dma_start(X[:, sl, :], x_t[:, sl, :]).then_inc(s_x[i], 16)
                if i == 0:
                    sp.dma_start(gWr[:], gW).then_inc(s_vec, 16)
                    rows = [(R_A, g_src.rearrange("(a d) -> a d", a=1)), (R_A + 1, g_dst.rearrange("(a d) -> a d", a=1)),
                            (R_B1A, f0_b1.rearrange("e (b p) -> (e b) p", p=P)), (R_B1B, f1_b1.rearrange("e (b p) -> (e b) p", p=P)),
                            (R_B2A, f0_b2), (R_B2B, f1_b2), (R_G, f1_g), (R_B, f1_b),
                            (R_IH, gr_bih.rearrange("(a p) -> a p", p=P)), (R_HH, gr_bhh.rearrange("(a p) -> a p", p=P))]
                    for r, src in rows:
                        sp.dma_start(ROWS[r:r + src.shape[0], :], src).then_inc(s_vec, 16)
                    sp.dma_start(raw1, f0_W1.rearrange("e d h -> d e h")).then_inc(s_raw, 16)
                    sp.dma_start(raw2, f0_W2.rearrange("e (b p) d -> p (e b) d", p=P)).then_inc(s_raw, 16)
            for w, raw in ((f1_W1.rearrange("e d h -> d e h"), raw1b), (f1_W2.rearrange("e (b p) d -> p (e b) d", p=P), raw2b)):
                sp.dma_start(raw, w).then_inc(s_raw1, 16)
            sp.wait_ge(s_padc, 2)
            for i in range((ROWS_X - SPARE) // CH):
                sp.dma_start(XS[SPARE + i * CH:SPARE + (i + 1) * CH, :].rearrange("(p i) w -> p i w", i=CT), padr[:][:, None, :].to_broadcast([P, CT, RW])).then_inc(s_wd, 16)
            for l, hid in enumerate((HID0, HID1)):
                for half, src, done in ((0, WHI, s_whi), (1, WLO, s_wlo)):
                    sp.wait_ge(done, 2 + 2 * l)
                    for k in range(2):
                        o = (2 * half + k) * hid
                        sp.dma_start(WD[l].rearrange("e p h -> p e h")[:, :, o:o + hid],
                                     src[:, k * E * hid:(k + 1) * E * hid].bitcast(F32).rearrange("p (e h) -> p e h", e=E)).then_inc(s_wd, 16)
                sp.wait_ge(s_bx, l + 1)
                sp.dma_start(BD[l].rearrange("e p c -> p e c"), BX[l][:]).then_inc(s_wd, 16)
            sp.wait_ge(s_wlo, 4)

            def adj_round(base, off):
                wait(sp, a_sel, base, off - U + 1)
                sp.dma_start(adjst[:, off % U, :].rearrange("p (r n) -> p r n", r=HALVES)[:, None],
                             adj_t[bass.ds(base + off, 1)].rearrange("g p r n -> p g r n")).then_inc(s_adj[off % U], 16)
            rounds(sp, B, 0, U, adj_round)


            def pads(l):
                sp.wait_ge(s_run, l + 1)
                for done in d_xs:
                    sp.wait_ge(done, (l + 1) * XS_L)
                for e in range(E):
                    end = sp.value_load(RUNU[0:1, e:e + 1], min_val=0, max_val=SPARE - CH)
                    sp.dma_start(XS[bass.ds(end, CH), :].rearrange("(p i) w -> p i w", i=CT), padr[:][:, None, :].to_broadcast([P, CT, RW])).then_inc(s_pad, 16)
                sp.wait_ge(s_pad, 16 * E * (l + 1))
                sp.wait_ge(s_tab, l + 1)

            def ffn(l):
                f, nb = F[l], NBS[l]
                hid = nb * P

                def block_loads(i, off):
                    base, slot = i * V, off % V
                    if live(base, off, NBLK):
                        row = sp.value_load(TBU[0:1, 0, bass.ds(base + off, 1)], min_val=0, max_val=ROWS_X - CH)
                        wait(sp, f["tr"], base, off - V + 1)
                        wait(sp, f["ix"], base, off - V + 1)
                        sp.dma_start(XB[:, slot], XS[bass.ds(row, CH), :].rearrange("(p i) w -> p i w", i=CT)).then_inc(d_xb[slot], 16)
                    if live(base, off - 1, NBLK):
                        b = off - 1
                        slot = b % V
                        wait(sp, f["yb"], base, b - V + 1, nb)
                        ex = sp.value_load(TBU[0:1, 1, bass.ds(base + b, 1)], min_val=0, max_val=E - 1)
                        new = sp.value_load(TBU[0:1, 2, bass.ds(base + b, 1)], min_val=0, max_val=1)
                        sp.dma_start(WS[:, slot:slot + 1, 0:4 * hid].bitcast(F32), WD[l][bass.ds(ex, 1)].rearrange("e p h -> p e h"),
                                     cond=new).then_inc(d_ws[slot], 16)
                        wait(sp, f["yev"], base, b - V + 1)
                        sp.dma_start(BS[:, slot:slot + 1, 0:nb + 1], BD[l][bass.ds(ex, 1)].rearrange("e p h -> p e h"),
                                     cond=new).then_inc(d_ws[slot], 16)
                block_rounds(sp, 1, block_loads)
                for done in d_ys:
                    sp.wait_ge(done, (l + 1) * YS_L)

                def chunk_loads(base, off):
                    wait(sp, f["ysum"], base, off - 1)
                    wait(sp, f["res"], base, off - 1)
                    for k in range(2):
                        sp.dma_start(YL[:, off % 2, k], YD[bass.ds((base + off) * CH + k * TILES * P, CH), :]
                                     .rearrange("(i p) d -> p i d", p=P)).then_inc(d_yl[off % 2], 16)
                    if l == 1 and live(base, off - 2, CHUNKS):
                        store(base, off - 2)
                rounds(sp, CHUNKS, 0, 4, chunk_loads)

            def store(base, c):
                wait(sp, F[1]["res"], base, c + 1)
                ts = bass.ds((base + c) * CT, CT)
                sp.dma_start(out_t[:, ts, :], X[:, ts, :]).then_inc(s_out, 16)

            if PHASES >= 2:
                sp.wait_ge(s_wd, INIT + 160)
                pads(0)
                ffn(0)
            if PHASES >= 4:
                pads(1)
                ffn(1)
                store(CHUNKS, -2)
                store(CHUNKS, -1)
                sp.wait_ge(s_out, 16 * CHUNKS)
            else:
                if PHASES == 1:
                    sp.wait_ge(a_res, B)
                elif PHASES == 2:
                    sp.wait_ge(F[0]["res"], CHUNKS)
                else:
                    sp.wait_ge(C["res"], B // 2)
                sp.dma_start(out_t, X[:]).then_inc(s_out, 16)
                sp.wait_ge(s_out, 16)

        @block.gpsimd
        def _(pool):
            pool.memset(ident[:], 0.0).then_inc(s_ident, 1)
            pool.memset(ones[:], 1.0).then_inc(s_const, 1)
            pool.memset(zero[:], 0.0).then_inc(s_const, 1)
            pool.iota(iota8[:], pattern=[[1, E]], base=0, channel_multiplier=0, allow_small_or_imprecise_dtypes=True).then_inc(s_const, 1)
            pool.iota(bidx[:], pattern=[[1, NBLK]], base=0, channel_multiplier=0, allow_small_or_imprecise_dtypes=True).then_inc(s_const, 1)
            pool.iota(TID[:], pattern=[[P, TILES]], base=0, channel_multiplier=1, allow_small_or_imprecise_dtypes=True).then_inc(s_const, 1)
            pool.wait_ge(s_ident, 1)
            pool.affine_select(out=ident[:], in_=ident[:], compare_op=ALU.not_equal, fill=1.0, base=0,
                               pattern=[[-1, P]], channel_multiplier=1).then_inc(s_ident, 1)
            pool.wait_ge(s_const, 2)
            pool.affine_select(out=TRI[:], in_=ones[:], compare_op=ALU.is_gt, fill=0.0, base=0,
                               pattern=[[1, P]], channel_multiplier=-1).then_inc(s_const, 1)
            pool.wait_ge(s_whi, 2)
            pool.wait_ge(s_wlo, 2)
            for i in range(4):
                pool.memset(a_h[:, i, :, D:D + 1], 1.0).then_inc(s_const, 1)

            def router(l):
                r = R[l]

                def chunk(base, off):
                    if live(base, off - 3, CHUNKS):
                        c = off - 3
                        wait(pool, r["rows"], base, c + 1)
                        nc.gpsimd.tensor_tensor(POSU[:, c % 2], PU[:, c % 2], zero[:].bitcast(U32), ALU.add).then_inc(r["posu"], 1)
                        carried(pool)
                        wait(pool, r["posu"], base, c + 1)
                        for j in range(2 * CT):
                            pool.indirect_dma_start(XS, bass.IndirectOffsetOnAxis(ap=POSU[:, c % 2, j:j + 1], axis=0),
                                                    XR[:, c % 2, j // CT, j % CT], None).then_inc(d_xs[c % 2], 16)
                rounds(pool, CHUNKS, 3, 8, chunk)

            def ffn(l):
                f = F[l]

                def block_round(i, off):
                    base = i * V
                    if live(base, off - 3, NBLK):
                        b = off - 3
                        waits(pool, d_ys[b % V], i, b, 16 * CT, l * YS_L)
                        wait(pool, f["wsc"], base, b + 1)
                        nc.gpsimd.tensor_tensor(IDX[:, b % V], IDF[:, b % V], zero[:, 0:CT].bitcast(U32), ALU.add).then_inc(f["ixu"], 1)
                        carried(pool)
                        wait(pool, f["ixu"], base, b + 1)
                        for j in range(CT):
                            pool.indirect_dma_start(YD, bass.IndirectOffsetOnAxis(ap=IDX[:, b % V, j:j + 1], axis=0),
                                                    YB[:, b % V, j], None, bounds_check=PAIRS - 1,
                                                    oob_is_err=False).then_inc(d_ys[b % V], 16)
                block_rounds(pool, 3, block_round)

                def chunk(base, off):
                    wait2(pool, d_yl[off % 2], base, off, 32, 32 + l * YL_L)
                    pool.tensor_tensor(YL[:, off % 2, 0], YL[:, off % 2, 0], YL[:, off % 2, 1], ALU.add).then_inc(f["ysum"], 1)
                rounds(pool, CHUNKS, 0, 4, chunk)

            if PHASES >= 2:
                router(0)
                ffn(0)

            def gru(i, k):
                if liveq(i, k - 3):
                    u = k - 3
                    waitq(pool, C["zd"], i, u, 1)
                    pool.tensor_tensor(q_h[:, u % 4], q_n[:, u % 2], q_d[:, u % 2], ALU.add).then_inc(C["h"], 1)
            if PHASES >= 3:
                unit_rounds(pool, 5, gru)
            if PHASES >= 4:
                router(1)
                ffn(1)

        @block.scalar
        def _(act):
            act.dma_start(wg[:, 0:E], f0_Wg).then_inc(s_wg, 16)
            act.dma_start(wg[:, E:], f1_Wr).then_inc(s_wg, 16)
            act.dma_start(bg[:, 0], f0_bg.rearrange("(a e) -> a e", a=1).to_broadcast([P, E])).then_inc(s_wg, 16)
            act.dma_start(bg[:, 1], f1_br.rearrange("(a e) -> a e", a=1).to_broadcast([P, E])).then_inc(s_wg, 16)
            act.dma_start(rgw, gr_w.rearrange("i d e -> d i e")).then_inc(s_gru, 16)
            act.dma_start(rih, gr_wih.rearrange("(a o) k -> o a k", o=P)).then_inc(s_gru, 16)
            act.dma_start(rhh, gr_whh.rearrange("(a o) k -> o a k", o=P)).then_inc(s_gru, 16)
            act.wait_ge(s_prep, 1)
            nc.scalar.copy(COLS[:], PS[0][:, 0:R_END]).then_inc(s_prepv, 1)
            nc.scalar.copy(WE[:, 0:D], PS[1][:, 0:D]).then_inc(s_prepv, 1)
            act.wait_ge(s_prep, 2)
            nc.scalar.copy(WE[:, D:D + 2], PS[0][:, 128:130]).then_inc(s_prepv, 1)
            act.wait_ge(s_prep, 3)
            nc.scalar.copy(gwT, PS[2][:, 0:3 * P].rearrange("p (a b) -> p a b", a=3)).then_inc(s_prepv, 1)
            nc.scalar.copy(ihT, PS[3][:, 0:3 * P]).then_inc(s_prepv, 1)
            nc.scalar.copy(WGH[:, 9 * P:], PS[4][:, 0:3 * P]).then_inc(s_hi, 1)
            for i in range(LAYERS):
                act.wait_ge(s_prep, 4 + i)
                nc.scalar.copy(WGH[:, 3 * i * P:3 * (i + 1) * P], PS[5 + i][:, 0:3 * P]).then_inc(s_hi, 1)
            act.wait_ge(s_wg, 64)
            nc.scalar.copy(wgh[:], wg[:]).then_inc(s_hi, 1)
            act.wait_ge(s_raw, 32)
            nc.scalar.copy(WHI[:, 0:2048], FA[:, 0:2048]).then_inc(s_whi, 1)
            nc.scalar.copy(WHI[:, 2048:4096], FA[:, 2048:4096]).then_inc(s_whi, 1)

            act.wait_ge(s_raw1, 32)
            nc.scalar.copy(WHI[:, 4096:8192], rawb[:, 4096:8192]).then_inc(s_whi, 1)
            act.wait_ge(s_wd, INIT + 80)
            act.wait_ge(s_scaled, 1)
            nc.scalar.copy(WHI[:, 0:4096], rawb[:, 0:4096]).then_inc(s_whi, 1)

            act.wait_ge(s_var, 1)
            nc.scalar.activation(NT[:, 1], NT[:, 1], ACT.Sqrt).then_inc(s_sqrt, 1)
            act.wait_ge(s_wlo, 2)

            def att_round(base, off):
                if live(base, off - 1, B):
                    g = off - 1
                    wait(act, a_tr, base, g + 1)
                    wait(act, a_prod, base, g - 1)
                    nc.scalar.copy(a_xT[:, g % 2], PS[g % 2][:, 0:N]).then_inc(a_trc, 1)
                if live(base, off - 2, B):
                    g = off - 2
                    wait(act, a_max, base, g + 1)
                    wait(act, a_ptr, base, g - 1)
                    for r in range(HALVES):
                        ins = nc.scalar.activation(a_p[:, g % 2, r], a_em[:, g % 2, r], ACT.Exp,
                                                   bias=a_mx[:, g % 2, r:r + 1])
                    ins.then_inc(a_exp, 1)
                if live(base, off - 1, B):
                    g = off - 1
                    wait(act, a_prod, base, g + 1)
                    wait(act, a_out, base, g - 3)
                    src = PS[2 + g % 2][:, 0:2 * (D + 1)].rearrange("p (r c) -> p r c", r=HALVES)
                    nc.scalar.copy(a_h[:, g % 4, :, 0:D], src[:, :, 0:D]).then_inc(a_hc, 1)
                    nc.scalar.copy(a_ss[:, g % 4], src[:, :, D]).then_inc(a_hc, 1)
                    wait(act, a_hc, base, g, 2, 2)
                    wait(act, a_sel, base, g - 1)
                    for r in range(HALVES):
                        ins = nc.scalar.activation(a_t[:, g % 2, r], PS[g % 2][:, N:2 * N], ACT.Identity,
                                                   bias=a_ss[:, g % 4, r:r + 1])
                    ins.then_inc(a_e, 1)
            rounds(act, B, 4, 8, att_round)

            def router(l):
                r = R[l]

                def chunk(base, off):
                    if live(base, off - 1, CHUNKS):
                        c = off - 1
                        wait(act, r["tr"], base, c + 1)
                        wait(act, r["log"], base, c - 1)
                        nc.scalar.copy(xTh[:, c % 2], PS[c % 2][:]).then_inc(r["hi"], 1)
                    if l == 1 and live(base, off, CHUNKS):
                        wait(act, r["var"], base, off + 1)
                        nc.scalar.activation(V4[:, 2, off % 4], V4[:, 1, off % 4], ACT.Sqrt).then_inc(r["sq"], 1)
                    if l == 1 and live(base, off - 2, CHUNKS):
                        c = off - 2
                        wait(act, r["ex"], base, c + 1)
                        nc.scalar.activation(D8[:, c % 4], D8[:, c % 4], ACT.Exp).then_inc(r["exd"], 1)
                rounds(act, CHUNKS, 3, 8, chunk)

            def ffn(l):
                f, nb = F[l], NBS[l]

                def block_round(i, off):
                    base = i * V
                    for n in range(nb):
                        if live(base, off - 1, NBLK):
                            b = off - 1
                            wait(act, f["h"], base, b, nb, n + 1)
                            wait(act, f["g"], base, b, 2 * nb, 2 * (n - 1))
                            nc.scalar.activation(f_G[:, n % 2], PS[(b * nb + n) % 3][:], ACT.Gelu,
                                                 bias=BS[:, b % V, n:n + 1]).then_inc(f["gelu"], 1)
                        if n == 0 and live(base, off, NBLK):
                            wait(act, f["tr"], base, off + 1)
                            wait(act, f["h"], base, off - V + 1, nb)
                            nc.scalar.copy(xTh[:, off % V], PS[6][:]).then_inc(f["xhi"], 1)
                        if n == 1 and live(base, off - 2, NBLK):
                            b = off - 2
                            wait(act, f["yb"], base, b, nb, nb)
                            wait(act, f["yt"], base, b - V + 1)
                            nc.scalar.activation(f_ye[:, b % V], PS[3 + b % V][:], ACT.Identity,
                                                 bias=BS[:, b % V, nb:nb + 1]).then_inc(f["yev"], 1)
                block_rounds(act, 3, block_round)

            if PHASES >= 2:
                act.wait_ge(s_var, 2)
                nc.scalar.activation(NT[:, 1], NT[:, 1], ACT.Sqrt).then_inc(s_sqrt, 1)
                router(0)
                ffn(0)

            def gru(i, k):
                l, w = k // 4, k % 4
                if liveq(i, k - 3):
                    u = k - 3
                    waitq(act, C["t2"], i, u, 1)
                    waitq(act, C["h"], i, u, -1)
                    nc.scalar.activation(q_n[:, u % 2], q_t[:, u % 2], ACT.Tanh, bias=COLS[:, R_IH + 2:R_IH + 3]).then_inc(C["n"], 1)
                if liveq(i, k):
                    T = PS[7 * (k % 2)]
                    if l == 0:
                        waitq(act, C["tr"], i, k, 1)
                        waitp(act, C["ft"], i, k, -3)
                        nc.scalar.copy(q_h[:, w], T[:]).then_inc(C["h0"], 1)
                        waitq(act, C["gn"], i, k, -3)
                        nc.scalar.copy(q_hh[:, w], T[:]).then_inc(C["hh"], 1)
                        waitq(act, C["ag"], i, k, -1)
                        nc.scalar.copy(q_mh[:, k % 2], q_xn[:, k % 2].rearrange("p t d -> p (t d)")).then_inc(C["mh"], 1)
                    else:
                        waitq(act, C["tr"], i, k, 1)
                        waitq(act, C["ag"], i, k, -1)
                        nc.scalar.copy(q_mh[:, k % 2], T[:]).then_inc(C["mh"], 1)
                if liveq(i, k - 1):
                    u = k - 1
                    waitq(act, C["ag"], i, u, 1)
                    waitq(act, C["gn"], i, u, -1)
                    nc.scalar.copy(q_ah[:, u % 2], PS[1][:]).then_inc(C["ah"], 1)
                if liveq(i, k - 2):
                    u = k - 2
                    waitq(act, C["gr"], i, u, 1)
                    waitq(act, C["t1"], i, u, -1)
                    nc.scalar.activation(q_r[:, u % 2], PS[2][:], ACT.Sigmoid, bias=brz[:, 0:1]).then_inc(C["r"], 1)
                    waitq(act, C["gz"], i, u, 1)
                    waitq(act, C["zd"], i, u, -1)
                    nc.scalar.activation(q_z[:, u % 2], PS[3][:], ACT.Sigmoid, bias=brz[:, 1:2]).then_inc(C["z"], 1)
                if liveq(i, k - 3) and (k - 3) % UNITS < UNITS - 4:
                    u = k - 3
                    waitq(act, C["h"], i, u, 1)
                    waitq(act, C["gn"], i, u, 1)
                    nc.scalar.copy(q_hh[:, u % 4], q_h[:, u % 4]).then_inc(C["hh"], 1)

            if PHASES >= 3:
                act.wait_ge(s_var, 3)
                nc.scalar.activation(NT[:, 1], NT[:, 1], ACT.Sqrt).then_inc(s_sqrt, 1)
                unit_rounds(act, 5, gru)
            if PHASES >= 4:
                act.wait_ge(s_var, 4)
                nc.scalar.activation(NT[:, 1], NT[:, 1], ACT.Sqrt).then_inc(s_sqrt, 1)
                router(1)
                ffn(1)

        @block.vector
        def _(dve):
            nc.vector.memset(padr[:], 0.0).then_inc(s_padc, 1)
            dve.wait_ge(s_padc, 1)
            nc.vector.memset(padr[:, C_ID:C_ID + 1], NOPAIR).then_inc(s_padc, 1)
            for t in range(TILES):
                if t % 16 == 0:
                    dve.wait_ge(s_x[t // 16], 16)
                ins = nc.vector.bn_stats(ST[:, t], X[:, t])
            ins.then_inc(a_stat, 1)
            dve.wait_ge(s_prepv, 3)
            nc.vector.tensor_scalar(wdst[:], ones[:], WE[:, D + 1:D + 2], None, ALU.mult).then_inc(s_lo, 1)
            dve.wait_ge(s_hi, 1)
            nc.vector.tensor_tensor(WGL[:, 9 * P:], PS[4][:, 0:3 * P], WGH[:, 9 * P:].bitcast(F32), ALU.subtract).then_inc(s_lo, 1)
            for i in range(LAYERS):
                dve.wait_ge(s_hi, 2 + i)
                nc.vector.tensor_tensor(WGL[:, 3 * i * P:3 * (i + 1) * P], PS[5 + i][:, 0:3 * P],
                                        WGH[:, 3 * i * P:3 * (i + 1) * P].bitcast(F32), ALU.subtract).then_inc(s_lo, 1)
            nc.vector.tensor_tensor(brz[:], COLS[:, R_IH:R_IH + 2], COLS[:, R_HH:R_HH + 2], ALU.add).then_inc(s_lo, 1)
            dve.wait_ge(s_hi, 2 + LAYERS)
            nc.vector.tensor_tensor(wgl[:], wg[:], wgh[:].bitcast(F32), ALU.subtract).then_inc(s_lo, 1)
            for i in range(2):
                dve.wait_ge(s_whi, 1 + i)
                nc.vector.tensor_tensor(WLO[:, 2048 * i:2048 * (i + 1)], FA[:, 2048 * i:2048 * (i + 1)],
                                        WHI[:, 2048 * i:2048 * (i + 1)].bitcast(F32), ALU.subtract).then_inc(s_wlo, 1)

            def finish_stats(k, mean, rstd):
                m0, v0, m1, v1 = (ST[:, :, i] for i in (1, 2, 4, 5))
                own(dve, nc.vector.tensor_tensor(NT[:, 1], m0, m1, ALU.subtract))
                own(dve, nc.vector.scalar_tensor_tensor(out=NT[:, 1], in0=NT[:, 1], scalar=0.25, in1=NT[:, 1], op0=ALU.mult, op1=ALU.mult))
                own(dve, nc.vector.tensor_tensor(NT[:, 0], v0, v1, ALU.add))
                own(dve, nc.vector.scalar_tensor_tensor(out=NT[:, 0], in0=NT[:, 0], scalar=1.0 / D, in1=NT[:, 1], op0=ALU.mult, op1=ALU.add))
                own(dve, nc.vector.tensor_tensor(mean[:], m0, m1, ALU.add))
                own(dve, nc.vector.tensor_scalar(mean[:], mean[:], 0.5, None, ALU.mult))
                own(dve, nc.vector.tensor_scalar(NT[:, 0], NT[:, 0], EPS, None, ALU.add))
                nc.vector.tensor_scalar(NT[:, 1], NT[:, 0], 1.0, None, ALU.mult).then_inc(s_var, 1)
                dve.wait_ge(s_sqrt, k)
                own(dve, nc.vector.reciprocal(rstd[:], NT[:, 1]))
                own(dve, nc.vector.tensor_tensor(NT[:, 1], rstd[:], rstd[:], ALU.mult))
                own(dve, nc.vector.tensor_tensor(NT[:, 1], NT[:, 1], NT[:, 0], ALU.mult))
                own(dve, nc.vector.tensor_scalar(NT[:, 1], NT[:, 1], -0.5, 1.5, ALU.mult, ALU.add))
                own(dve, nc.vector.tensor_tensor(rstd[:], rstd[:], NT[:, 1], ALU.mult))

            nc.vector.tensor_copy(BX0[:, :, 0:2], COLS[:, R_B1A:R_B1A + 16].rearrange("p (e b) -> p e b", e=E))
            nc.vector.tensor_copy(BX0[:, :, 2], COLS[:, R_B2A:R_B2A + E]).then_inc(s_bx, 1)
            dve.wait_ge(s_prep, 4 + LAYERS)
            nc.vector.tensor_tensor(BX1[:, :, 0:4], PS[0][:, 256:256 + E * HID1 // P].rearrange("p (e b) -> p e b", e=E),
                                    COLS[:, R_B1B:R_B1B + E * HID1 // P].rearrange("p (e b) -> p e b", e=E), ALU.add)
            nc.vector.tensor_copy(BX1[:, :, 4], COLS[:, R_B2B:R_B2B + E]).then_inc(s_bx, 1)
            for e in range(E):
                ins = nc.vector.tensor_scalar(raw1b[:, e], raw1b[:, e], COLS[:, R_G + e:R_G + e + 1], None, ALU.mult)
            ins.then_inc(s_scaled, 1)
            dve.wait_ge(s_whi, 3)
            nc.vector.tensor_tensor(WLO[:, 4096:8192], rawb[:, 4096:8192], WHI[:, 4096:8192].bitcast(F32), ALU.subtract).then_inc(s_wlo, 1)
            dve.wait_ge(s_scaled, 1)
            dve.wait_ge(s_whi, 4)
            dve.wait_ge(s_wd, INIT + 80)
            nc.vector.tensor_tensor(WLO[:, 0:4096], rawb[:, 0:4096], WHI[:, 0:4096].bitcast(F32), ALU.subtract).then_inc(s_wlo, 1)

            dve.wait_ge(s_const, 6)
            nc.vector.tensor_copy(TRIR[:], TRI[:])
            nc.vector.tensor_copy(ONER[:], ones[:]).then_inc(s_lo, 1)
            dve.wait_ge(a_stat, 1)
            finish_stats(1, MEAN, RSTD)

            def att_round(base, off):
                if live(base, off, B):
                    g = off
                    wait(dve, a_tr, base, g - 1)
                    for r in range(HALVES):
                        t = tile(base + g, r)
                        ins = nc.vector.tensor_scalar(a_xn[:, g % 2, r][:, None], X[:, t, :], MEAN[:, t], RSTD[:, t],
                                                      ALU.subtract, ALU.mult)
                    ins.then_inc(a_norm, 1)
                if live(base, off - 2, B):
                    g = off - 2
                    wait(dve, a_exp, base, g - 1)
                    nc.vector.memset(a_em[:, g % 2], NEG_INF).then_inc(a_fill, 1)
                    wait(dve, a_e, base, g + 1)
                    nc.vector.scalar_tensor_tensor(out=a_t[:, g % 2], in0=a_t[:, g % 2], scalar=SLOPE, in1=a_t[:, g % 2],
                                                   op0=ALU.mult, op1=ALU.max).then_inc(a_lk, 1)
                    if isinstance(base, int):
                        dve.wait_ge(s_adj[g % U], 16 * ((base + g) // U + 1))
                    else:
                        dve.wait_ge(s_adj[g % U], base * (16 // U) + 16 * (g // U + 1))
                    for r in range(HALVES):
                        nc.vector.tensor_scalar(ADJ[:, tile(base + g, r), :], adjst[:, g % U, r * N:(r + 1) * N][:, None], 0, None,
                                                ALU.not_equal)
                    carried(dve)
                    wait(dve, a_fill, base, g + 1)
                    wait(dve, a_lk, base, g + 1)
                    nc.vector.copy_predicated(a_em[:, g % 2], mask=adjst[:, g % U, :].rearrange("p (r n) -> p r n", r=HALVES),
                                              data=a_t[:, g % 2]).then_inc(a_sel, 1)
                    wait(dve, a_sel, base, g + 1)
                    nc.vector.tensor_reduce(out=a_mx[:, g % 2], in_=a_em[:, g % 2], op=ALU.max, axis=AX.X,
                                            negate=True).then_inc(a_max, 1)
                if live(base, off - 3, B):
                    g = off - 3
                    wait(dve, a_ptr, base, g + 1)
                    wait(dve, a_out, base, g - 1)
                    nc.vector.tensor_copy(a_pT[:, g % 2], PS[4 + g % 2][:].rearrange("p (r n) -> p r n", r=HALVES)).then_inc(a_ptc, 1)
                if live(base, off - 4, B):
                    g = off - 4
                    wait(dve, a_out, base, g + 1)
                    o = PS[6 + g % 2][:, 0:2 * (D + 1)].rearrange("p (r c) -> p r c", r=HALVES)
                    nc.vector.reciprocal(a_rc[:, g % 2], o[:, :, D]).then_inc(a_rec, 1)
                    wait(dve, a_rec, base, g + 1)
                    for r in range(HALVES):
                        t = tile(base + g, r)
                        ins = nc.vector.scalar_tensor_tensor(out=X[:, t, :], in0=o[:, r, 0:D][:, None], scalar=a_rc[:, g % 2, r:r + 1],
                                                             in1=X[:, t, :], op0=ALU.mult, op1=ALU.add)
                    ins.then_inc(a_res, 1)
                    wait(dve, a_res, base, g + 1)
                    for r in range(HALVES):
                        t = tile(base + g, r)
                        ins = nc.vector.bn_stats(ST[:, t, :].rearrange("p a s -> p (a s)"), X[:, t, :].rearrange("p a d -> p (a d)"))
                    ins.then_inc(a_stat, 1)
            rounds(dve, B, 4, 8, att_round)

            def normalise(out_, t, mean, rstd, src):
                return nc.vector.tensor_scalar(out_, src, mean[:, t], rstd[:, t], ALU.subtract, ALU.mult)

            def token_stats(t, src):
                return nc.vector.bn_stats(ST[:, t, :].rearrange("p a s -> p (a s)"), src)

            def chain(sem_, base, c, count):
                done = [0]

                def link(ins):
                    done[0] += 1
                    ins.then_inc(sem_, 1)
                    wait(dve, sem_, base, c, count, done[0])
                return link

            def router(l):
                r = R[l]
                own(dve, nc.vector.tensor_scalar(RUN[:], iota8[:], float(REGION), None, ALU.mult))
                own(dve, nc.vector.memset(XR[:, :, :, :, D:RW], 1.0))
                if l == 0:
                    own(dve, nc.vector.memset(OHR[:], 0.0))

                def chunk(base, off):
                    if live(base, off, CHUNKS):
                        wait(dve, r["tr"], base, off - 3)
                        wait(dve, r["rows"], base, off - 3)
                        for i in range(CT):
                            t = tile(base + off, i, CT)
                            ins = normalise(f_y[:, off % 4, i][:, None], t, MEAN, RSTD, X[:, t, :])
                        ins.then_inc(r["norm"], 1)
                        if l == 1:
                            wait(dve, r["norm"], base, off + 1)
                            s4 = off % 4
                            link = chain(r["s0"], base, off, 6)
                            for i in range(CT):
                                ins = nc.vector.bn_stats(V6[:, s4, i], f_y[:, s4, i])
                            link(ins)
                            m0, v0, m1, v1 = (V6[:, s4, :, i] for i in (1, 2, 4, 5))
                            va, ve, mean, tmp = V4[:, 0, s4], V4[:, 1, s4], V4[:, 3, s4], V4[:, 5, s4]
                            nc.vector.tensor_tensor(mean, m0, m1, ALU.add)
                            nc.vector.tensor_tensor(va, v0, v1, ALU.add)
                            link(nc.vector.tensor_tensor(tmp, m0, m1, ALU.subtract))
                            nc.vector.tensor_scalar(va, va, 1.0 / D, EPS, ALU.mult, ALU.add)
                            link(nc.vector.scalar_tensor_tensor(out=tmp, in0=tmp, scalar=0.25, in1=tmp, op0=ALU.mult, op1=ALU.mult))
                            link(nc.vector.tensor_tensor(ve, va, tmp, ALU.add))
                            link(nc.vector.tensor_scalar(mean, mean, 0.5, None, ALU.mult))
                            link(nc.vector.tensor_scalar(va, ve, -0.5, None, ALU.mult))
                            nc.vector.tensor_scalar(tmp, tmp, 0.0, None, ALU.mult).then_inc(r["var"], 1)
                    if live(base, off - 1, CHUNKS):
                        c = off - 1
                        wait(dve, r["hi"], base, c + 1)
                        nc.vector.tensor_tensor(xTl[:, c % 2], PS[c % 2][:], xTh[:, c % 2].bitcast(F32), ALU.subtract).then_inc(r["lo"], 1)
                        if l == 1:
                            s4 = c % 4
                            wait(dve, r["sq"], base, c + 1)
                            link = chain(r["s1"], base, c, 5)
                            va, rs, tmp = V4[:, 0, s4], V4[:, 4, s4], V4[:, 5, s4]
                            link(nc.vector.reciprocal(rs, V4[:, 2, s4]))
                            link(nc.vector.tensor_tensor(tmp, rs, rs, ALU.mult))
                            link(nc.vector.tensor_tensor(tmp, tmp, va, ALU.mult))
                            link(nc.vector.scalar_tensor_tensor(out=tmp, in0=tmp, scalar=1.5, in1=rs, op0=ALU.add, op1=ALU.mult))
                            link(nc.vector.tensor_copy(rs, tmp))
                    if live(base, off - 2, CHUNKS):
                        c = off - 2
                        wait(dve, r["log"], base, c + 1)
                        nc.vector.tensor_tensor(L8[:, c % 2], PS[2 + c % 2][:, 0:CT * E].rearrange("p (t e) -> p t e", e=E),
                                                bg[:, l][:, None, :].to_broadcast([P, CT, E]), ALU.add).then_inc(r["lg"], 1)
                        carried(dve)
                        wait(dve, r["lg"], base, c + 1)
                        for i in range(CT):
                            ins = nc.vector.max(M8[:, c % 2, i], L8[:, c % 2, i])
                        ins.then_inc(r["max"], 1)
                        carried(dve)
                        wait(dve, r["max"], base, c + 1)
                        for i in range(CT):
                            ins = nc.vector.max_index(I8[:, c % 2, i], M8[:, c % 2, i], L8[:, c % 2, i])
                        ins.then_inc(r["s2"], 1)
                        if l == 1:
                            nc.vector.tensor_tensor(D8[:, c % 4], L8[:, c % 2], M8[:, c % 2, :, 0:1].to_broadcast([P, CT, E]),
                                                    ALU.subtract).then_inc(r["ex"], 1)
                        wait(dve, r["s2"], base, c, 3, 1)
                        nc.vector.tensor_copy(IF[:, c % 2], I8[:, c % 2, :, 0:2]).then_inc(r["s2"], 1)
                        wait(dve, r["s2"], base, c, 3, 2)
                        for k in range(2):
                            ins = nc.vector.tensor_tensor(OH[:, c % 4, k * CT:(k + 1) * CT], iota8[:, None, :].to_broadcast([P, CT, E]),
                                                          IF[:, c % 2, :, k:k + 1].to_broadcast([P, CT, E]), ALU.is_equal)
                        ins.then_inc(r["s2"], 1)
                        wait(dve, r["s2"], base, c, 3, 3)
                        wait(dve, r["pre"], base, c - 1)
                        nc.vector.tensor_copy(OHR[:, c % 2, 2 * CT * E:4 * CT * E], OH[:, c % 4].rearrange("p j e -> p (j e)")).then_inc(r["ohr"], 1)
                    if live(base, off - 3, CHUNKS):
                        c = off - 3
                        wait(dve, r["pre"], base, c + 1)
                        pre = PS[4 + c % 2]
                        link = chain(r["s4"], base, c, 10 if l else 3)
                        t = T64[:, c % 2]
                        wait(dve, r["pos"], base, c)
                        link(nc.vector.tensor_tensor(t, pre[:, 0:8 * E].rearrange("p (j e) -> p j e", e=E),
                                                     RUN[:][:, None, :].to_broadcast([P, 2 * CT, E]), ALU.add))
                        link(nc.vector.tensor_tensor(t, t, OH[:, c % 4], ALU.mult))
                        link(nc.vector.tensor_reduce(out=PF[:, c % 2], in_=t, op=ALU.add, axis=AX.X))
                        nc.vector.tensor_tensor(RUN[:], pre[:, 8 * E:9 * E], RUN[:], ALU.add).then_inc(r["pos"], 1)
                        if l:
                            wait(dve, r["exd"], base, c + 1)
                            n4, d, q, w = N4[:, c % 2], D8[:, c % 4], Q8[:, c % 2], W2[:, c % 2]
                            link(nc.vector.tensor_reduce(out=n4[:, 0], in_=d, op=ALU.add, axis=AX.X))
                            link(nc.vector.reciprocal(n4[:, 1], n4[:, 0]))
                            link(nc.vector.tensor_tensor(q, d, n4[:, 1][:, :, None].to_broadcast([P, CT, E]), ALU.mult))
                            for k in range(2):
                                ins = nc.vector.tensor_tensor(t[:, k * CT:(k + 1) * CT], OH[:, c % 4, k * CT:(k + 1) * CT], q, ALU.mult)
                            link(ins)
                            link(nc.vector.tensor_reduce(out=w.rearrange("p k t -> p (k t)"), in_=t, op=ALU.add, axis=AX.X))
                            link(nc.vector.tensor_tensor(n4[:, 0], w[:, 0], w[:, 1], ALU.add))
                            link(nc.vector.reciprocal(n4[:, 1], n4[:, 0]))
                        wait2(dve, d_xs[c % 2], base, c, 16 * 2 * CT, l * XS_L)
                        wait(dve, r["posu"], base, c - 1)
                        nc.vector.tensor_copy(PU[:, c % 2], PF[:, c % 2])
                        ts = bass.ds((base + c) * CT, CT)
                        for k in range(2):
                            xr = XR[:, c % 2, k]
                            if l == 0:
                                nc.vector.tensor_copy(xr[:, :, 0:D], f_y[:, c % 4])
                            else:
                                for i in range(CT):
                                    nc.vector.tensor_scalar(xr[:, i, 0:D], f_y[:, c % 4, i], V4[:, 3, c % 4, i:i + 1],
                                                            V4[:, 4, c % 4, i:i + 1], ALU.subtract, ALU.mult)
                                nc.vector.tensor_tensor(xr[:, :, C_W], w[:, k], n4[:, 1], ALU.mult)
                            ins = nc.vector.tensor_scalar(xr[:, :, C_ID], TID[:, ts], float(k * TILES * P), None, ALU.add)
                        ins.then_inc(r["rows"], 1)
                rounds(dve, CHUNKS, 3, 8, chunk)
                dve.wait_ge(r["pos"], CHUNKS)
                nc.vector.tensor_copy(RUNU[:], RUN[:]).then_inc(s_run, 1)
                cnt, nbf, cum, gap = (t8[:, i] for i in range(4))
                own(dve, nc.vector.scalar_tensor_tensor(out=cnt, in0=iota8[:], scalar=-float(REGION), in1=RUN[:], op0=ALU.mult, op1=ALU.add))
                own(dve, nc.vector.tensor_scalar(t8i[:, 0], cnt, float(CH - 1), None, ALU.add))
                own(dve, nc.vector.tensor_scalar(t8i[:, 1], t8i[:, 0], CH.bit_length() - 1, None, ALU.logical_shift_right))
                own(dve, nc.vector.tensor_copy(nbf, t8i[:, 1]))
                own(dve, nc.vector.tensor_copy(cum, nbf))
                for e in range(1, E):
                    own(dve, nc.vector.tensor_tensor(cum[:, e:e + 1], cum[:, e - 1:e], cum[:, e:e + 1], ALU.add))
                own(dve, nc.vector.tensor_scalar(gap, nbf, -float(CH), float(REGION), ALU.mult, ALU.add))
                own(dve, nc.vector.tensor_tensor(tge, bidx[:, None, :].to_broadcast([P, E, NBLK]),
                                                 cum[:, :, None].to_broadcast([P, E, NBLK]), ALU.is_ge))
                own(dve, nc.vector.tensor_tensor(tgr, tge, gap[:, :, None].to_broadcast([P, E, NBLK]), ALU.mult))
                nc.vector.tensor_reduce(out=tb[:, 0], in_=tge.rearrange("p e b -> p b e"), op=ALU.add, axis=AX.X)
                own(dve, nc.vector.tensor_reduce(out=tb[:, 1], in_=tgr.rearrange("p e b -> p b e"), op=ALU.add, axis=AX.X))
                nc.vector.tensor_scalar(tb[:, 2], tb[:, 0], float(E - 1), None, ALU.min)
                own(dve, nc.vector.scalar_tensor_tensor(out=tb[:, 3], in0=bidx[:], scalar=float(CH), in1=tb[:, 1], op0=ALU.mult, op1=ALU.add))
                nc.vector.memset(tb[:, 4, 0:V], 1.0)
                own(dve, nc.vector.tensor_tensor(tb[:, 4, V:NBLK], tb[:, 2, V:NBLK], tb[:, 2, 0:NBLK - V], ALU.not_equal))
                for j, src in enumerate((3, 2, 4)):
                    ins = nc.vector.tensor_copy(TBU[:, j], tb[:, src])
                ins.then_inc(s_tab, 1)

            def ffn(l):
                f, nb = F[l], NBS[l]

                def block_round(i, off):
                    base = i * V
                    for n in range(nb):
                        if live(base, off - 1, NBLK):
                            b = off - 1
                            wait(dve, f["gelu"], base, b, nb, n + 1)
                            wait(dve, f["yb"], base, b, nb, n - 1)
                            nc.vector.tensor_copy(Gh[:, n % 2], f_G[:, n % 2]).then_inc(f["g"], 1)
                            wait(dve, f["g"], base, b, 2 * nb, 2 * n + 1)
                            nc.vector.tensor_tensor(Gl[:, n % 2], f_G[:, n % 2], Gh[:, n % 2].bitcast(F32), ALU.subtract).then_inc(f["g"], 1)
                        if n == 0 and live(base, off, NBLK):
                            wait(dve, f["xhi"], base, off + 1)
                            nc.vector.tensor_tensor(xTl[:, off % V], PS[6][:], xTh[:, off % V].bitcast(F32), ALU.subtract).then_inc(f["xlo"], 1)
                        if n == 1 and live(base, off - 3, NBLK):
                            b = off - 3
                            wait(dve, f["yt"], base, b + 1)
                            waits(dve, d_ys[b % V], i, b, 16 * CT, l * YS_L)
                            nc.vector.tensor_tensor(YB[:, b % V], PS[7][:].rearrange("p (t d) -> p t d", d=D),
                                                    WR[:, b % V][:, :, None].to_broadcast([P, CT, D]), ALU.mult).then_inc(f["wsc"], 1)
                        if n == 1 and live(base, off - 1, NBLK):
                            b = off - 1
                            waits(dve, d_xb[b % V], i, b, 16, 16 + l * XB_L)
                            wait(dve, f["ixu"], base, b - V + 1)
                            nc.vector.tensor_copy(IDF[:, b % V], XB[:, b % V, :, C_ID])
                            nc.vector.tensor_copy(WR[:, b % V], XB[:, b % V, :, C_W]).then_inc(f["ix"], 1)
                block_rounds(dve, 3, block_round)

                def chunk(base, off):
                    wait(dve, f["ysum"], base, off + 1)
                    ts = bass.ds((base + off) * CT, CT)
                    nc.vector.tensor_tensor(X[:, ts, :], YL[:, off % 2, 0], X[:, ts, :], ALU.add).then_inc(f["res"], 1)
                    if l == 0:
                        wait(dve, f["res"], base, off + 1)
                        for i in range(CT):
                            t = tile(base + off, i, CT)
                            ins = token_stats(t, X[:, t, :].rearrange("p a d -> p (a d)"))
                        ins.then_inc(f["st"], 1)
                rounds(dve, CHUNKS, 0, 4, chunk)

            if PHASES >= 2:
                dve.wait_ge(a_stat, 1 + B)
                finish_stats(2, MEAN, RSTD)
                router(0)
                ffn(0)

            def gru(i, k):
                if liveq(i, k) and k < 4:
                    start_pair(i, k)
                if liveq(i, k - 3):
                    u = k - 3
                    waitq(dve, C["n"], i, u, 1)
                    waitq(dve, C["h"], i, u, -1)
                    nc.vector.tensor_tensor(q_d[:, u % 2], q_h[:, u % 4], q_n[:, u % 2], ALU.subtract).then_inc(C["d"], 1)
                    waitq(dve, C["d"], i, u, 1)
                    nc.vector.tensor_tensor(q_d[:, u % 2], q_d[:, u % 2], q_z[:, u % 2], ALU.mult).then_inc(C["zd"], 1)
                if liveq(i, k):
                    T = PS[7 * (k % 2)]
                    if k // 4 == 0:
                        waitq(dve, C["hh"], i, k, 1)
                        nc.vector.tensor_tensor(q_hl[:, k % 4], T[:], q_hh[:, k % 4].bitcast(F32), ALU.subtract).then_inc(C["hl"], 1)
                        T = q_xn[:, k % 2].rearrange("p t d -> p (t d)")
                    waitq(dve, C["mh"], i, k, 1)
                    nc.vector.tensor_tensor(q_ml[:, k % 2], T[:], q_mh[:, k % 2].bitcast(F32), ALU.subtract).then_inc(C["ml"], 1)
                if liveq(i, k - 1):
                    u = k - 1
                    waitq(dve, C["ah"], i, u, 1)
                    nc.vector.tensor_tensor(q_al[:, u % 2], PS[1][:], q_ah[:, u % 2].bitcast(F32), ALU.subtract).then_inc(C["al"], 1)
                if liveq(i, k - 2):
                    u = k - 2
                    waitq(dve, C["gn"], i, u, 1)
                    waitq(dve, C["r"], i, u, 1)
                    waitq(dve, C["n"], i, u, -1)
                    nc.vector.scalar_tensor_tensor(out=q_t[:, u % 2], in0=PS[4][:], scalar=COLS[:, R_HH + 2:R_HH + 3], in1=q_r[:, u % 2],
                                                   op0=ALU.add, op1=ALU.mult).then_inc(C["t1"], 1)
                    waitq(dve, C["t1"], i, u, 1)
                    nc.vector.tensor_tensor(q_t[:, u % 2], PS[5][:], q_t[:, u % 2], ALU.add).then_inc(C["t2"], 1)
                if liveq(i, k - 3) and (k - 3) % UNITS < UNITS - 4:
                    u = k - 3
                    waitq(dve, C["hh"], i, u + 4, 1)
                    nc.vector.tensor_tensor(q_hl[:, u % 4], q_h[:, u % 4], q_hh[:, u % 4].bitcast(F32), ALU.subtract).then_inc(C["hl"], 1)
                if liveq(i, k - 4) and (k - 4) % UNITS >= UNITS - 4:
                    u = k - 4
                    waitp(dve, C["ft"], i, u, 1)
                    pair = i * 4 + (u // UNITS * 4 + u % 4)
                    ts = bass.ds(pair * CT, CT)
                    nc.vector.tensor_tensor(X[:, ts, :], PS[6][:].rearrange("p (t d) -> p t d", d=D), X[:, ts, :], ALU.add).then_inc(C["res"], 1)
                    waitp(dve, C["res"], i, u, 1)
                    for j in range(CT):
                        t = bass.ds(pair * CT + j, 1)
                        ins = token_stats(t, X[:, t, :].rearrange("p a d -> p (a d)"))
                    ins.then_inc(a_stat, 1)

            def start_pair(i, u):
                pair = i * 4 + (u // UNITS * 4 + u % 4)
                back = 1 if u % 4 >= 2 else 9
                waitq(dve, C["tr"], i, u, -back)
                waitq(dve, C["mh"], i, u, -back)
                for j in range(CT):
                    t = bass.ds(pair * CT + j, 1)
                    ins = normalise(q_xn[:, u % 2, j][:, None], t, MEAN, RSTD, X[:, t, :])
                ins.then_inc(C["xn"], 1)
                waitq(dve, C["ag"], i, u, -3)
                nc.vector.tensor_copy(q_A[:, u % 4], ADJ[:, bass.ds(pair * CT, CT), :]).then_inc(C["adj"], 1)

            if PHASES >= 3:
                dve.wait_ge(F[0]["st"], CHUNKS)
                finish_stats(3, MEAN, RSTD)
                unit_rounds(dve, 5, gru)
            if PHASES >= 4:
                dve.wait_ge(a_stat, 1 + B + B // 2)
                finish_stats(4, MEAN, RSTD)
                router(1)
                ffn(1)

        @block.tensor
        def _(pe):
            pe.wait_ge(s_ident, 2)
            pe.wait_ge(s_vec, 176)
            nc.tensor.transpose(PS[0][:, 0:R_END], ROWS[:], ident[0:R_END, 0:R_END])
            nc.tensor.transpose(PS[1][:, 0:P], gWr[:], ident[:]).then_inc(s_prep, 1)
            pe.wait_ge(s_prepv, 2)
            nc.tensor.matmul(PS[0][:, 128:130], gWr[:], COLS[:, 0:2], start=True, stop=True).then_inc(s_prep, 1)
            pe.wait_ge(s_gru, 48)
            for i in range(3):
                nc.tensor.transpose(PS[2][:, i * P:(i + 1) * P], rgw[:, i], ident[:])
                nc.tensor.transpose(PS[3][:, i * P:(i + 1) * P], rih[:, i], ident[:])
                ins = nc.tensor.transpose(PS[4][:, i * P:(i + 1) * P], rhh[:, i], ident[:])
            ins.then_inc(s_prep, 1)
            pe.wait_ge(s_prepv, 5)
            for i in range(LAYERS):
                nc.tensor.matmul(PS[5 + i][:, 0:3 * P], gwT[:, i], ihT, start=True, stop=True).then_inc(s_prep, 1)
            pe.wait_ge(s_raw1, 32)
            for n in range(E * HID1 // P):
                e, b = divmod(n, HID1 // P)
                ins = nc.tensor.matmul(PS[0][:, 256 + n:257 + n], raw1b[:, e, b * P:(b + 1) * P], COLS[:, R_B + e:R_B + e + 1], start=True, stop=True)
            ins.then_inc(s_prep, 1)
            pe.wait_ge(s_lo, 7)
            pe.wait_ge(s_wlo, 4)
            pe.wait_ge(s_bx, 2)
            pe.wait_ge(s_const, 10)

            def att_round(base, off):
                if live(base, off - 1, B):
                    g = off - 1
                    wait(pe, a_norm, base, g + 1)
                    wait(pe, a_e, base, g - 1)
                    for r in range(HALVES):
                        ins = nc.tensor.transpose(PS[g % 2][:, r * P:(r + 1) * P], a_xn[:, g % 2, r], ident[:])
                    ins.then_inc(a_tr, 1)
                if live(base, off - 3, B):
                    g = off - 3
                    wait(pe, a_exp, base, g + 1)
                    wait(pe, a_ptc, base, g - 1)
                    for j in range(HALVES):
                        for r in range(HALVES):
                            ins = nc.tensor.transpose(PS[4 + g % 2][:, j * N + r * P:j * N + (r + 1) * P],
                                                      a_p[:, g % 2, r, j * P:(j + 1) * P], ident[:])
                    ins.then_inc(a_ptr, 1)
                if live(base, off - 4, B):
                    g = off - 4
                    wait(pe, a_ptc, base, g + 1)
                    wait(pe, a_res, base, g - 1)
                    for r in range(HALVES):
                        for j in range(HALVES):
                            ins = nc.tensor.matmul(PS[6 + g % 2][:, r * (D + 1):(r + 1) * (D + 1)],
                                                   a_pT[:, g % 2, j, r * P:(r + 1) * P], a_h[:, g % 4, j],
                                                   start=(j == 0), stop=(j == HALVES - 1))
                    ins.then_inc(a_out, 1)
                if live(base, off - 1, B):
                    g = off - 1
                    wait(pe, a_trc, base, g + 1)
                    wait(pe, a_hc, base, g, 2, -2)
                    for r in range(HALVES):
                        nc.tensor.matmul(PS[2 + g % 2][:, r * (D + 1):(r + 1) * (D + 1)],
                                         a_xT[:, g % 2, r * P:(r + 1) * P], WE[:, 0:D + 1], start=True, stop=True)
                    nc.tensor.matmul(PS[g % 2][:, N:2 * N], wdst[:], a_xT[:, g % 2], start=True, stop=True).then_inc(a_prod, 1)
            rounds(pe, B, 4, 8, att_round)

            def mm3(o, lh, ll, rh, rl, start=True, stop=True):
                nc.tensor.matmul(o, lh, rh, start=start, stop=False)
                nc.tensor.matmul(o, lh, rl, start=False, stop=False)
                return nc.tensor.matmul(o, ll, rh, start=False, stop=stop)

            def router(l):
                r = R[l]

                def chunk(base, off):
                    if live(base, off - 1, CHUNKS):
                        c = off - 1
                        wait(pe, r["norm"], base, c + 1)
                        wait(pe, r["lo"], base, c - 1)
                        for i in range(CT):
                            ins = nc.tensor.transpose(PS[c % 2][:, i * P:(i + 1) * P], f_y[:, c % 4, i], ident[:])
                        ins.then_inc(r["tr"], 1)
                    if live(base, off - 2, CHUNKS):
                        c = off - 2
                        wait(pe, r["lo"], base, c + 1)
                        wait(pe, r["lg"], base, c - 1)
                        for i in range(CT):
                            ins = mm3(PS[2 + c % 2][:, i * E:(i + 1) * E], xTh[:, c % 2, i * P:(i + 1) * P],
                                      xTl[:, c % 2, i * P:(i + 1) * P], wgh[:, l * E:(l + 1) * E], wgl[:, l * E:(l + 1) * E])
                        ins.then_inc(r["log"], 1)
                    if live(base, off - 3, CHUNKS):
                        c = off - 3
                        wait(pe, r["ohr"], base, c + 1)
                        wait(pe, r["pos"], base, c - 1)
                        cols = 2 * CT
                        for j in range(cols + 1):
                            ins = nc.tensor.matmul(PS[4 + c % 2][:, 0:(cols + 1) * E], (ONER if j else TRIR)[:],
                                                   OHR[:, c % 2, (cols - j) * E:(2 * cols - j + 1) * E], start=j == 0, stop=j == cols)
                        ins.then_inc(r["pre"], 1)
                rounds(pe, CHUNKS, 3, 8, chunk)

            def ffn(l):
                f, nb = F[l], NBS[l]
                hid = nb * P

                def block_round(i, off):
                    base = i * V
                    if live(base, off - 3, NBLK):
                        b = off - 3
                        wait(pe, f["yev"], base, b + 1)
                        wait(pe, f["wsc"], base, b)
                        for j in range(CT):
                            ins = nc.tensor.transpose(PS[7][:, j * P:(j + 1) * P], f_ye[:, b % V, j * P:(j + 1) * P], ident[:])
                        ins.then_inc(f["yt"], 1)
                    for n in range(nb):
                        if live(base, off - 1, NBLK):
                            b = off - 1
                            if n == 0:
                                wait(pe, f["xlo"], base, b + 1)
                                waits(pe, d_ws[b % V], i, b, 32, 32 + l * WS_L)
                            wait(pe, f["gelu"], base, b, nb, n - 2)
                            w = WS[:, b % V]
                            mm3(PS[(b * nb + n) % 3][:], w[:, n * P:(n + 1) * P], w[:, 2 * hid + n * P:2 * hid + (n + 1) * P],
                                xTh[:, b % V], xTl[:, b % V]).then_inc(f["h"], 1)
                        if n == 0 and live(base, off, NBLK):
                            waits(pe, d_xb[off % V], i, off, 16, 16 + l * XB_L)
                            wait(pe, f["xlo"], base, off)
                            for j in range(CT):
                                ins = nc.tensor.transpose(PS[6][:, j * P:(j + 1) * P], XB[:, off % V, j, 0:D], ident[:])
                            ins.then_inc(f["tr"], 1)
                        b, m = off - 1 + (n - 2) // nb, (n - 2) % nb
                        if live(base, b, NBLK):
                            wait(pe, f["g"], base, b, 2 * nb, 2 * (m + 1))
                            if m == 0:
                                wait(pe, f["yev"], base, b - V + 1)
                            w = WS[:, b % V]
                            mm3(PS[3 + b % V][:], w[:, hid + m * P:hid + (m + 1) * P], w[:, 3 * hid + m * P:3 * hid + (m + 1) * P],
                                Gh[:, m % 2], Gl[:, m % 2], start=m == 0, stop=m == nb - 1).then_inc(f["yb"], 1)
                block_rounds(pe, 3, block_round)

            if PHASES >= 2:
                router(0)
                ffn(0)

            def gru(i, k):
                w = k % 4
                if liveq(i, k):
                    T = PS[7 * (k % 2)]
                    if k // 4 == 0:
                        waitp(pe, C["xn"], i, k, 1)
                    else:
                        waitq(pe, C["h"], i, k, -3)
                    waitq(pe, C["ml"], i, k, -1)
                    waitq(pe, C["hl"], i, k, -1)
                    for j in range(CT):
                        src = q_xn[:, k % 2, j] if k // 4 == 0 else q_h[:, w, j * P:(j + 1) * P]
                        ins = nc.tensor.transpose(T[:, j * P:(j + 1) * P], src, ident[:])
                    ins.then_inc(C["tr"], 1)
                if liveq(i, k - 1):
                    u = k - 1
                    waitq(pe, C["ml"], i, u, 1)
                    if u // 4 % 3 == 0:
                        waitp(pe, C["adj"], i, u, 1)
                    waitq(pe, C["al"], i, u)
                    for g in range(2):
                        for j in range(HALVES):
                            t = g * HALVES + j
                            for m in (q_mh, q_ml):
                                ins = nc.tensor.matmul(PS[1][:, g * N:(g + 1) * N], m[:, u % 2, t * P:(t + 1) * P], q_A[:, u % 4, t],
                                                       start=j == 0 and m is q_mh, stop=j == 1 and m is q_ml)
                    ins.then_inc(C["ag"], 1)
                if liveq(i, k - 2):
                    u = k - 2
                    lay = u // 4 % LAYERS
                    ai, hi = (q_ah[:, u % 2], q_al[:, u % 2]), (q_hh[:, u % 4], q_hl[:, u % 4])

                    def part(bank, row, rhs, start, stop):
                        return mm3(PS[bank][:], WGH[:, row * P:(row + 1) * P], WGL[:, row * P:(row + 1) * P], *rhs, start, stop)
                    waitq(pe, C["hl"], i, u, 1)
                    waitq(pe, C["r"], i, u)
                    part(2, 9, hi, True, False)
                    waitq(pe, C["al"], i, u, 1)
                    part(2, 3 * lay, ai, False, True).then_inc(C["gr"], 1)
                    waitq(pe, C["z"], i, u)
                    part(3, 10, hi, True, False)
                    part(3, 3 * lay + 1, ai, False, True).then_inc(C["gz"], 1)
                    waitq(pe, C["t2"], i, u)
                    part(4, 11, hi, True, True)
                    part(5, 3 * lay + 2, ai, True, True).then_inc(C["gn"], 1)
                if liveq(i, k - 4) and (k - 4) % UNITS >= UNITS - 4:
                    u = k - 4
                    waitq(pe, C["h"], i, u, 1)
                    waitp(pe, C["res"], i, u)
                    for j in range(CT):
                        ins = nc.tensor.transpose(PS[6][:, j * P:(j + 1) * P], q_h[:, u % 4, j * P:(j + 1) * P], ident[:])
                    ins.then_inc(C["ft"], 1)

            if PHASES >= 3:
                unit_rounds(pe, 5, gru)
            if PHASES >= 4:
                router(1)
                ffn(1)


_INS = ['x', 'adj', 'L0_gnn_W', 'L0_gnn_a_src', 'L0_gnn_a_dst', 'L0_ffn_Wg', 'L0_ffn_bg', 'L0_ffn_W1', 'L0_ffn_b1',
        'L0_ffn_W2', 'L0_ffn_b2', 'L1_gnn_weight', 'L1_gnn_w_ih', 'L1_gnn_w_hh', 'L1_gnn_b_ih', 'L1_gnn_b_hh',
        'L1_ffn_Wr', 'L1_ffn_br', 'L1_ffn_ln_g', 'L1_ffn_ln_b', 'L1_ffn_W1', 'L1_ffn_b1', 'L1_ffn_W2', 'L1_ffn_b2']


def kernel(**inputs):
    import numpy as np
    import concourse.bacc as bacc
    from concourse.bass_utils import run_bass_kernel_spmd

    nc = bacc.Bacc("TRN2", target_bir_lowering=False, num_devices=1)
    arrays, args = {}, []
    for name in _INS:
        a = np.ascontiguousarray(inputs[name])
        arrays[f"in_{name}"] = a
        args.append(nc.dram_tensor(f"in_{name}", a.shape, mybir.dt.from_np(a.dtype), kind="ExternalInput").ap())
    args.append(nc.dram_tensor("out_x", (B, N, D), F32, kind="ExternalOutput").ap())
    build(nc, *args)
    r = run_bass_kernel_spmd(nc, [arrays], core_ids=[0])
    return r.results[0]["out_x"]
```

```python
import concourse.bass as bass
from concourse import mybir
from concourse.alu_op_type import AluOpType as ALU
from contextlib import ExitStack

F32 = mybir.dt.float32
F32R = mybir.dt.float32r
BF16 = mybir.dt.bfloat16
I32 = mybir.dt.int32
U32 = mybir.dt.uint32
ACT = mybir.ActivationFunctionType
AX = mybir.AxisListType

P = 128
B, N, D = 32, 256, 128
HALVES = N // P
TILES = B * HALVES
E = 8
CH = 512
CT = CH // P
CHUNKS = TILES // CT
HID0, HID1 = 256, 512
LAYERS = 3
NEG_INF = -1e9
SLOPE = 0.2
EPS = 1e-5
U = 4

R_A, R_B1A, R_B1B, R_B2A, R_B2B, R_G, R_B, R_IH, R_HH, R_END = 0, 2, 18, 50, 58, 66, 74, 82, 85, 88

PAIRS = 2 * TILES * P
V = 3
NBLK = (PAIRS + E * (CH - 1)) // CH
assert NBLK % V == 0
REGION = TILES * P + CH
SPARE = E * REGION
ROWS_X = SPARE + (NBLK - PAIRS // CH) * CH
RW = D + 4
C_ID, C_W = D, D + 1
NOPAIR = 65536.0


def wait(eng, sem, base, off, mul=1, add=0):
    v = base * mul + (off * mul + add)
    if not isinstance(v, int) or v > 0:
        eng.wait_ge(sem, v)


def rounds(eng, n, depth, first, step, U=U):
    for k in range(first):
        step(0, k)
    with eng.Fori(first // U, n // U) as i:
        for u in range(U):
            step(i * U, u)
    for k in range(depth):
        step(n, k)


def block_rounds(eng, depth, step):
    for k in range(2 * V):
        step(0, k)
    with eng.Fori(2, NBLK // V) as i:
        for k in range(V):
            step(i, k)
    for k in range(depth):
        step(NBLK // V, k)


def waits(eng, sem, i, off, each, add=0):
    v = i * each + (off // V * each + add)
    if not isinstance(v, int) or v > 0:
        eng.wait_ge(sem, v)


def wait2(eng, sem, base, off, mul, add=0):
    v = base * (mul // 2) + (off // 2 * mul + add)
    if not isinstance(v, int) or v > 0:
        eng.wait_ge(sem, v)


def live(base, off, n):
    return not isinstance(base, int) or 0 <= base + off < n


UNITS = LAYERS * 4
QUADS = B // 2 // 4


def waitq(eng, sem, i, off, add=0):
    v = i * UNITS + (off + add)
    if not isinstance(v, int) or v > 0:
        eng.wait_ge(sem, v)


def waitp(eng, sem, i, off, add=0):
    v = i * 4 + (off // UNITS * 4 + off % 4 + add)
    if not isinstance(v, int) or v > 0:
        eng.wait_ge(sem, v)


def liveq(i, off):
    return not isinstance(i, int) or 0 <= i * UNITS + off < QUADS * UNITS


def unit_rounds(eng, depth, step):
    for k in range(UNITS):
        step(0, k)
    with eng.Fori(1, QUADS) as i:
        for k in range(UNITS):
            step(i, k)
    for k in range(depth):
        step(QUADS, k)


def build(nc, x, adj, gW, g_src, g_dst, f0_Wg, f0_bg, f0_W1, f0_b1, f0_W2, f0_b2,
          gr_w, gr_wih, gr_whh, gr_bih, gr_bhh, f1_Wr, f1_br, f1_g, f1_b, f1_W1, f1_b1, f1_W2, f1_b2, out):
    ctx = ExitStack()
    with ctx:
        def sb(name, shape, dt=F32):
            return ctx.enter_context(nc.sbuf_tensor(name, shape, dt))

        def sem(name):
            return ctx.enter_context(nc.semaphore(name))

        X = sb("X", [P, TILES, D])
        ADJ = sb("ADJ", [P, TILES, N], BF16)
        WHI = sb("WHI", [P, 8192], F32R)
        WLO = sb("WLO", [P, 8192], F32R)
        FA = sb("FA", [P, 8448])
        RA = sb("RA", [P, 5120], F32R)
        ident = sb("ident", [P, P])
        ones = sb("ones", [P, P])
        iota8 = sb("iota8", [P, E])
        bidx = sb("bidx", [P, NBLK])
        zero = sb("zero", [P, 2 * CT])
        neg = sb("neg", [P, 1])
        padr = sb("padr", [P, RW])
        ST = sb("ST", [P, TILES, 6])
        MEAN = sb("MEAN", [P, TILES])
        RSTD = sb("RSTD", [P, TILES])
        RS2 = sb("RS2", [P, TILES])
        NT = sb("NT", [P, 2, TILES])
        RUN = sb("RUN", [P, E])
        RUNU = sb("RUNU", [P, E], U32)
        TBU = sb("TBU", [P, 3, NBLK], U32)
        TID = sb("TID", [P, TILES])
        TRI = sb("TRI", [P, P])
        TRIR = sb("TRIR", [P, P], BF16)
        ONER = sb("ONER", [P, P], BF16)
        OHR = sb("OHR", [P, 2, (4 * CT + 1) * E], BF16)
        BX0 = sb("BX0", [P, E, HID0 // P + 1])
        BX1 = sb("BX1", [P, E, HID1 // P + 1])
        BS = sb("BS", [P, V, HID1 // P + 1])
        ROWS = sb("ROWS", [R_END, P])
        COLS = sb("COLS", [P, R_END])
        gWr = sb("gWr", [P, D])
        WE = sb("WE", [P, D + 2])
        wdst = sb("wdst", [P, P])
        wg = sb("wg", [P, 2 * E])
        wgh = sb("wgh", [P, 2 * E], F32R)
        wgl = sb("wgl", [P, 2 * E], F32R)
        bg = sb("bg", [P, 2, E])
        brz = sb("brz", [P, 2])
        WGH = sb("WGH", [P, 12 * P], F32R)
        WGL = sb("WGL", [P, 12 * P], F32R)

        PS = [ctx.enter_context(nc.psum_tensor(f"PS{i}", [P, 512], F32)) for i in range(8)]

        x_t = x.rearrange("g (r p) d -> p (g r) d", p=P)
        out_t = out.rearrange("g (r p) d -> p (g r) d", p=P)
        adj_t = adj.rearrange("g (r p) n -> g p r n", p=P)

        def fa(off, *shape):
            n = 1
            for s in shape:
                n *= s
            v = FA[:, off:off + n]
            if len(shape) == 2:
                v = v.rearrange("p (a b) -> p a b", a=shape[0])
            elif len(shape) == 3:
                v = v.rearrange("p (a b c) -> p a b c", a=shape[0], b=shape[1])
            return v

        rgw = fa(4096, 3, P)
        rih = fa(4480, 3, P)
        rhh = fa(4864, 3, P)
        gwT = fa(5248, 3, P)
        ihT = fa(5632, 3 * P)

        a_xn = fa(0, 2, HALVES, D)
        a_xT = fa(512, 2, N)
        a_h = fa(1024, 4, HALVES, D + 1)
        a_ss = fa(2056, 4, HALVES)
        a_t = fa(2080, 2, HALVES, N)
        a_em = fa(3104, 2, HALVES, N)
        a_p = fa(4128, 2, HALVES, N)
        a_pT = fa(5152, 2, HALVES, N)
        a_mx = fa(6176, 2, HALVES)
        a_rc = fa(6184, 2, HALVES)
        adjst = fa(6208, U, HALVES * N).bitcast(I32)

        f_y = fa(0, 4, CT, D)
        XR = fa(2048, 4, CT, RW).rearrange("p (s k) t w -> p s k t w", k=2)
        L8 = fa(4880, 2, CT, E)
        M8 = fa(4944, 2, CT, 8)
        I8 = fa(5008, 2, CT, 8).bitcast(U32)
        IF = fa(5072, 2, CT, 2)
        OH = fa(5088, 4, 2 * CT, E)
        D8 = fa(5344, 4, CT, E)
        Q8 = fa(5472, 2, CT, E)
        T64 = fa(5536, 2, 2 * CT, E)
        N4 = fa(5664, 2, 2, CT)
        PF = fa(5680, 2, 2 * CT)
        POSU = fa(5696, 2, 2 * CT).bitcast(U32)
        PU = fa(6768, 2, 2 * CT).bitcast(U32)
        W2 = fa(5712, 2, 2, CT)
        tb = fa(5728, 8, NBLK)
        t8 = fa(6048, 8, E)
        t8i = fa(6112, 2, E).bitcast(I32)
        tge = fa(6128, E, NBLK)
        tgr = fa(6448, E, NBLK)
        XB = fa(0, V, CT, RW)
        f_G = fa(1584, 2, CH)
        f_ye = fa(2608, V, CH)
        YB = fa(4144, V, CT, D)
        IDF = fa(5680, V, CT).bitcast(U32)
        IDX = fa(5692, V, CT).bitcast(U32)
        WR = fa(5704, V, CT)
        YL = fa(0, 2 * U, CT, D).rearrange("p (s k) t d -> p s k t d", k=2)
        xTh = RA[:, 0:1536].rearrange("p (a b) -> p a b", a=V)
        xTl = RA[:, 1536:3072].rearrange("p (a b) -> p a b", a=V)
        Gh = RA[:, 3072:4096].rearrange("p (a b) -> p a b", a=2)
        Gl = RA[:, 4096:5120].rearrange("p (a b) -> p a b", a=2)
        WS = WHI[:, 0:4 * HID1 * V].rearrange("p (a b) -> p a b", a=V)

        XS = nc.dram_tensor("XS", [ROWS_X, RW], F32, kind="Internal").ap()
        YD = nc.dram_tensor("YD", [PAIRS, D], F32, kind="Internal").ap()
        WD = [nc.dram_tensor(f"WD{l}", [E, P, 4 * h], F32, kind="Internal").ap() for l, h in enumerate((HID0, HID1))]
        BD = [nc.dram_tensor(f"BD{l}", [E, P, h // P + 1], F32, kind="Internal").ap() for l, h in enumerate((HID0, HID1))]

        q_hh = WHI[:, 0:2048].rearrange("p (a b) -> p a b", a=4)
        q_A = WHI[:, 2048:6144].rearrange("p (a t n) -> p a t n", a=4, t=CT)
        q_mh = WHI[:, 6144:7168].rearrange("p (a b) -> p a b", a=2)
        q_ah = WHI[:, 7168:8192].rearrange("p (a b) -> p a b", a=2)
        q_hl = WLO[:, 0:2048].rearrange("p (a b) -> p a b", a=4)
        q_ml = WLO[:, 6144:7168].rearrange("p (a b) -> p a b", a=2)
        q_al = WLO[:, 7168:8192].rearrange("p (a b) -> p a b", a=2)
        q_h = fa(0, 4, CH)
        q_xn = fa(2048, 2, CT, D)
        q_r = fa(3072, 2, CH)
        q_z = fa(4096, 2, CH)
        q_t = fa(5120, 2, CH)
        q_n = fa(6144, 2, CH)
        q_d = fa(7168, 2, CH)
        rawb = ADJ[:].rearrange("p a b -> p (a b)").bitcast(F32)
        PIECE = E * HID0
        PIECES = [(4096, f1_W1[0:4].rearrange("e d h -> d e h"), 4), (6144, f1_W1[4:8].rearrange("e d h -> d e h"), 4),
                  (0, f0_W1.rearrange("e d h -> d e h"), 8), (2048, f0_W2.rearrange("e (b p) d -> p (e b) d", p=P), 16),
                  (4096, f1_W2[0:4].rearrange("e (b p) d -> p (e b) d", p=P), 16),
                  (6144, f1_W2[4:8].rearrange("e (b p) d -> p (e b) d", p=P), 16)]

        def raw(j):
            o = (3 - j % 3) * PIECE
            return rawb[:, o:o + PIECE]

        s_x = [sem(f"s_x{i}") for i in range(4)]
        s_vec, s_wg, s_gru = (sem(n) for n in ("s_vec", "s_wg", "s_gru"))
        s_raw = [sem(f"s_raw{i}") for i in range(3)]
        s_const = sem("s_const")
        s_ident = sem("s_ident")
        s_prep = sem("s_prep")
        s_prepv = sem("s_prepv")
        s_hi, s_lo, s_whi, s_wlo = (sem(n) for n in ("s_hi", "s_lo", "s_whi", "s_wlo"))
        s_dve = sem("s_dve")
        s_var, s_sqrt = sem("s_var"), sem("s_sqrt")
        s_adj = [sem(f"s_adj{i}") for i in range(U)]
        (a_norm, a_tr, a_trc, a_prod, a_hc, a_e, a_fill, a_lk, a_sel, a_max, a_exp, a_ptr, a_ptc, a_out, a_rec,
         a_res, a_stat) = (sem("a_" + n) for n in (
            "norm", "tr", "trc", "prod", "hc", "e", "fill", "lk", "sel", "max", "exp", "ptr", "ptc", "out", "rec",
            "res", "stat"))
        C = {n: sem(f"c_{n}") for n in ("xn", "adj", "tr", "hh", "hl", "mh", "ml", "ag", "ah", "al", "gr", "gz", "gn",
                                        "r", "z", "t1", "t2", "n", "d", "zd", "h", "ft", "res")}
        s_out = sem("s_out")
        R = [{n: sem(f"r{l}_{n}") for n in ("norm", "tr", "hi", "lo", "log", "lg", "max", "s2", "ohr", "pre", "pos", "x0", "x1", "rows", "s4",
                                            "posu") + ("ex", "exd") * l} for l in range(2)]
        F = [{n: sem(f"f{l}_{n}") for n in ("tr", "xhi", "xlo", "h", "gelu", "g", "yb", "yev", "yt", "wsc", "ix", "ixu", "ysum",
                                            "res") + ("st",) * (1 - l)} for l in range(2)]
        d_xs, d_xb, d_ws, d_ys, d_yl = ([sem(f"d_{n}{i}") for i in range(k)] for n, k in (("xs", 2), ("xb", V), ("ws", V), ("ys", V), ("yl", U)))
        XS_L, XB_L, WS_L, YS_L, YL_L = (16 * 2 * CT * CHUNKS // 2, 16 * NBLK // V, 32 * NBLK // V, 16 * CT * NBLK // V,
                                        32 * CHUNKS // U)
        s_run, s_pad = sem("s_run"), sem("s_pad")
        s_bias = sem("s_bias")
        s_wd = [sem(f"s_wd{i}") for i in range(3)]
        s_init, s_padc, s_tab, s_bx = (sem(n) for n in ("s_init", "s_padc", "s_tab", "s_bx"))
        INIT = 16 * ((ROWS_X - SPARE) // CH)
        NBS = (HID0 // P, HID1 // P)
        BX = (BX0, BX1)

        tick = [0]

        def own(dve, ins):
            tick[0] += 1
            ins.then_inc(s_dve, 1)
            dve.wait_ge(s_dve, tick[0])

        def carried(eng):
            eng.wait_ge(*((s_x[0], 16) if eng is nc.gpsimd else (s_ident, 2)))

        def tile(g, r, h=HALVES):
            return bass.ds(g * h + r, 1)

        def pool_fills(base, off):
            return not (isinstance(base, int) and base == 0 and off < 12)

        block = ctx.enter_context(nc.Block())

        @block.sync
        def _(sp):
            for i in range(4):
                sl = slice(i * TILES // 4, (i + 1) * TILES // 4)
                sp.dma_start(X[:, sl, :], x_t[:, sl, :]).then_inc(s_x[i], 16)
                if i == 0:
                    sp.dma_start(gWr[:], gW).then_inc(s_vec, 16)
                    rows = [(R_A, g_src.rearrange("(a d) -> a d", a=1)), (R_A + 1, g_dst.rearrange("(a d) -> a d", a=1)),
                            (R_B1A, f0_b1.rearrange("e (b p) -> (e b) p", p=P)), (R_B1B, f1_b1.rearrange("e (b p) -> (e b) p", p=P)),
                            (R_B2A, f0_b2), (R_B2B, f1_b2), (R_G, f1_g), (R_B, f1_b),
                            (R_IH, gr_bih.rearrange("(a p) -> a p", p=P)), (R_HH, gr_bhh.rearrange("(a p) -> a p", p=P))]
                    for r, src in rows:
                        sp.dma_start(ROWS[r:r + src.shape[0], :], src).then_inc(s_vec, 16)
            def adj_round(base, off):
                wait(sp, a_sel, base, off - U + 1)
                sp.dma_start(adjst[:, off % U, :].rearrange("p (r n) -> p r n", r=HALVES)[:, None],
                             adj_t[bass.ds(base + off, 1)].rearrange("g p r n -> p g r n")).then_inc(s_adj[off % U], 16)
            rounds(sp, B, 0, U, adj_round)
            sp.wait_ge(s_padc, 2)
            for i in range((ROWS_X - SPARE) // CH):
                sp.dma_start(XS[SPARE + i * CH:SPARE + (i + 1) * CH, :].rearrange("(p i) w -> p i w", i=CT),
                             padr[:][:, None, :].to_broadcast([P, CT, RW])).then_inc(s_init, 16)
            for l in range(2):
                sp.wait_ge(s_bx, l + 1)
                sp.dma_start(BD[l].rearrange("e p c -> p e c"), BX[l][:]).then_inc(s_init, 16)

            def pads(l):
                sp.wait_ge(s_run, l + 1)
                for e in range(E):
                    end = sp.value_load(RUNU[0:1, e:e + 1], min_val=0, max_val=SPARE - CH)
                    sp.dma_start(XS[bass.ds(end, CH), :].rearrange("(p i) w -> p i w", i=CT), padr[:][:, None, :].to_broadcast([P, CT, RW])).then_inc(s_pad, 16)
                for done in d_xs:
                    sp.wait_ge(done, (l + 1) * XS_L)
                sp.wait_ge(s_pad, 16 * E * (l + 1))
                sp.wait_ge(s_tab, l + 1)

            def ffn(l):
                f, nb = F[l], NBS[l]
                hid = nb * P

                def block_loads(i, off):
                    base, slot = i * V, off % V
                    if live(base, off, NBLK):
                        row = sp.value_load(TBU[0:1, 0, bass.ds(base + off, 1)], min_val=0, max_val=ROWS_X - CH)
                        wait(sp, f["tr"], base, off - V + 1)
                        wait(sp, f["ix"], base, off - V + 1)
                        sp.dma_start(XB[:, slot], XS[bass.ds(row, CH), :].rearrange("(p i) w -> p i w", i=CT)).then_inc(d_xb[slot], 16)
                    if live(base, off - 1, NBLK):
                        b = off - 1
                        slot = b % V
                        wait(sp, f["yb"], base, b - V + 1, nb)
                        ex = sp.value_load(TBU[0:1, 1, bass.ds(base + b, 1)], min_val=0, max_val=E - 1)
                        new = sp.value_load(TBU[0:1, 2, bass.ds(base + b, 1)], min_val=0, max_val=1)
                        sp.dma_start(WS[:, slot:slot + 1, 0:4 * hid].bitcast(F32), WD[l][bass.ds(ex, 1)].rearrange("e p h -> p e h"),
                                     cond=new).then_inc(d_ws[slot], 16)
                        wait(sp, f["yev"], base, b - V + 1)
                        sp.dma_start(BS[:, slot:slot + 1, 0:nb + 1], BD[l][bass.ds(ex, 1)].rearrange("e p h -> p e h"),
                                     cond=new).then_inc(d_ws[slot], 16)
                block_rounds(sp, 1, block_loads)
                for done in d_ys:
                    sp.wait_ge(done, (l + 1) * YS_L)

                def chunk_loads(base, off):
                    wait(sp, f["ysum"], base, off - U + 1)
                    wait(sp, f["res"], base, off - U + 1)
                    for k in range(2):
                        sp.dma_start(YL[:, off % U, k], YD[bass.ds((base + off) * CH + k * TILES * P, CH), :]
                                     .rearrange("(i p) d -> p i d", p=P)).then_inc(d_yl[off % U], 16)
                    if l == 1 and live(base, off - 2, CHUNKS):
                        store(base, off - 2)
                rounds(sp, CHUNKS, 0, 4, chunk_loads)

            def store(base, c):
                wait(sp, F[1]["res"], base, c + 1)
                ts = bass.ds((base + c) * CT, CT)
                sp.dma_start(out_t[:, ts, :], X[:, ts, :]).then_inc(s_out, 16)

            for done in s_wd:
                sp.wait_ge(done, 64)
            sp.wait_ge(s_init, INIT + 32)
            pads(0)
            ffn(0)
            pads(1)
            ffn(1)
            store(CHUNKS, -2)
            store(CHUNKS, -1)
            sp.wait_ge(s_out, 16 * CHUNKS)

        @block.gpsimd
        def _(pool):
            pool.memset(ident[:], 0.0).then_inc(s_ident, 1)
            pool.memset(ones[:], 1.0).then_inc(s_const, 1)
            pool.memset(zero[:], 0.0).then_inc(s_const, 1)
            pool.memset(neg[:], NEG_INF / 2).then_inc(s_const, 1)
            pool.iota(iota8[:], pattern=[[1, E]], base=0, channel_multiplier=0, allow_small_or_imprecise_dtypes=True).then_inc(s_const, 1)
            pool.iota(bidx[:], pattern=[[1, NBLK]], base=0, channel_multiplier=0, allow_small_or_imprecise_dtypes=True).then_inc(s_const, 1)
            pool.iota(TID[:], pattern=[[P, TILES]], base=0, channel_multiplier=1, allow_small_or_imprecise_dtypes=True).then_inc(s_const, 1)
            pool.wait_ge(s_ident, 1)
            pool.affine_select(out=ident[:], in_=ident[:], compare_op=ALU.not_equal, fill=1.0, base=0,
                               pattern=[[-1, P]], channel_multiplier=1).then_inc(s_ident, 1)
            pool.wait_ge(s_const, 2)
            pool.affine_select(out=TRI[:], in_=ones[:], compare_op=ALU.is_gt, fill=0.0, base=0,
                               pattern=[[1, P]], channel_multiplier=-1).then_inc(s_const, 1)
            for i in range(4):
                pool.memset(a_h[:, i, :, D:D + 1], 1.0).then_inc(s_const, 1)

            for j, (c0, _, _) in enumerate(PIECES):
                if j >= 2:
                    pool.wait_ge(s_whi, j + 1)
                    pool.tensor_tensor(WLO[:, c0:c0 + PIECE], raw(j), WHI[:, c0:c0 + PIECE].bitcast(F32), ALU.subtract).then_inc(s_wlo, 1)
                pool.wait_ge(s_wlo, j + 1)
                l, hid, e0, n, which = ((1, HID1, 4 * (j % 2), 4, j // 4), (0, HID0, 0, 8, j - 2))[j in (2, 3)]
                for half, src in ((0, WHI), (1, WLO)):
                    o = (2 * half + which) * hid
                    pool.dma_start(WD[l][e0:e0 + n].rearrange("e p h -> p e h")[:, :, o:o + hid],
                                   src[:, c0:c0 + PIECE].bitcast(F32).rearrange("p (e h) -> p e h", e=n)).then_inc(s_wd[j // 2], 16)

            def att_round(base, off):
                if pool_fills(base, off) and live(base, off - 2, B):
                    g = off - 2
                    wait(pool, a_exp, base, g - 1)
                    half = neg[:][:, None, :].to_broadcast([P, HALVES, N])
                    pool.tensor_tensor(a_em[:, g % 2], half, half, ALU.add).then_inc(a_fill, 1)
            rounds(pool, B, 2, 12, att_round)

            def router(l):
                r = R[l]

                def chunk(base, off):
                    if live(base, off - 3, CHUNKS):
                        c = off - 3
                        wait(pool, r["rows"], base, c + 1)
                        nc.gpsimd.tensor_tensor(POSU[:, c % 2], PU[:, c % 2], zero[:].bitcast(U32), ALU.add).then_inc(r["posu"], 1)
                        carried(pool)
                        wait(pool, r["posu"], base, c + 1)
                        for j in range(2 * CT):
                            if j == CT:
                                carried(pool)
                                wait(pool, r["x1"], base, c + 1)
                            pool.indirect_dma_start(XS, bass.IndirectOffsetOnAxis(ap=POSU[:, c % 2, j:j + 1], axis=0),
                                                    XR[:, c % 2, j // CT, j % CT], None).then_inc(d_xs[c % 2], 16)
                rounds(pool, CHUNKS, 3, 8, chunk)

            def ffn(l):
                f = F[l]

                def block_round(i, off):
                    base = i * V
                    if live(base, off - 3, NBLK):
                        b = off - 3
                        waits(pool, d_ys[b % V], i, b, 16 * CT, l * YS_L)
                        wait(pool, f["wsc"], base, b + 1)
                        nc.gpsimd.tensor_tensor(IDX[:, b % V], IDF[:, b % V], zero[:, 0:CT].bitcast(U32), ALU.add).then_inc(f["ixu"], 1)
                        carried(pool)
                        wait(pool, f["ixu"], base, b + 1)
                        for j in range(CT):
                            pool.indirect_dma_start(YD, bass.IndirectOffsetOnAxis(ap=IDX[:, b % V, j:j + 1], axis=0),
                                                    YB[:, b % V, j], None, bounds_check=PAIRS - 1,
                                                    oob_is_err=False).then_inc(d_ys[b % V], 16)
                block_rounds(pool, 3, block_round)

                def chunk(base, off):
                    wait(pool, d_yl[off % U], base, off // U * U, 32 // U, 32 + l * YL_L)
                    pool.tensor_tensor(YL[:, off % U, 0], YL[:, off % U, 0], YL[:, off % U, 1], ALU.add).then_inc(f["ysum"], 1)
                rounds(pool, CHUNKS, 0, 4, chunk)

            router(0)
            ffn(0)

            def gru(i, k):
                if liveq(i, k - 3):
                    u = k - 3
                    waitq(pool, C["zd"], i, u, 1)
                    pool.tensor_tensor(q_h[:, u % 4], q_n[:, u % 2], q_d[:, u % 2], ALU.add).then_inc(C["h"], 1)
                for u in ((0, 1), (2,), (3,))[k] if k < 3 and liveq(i, k) else ():
                    waitq(pool, C["ag"], i, u, -3)
                    a = ADJ[:, bass.ds((i * 4 + u) * CT, CT), :]
                    pool.tensor_tensor(q_A[:, u % 4], a, a, ALU.mult).then_inc(C["adj"], 1)
            unit_rounds(pool, 5, gru)
            router(1)
            ffn(1)

        @block.scalar
        def _(act):
            act.dma_start(wg[:, 0:E], f0_Wg).then_inc(s_wg, 16)
            act.dma_start(wg[:, E:], f1_Wr).then_inc(s_wg, 16)
            act.dma_start(bg[:, 0], f0_bg.rearrange("(a e) -> a e", a=1).to_broadcast([P, E])).then_inc(s_wg, 16)
            act.dma_start(bg[:, 1], f1_br.rearrange("(a e) -> a e", a=1).to_broadcast([P, E])).then_inc(s_wg, 16)
            act.dma_start(rgw, gr_w.rearrange("i d e -> d i e")).then_inc(s_gru, 16)
            act.dma_start(rih, gr_wih.rearrange("(a o) k -> o a k", o=P)).then_inc(s_gru, 16)
            act.dma_start(rhh, gr_whh.rearrange("(a o) k -> o a k", o=P)).then_inc(s_gru, 16)
            act.wait_ge(s_prep, 1)
            nc.scalar.copy(COLS[:], PS[0][:, 0:R_END]).then_inc(s_prepv, 1)
            nc.scalar.copy(WE[:, 0:D], PS[1][:, 0:D]).then_inc(s_prepv, 1)
            act.wait_ge(s_prep, 2)
            nc.scalar.copy(WE[:, D:D + 2], PS[0][:, 128:130]).then_inc(s_prepv, 1)
            act.wait_ge(s_prep, 3)
            nc.scalar.copy(gwT, PS[2][:, 0:3 * P].rearrange("p (a b) -> p a b", a=3)).then_inc(s_prepv, 1)
            nc.scalar.copy(ihT, PS[3][:, 0:3 * P]).then_inc(s_prepv, 1)
            nc.scalar.copy(WGH[:, 9 * P:], PS[4][:, 0:3 * P]).then_inc(s_hi, 1)
            for i in range(LAYERS):
                act.wait_ge(s_prep, 4 + i)
                nc.scalar.copy(WGH[:, 3 * i * P:3 * (i + 1) * P], PS[5 + i][:, 0:3 * P]).then_inc(s_hi, 1)
            act.wait_ge(s_wg, 64)
            nc.scalar.copy(wgh[:], wg[:]).then_inc(s_hi, 1)
            def load_piece(j):
                _, w, n = PIECES[j]
                act.dma_start(raw(j).rearrange("p (a b) -> p a b", a=n), w).then_inc(s_raw[j % 3], 16)
            act.wait_ge(s_x[3], 16)
            for j in range(3):
                load_piece(j)

            HI_ROUNDS = (2, 3, 4, 6, 7, 8)

            def hi_piece(j):
                c0 = PIECES[j][0]
                act.wait_ge(s_raw[j % 3], 16 * (j // 3 + 1))
                if j < 2:
                    for e in range(4):
                        ins = nc.scalar.activation(WHI[:, c0 + e * HID1:c0 + (e + 1) * HID1], raw(j)[:, e * HID1:(e + 1) * HID1],
                                                   ACT.Copy, scale=COLS[:, R_G + 4 * j + e:R_G + 4 * j + e + 1])
                    ins.then_inc(s_whi, 1)
                else:
                    if j >= 4:
                        act.wait_ge(s_wd[0], 64)
                    nc.scalar.copy(WHI[:, c0:c0 + PIECE], raw(j)).then_inc(s_whi, 1)

            act.wait_ge(s_var, 1)
            nc.scalar.activation(NT[:, 1], NT[:, 1], ACT.Sqrt).then_inc(s_sqrt, 1)

            def att_round(base, off):
                if isinstance(base, int) and base == 0:
                    if off in HI_ROUNDS:
                        hi_piece(HI_ROUNDS.index(off))
                    if 4 <= off < 7:
                        act.wait_ge(s_wlo, off - 3)
                        act.wait_ge(s_bias, min(off - 3, 2))
                        load_piece(off - 1)
                if live(base, off - 1, B):
                    g = off - 1
                    wait(act, a_tr, base, g + 1)
                    wait(act, a_prod, base, g - 1)
                    nc.scalar.copy(a_xT[:, g % 2], PS[g % 2][:, 0:N]).then_inc(a_trc, 1)
                if live(base, off - 2, B):
                    g = off - 2
                    wait(act, a_max, base, g + 1)
                    wait(act, a_ptr, base, g - 1)
                    for r in range(HALVES):
                        ins = nc.scalar.activation(a_p[:, g % 2, r], a_em[:, g % 2, r], ACT.Exp,
                                                   bias=a_mx[:, g % 2, r:r + 1])
                    ins.then_inc(a_exp, 1)
                if live(base, off - 1, B):
                    g = off - 1
                    wait(act, a_prod, base, g + 1)
                    wait(act, a_out, base, g - 3)
                    src = PS[2 + g % 2][:, 0:2 * (D + 1)].rearrange("p (r c) -> p r c", r=HALVES)
                    nc.scalar.copy(a_h[:, g % 4, :, 0:D], src[:, :, 0:D]).then_inc(a_hc, 1)
                    nc.scalar.copy(a_ss[:, g % 4], src[:, :, D]).then_inc(a_hc, 1)
                    wait(act, a_hc, base, g, 2, 2)
                    wait(act, a_sel, base, g - 1)
                    for r in range(HALVES):
                        ins = nc.scalar.activation(a_t[:, g % 2, r], PS[g % 2][:, N:2 * N], ACT.Identity,
                                                   bias=a_ss[:, g % 4, r:r + 1])
                    ins.then_inc(a_e, 1)
            rounds(act, B, 4, 12, att_round)

            def router(l):
                r = R[l]

                def chunk(base, off):
                    if live(base, off - 1, CHUNKS):
                        c = off - 1
                        wait(act, r["tr"], base, c + 1)
                        wait(act, r["log"], base, c - 1)
                        nc.scalar.copy(xTh[:, c % 2], PS[c % 2][:]).then_inc(r["hi"], 1)
                    if live(base, off - 3, CHUNKS):
                        c = off - 3
                        wait(act, r["x0"], base, c + 1)
                        nc.scalar.copy(XR[:, c % 2, 1, :, 0:D], XR[:, c % 2, 0, :, 0:D]).then_inc(r["x1"], 1)
                    if l == 1 and live(base, off - 2, CHUNKS):
                        c = off - 2
                        wait(act, r["ex"], base, c + 1)
                        nc.scalar.activation(D8[:, c % 4], D8[:, c % 4], ACT.Exp).then_inc(r["exd"], 1)
                rounds(act, CHUNKS, 3, 8, chunk)

            def ffn(l):
                f, nb = F[l], NBS[l]

                def block_round(i, off):
                    base = i * V
                    for n in range(nb):
                        if n == 0 and live(base, off, NBLK):
                            wait(act, f["tr"], base, off + 1)
                            wait(act, f["h"], base, off - V + 1, nb)
                            nc.scalar.copy(xTh[:, off % V], PS[6][:]).then_inc(f["xhi"], 1)
                        if live(base, off - 1, NBLK):
                            b = off - 1
                            wait(act, f["h"], base, b, nb, n + 1)
                            wait(act, f["g"], base, b, 2 * nb, 2 * (n - 1))
                            nc.scalar.activation(f_G[:, n % 2], PS[(b * nb + n) % 3][:], ACT.Gelu,
                                                 bias=BS[:, b % V, n:n + 1]).then_inc(f["gelu"], 1)
                        if n == 1 and live(base, off - 2, NBLK):
                            b = off - 2
                            wait(act, f["yb"], base, b, nb, nb)
                            wait(act, f["yt"], base, b - V + 1)
                            nc.scalar.activation(f_ye[:, b % V], PS[3 + b % V][:], ACT.Identity,
                                                 bias=BS[:, b % V, nb:nb + 1]).then_inc(f["yev"], 1)
                block_rounds(act, 3, block_round)

            act.wait_ge(s_var, 2)
            nc.scalar.activation(NT[:, 1], NT[:, 1], ACT.Sqrt).then_inc(s_sqrt, 1)
            router(0)
            ffn(0)

            def gru(i, k):
                l, w = k // 4, k % 4
                if liveq(i, k - 3):
                    u = k - 3
                    waitq(act, C["t2"], i, u, 1)
                    waitq(act, C["h"], i, u, -1)
                    nc.scalar.activation(q_n[:, u % 2], q_t[:, u % 2], ACT.Tanh, bias=COLS[:, R_IH + 2:R_IH + 3]).then_inc(C["n"], 1)
                if liveq(i, k):
                    T = PS[7 * (k % 2)]
                    if l == 0:
                        waitq(act, C["tr"], i, k, 1)
                        waitp(act, C["ft"], i, k, -3)
                        nc.scalar.copy(q_h[:, w], T[:])
                        waitq(act, C["gn"], i, k, -3)
                        nc.scalar.copy(q_hh[:, w], T[:]).then_inc(C["hh"], 1)
                        waitq(act, C["ag"], i, k, -1)
                        nc.scalar.copy(q_mh[:, k % 2], q_xn[:, k % 2].rearrange("p t d -> p (t d)")).then_inc(C["mh"], 1)
                    else:
                        waitq(act, C["tr"], i, k, 1)
                        waitq(act, C["ag"], i, k, -1)
                        nc.scalar.copy(q_mh[:, k % 2], T[:]).then_inc(C["mh"], 1)
                if liveq(i, k - 1):
                    u = k - 1
                    waitq(act, C["ag"], i, u, 1)
                    waitq(act, C["gn"], i, u, -1)
                    nc.scalar.copy(q_ah[:, u % 2], PS[1][:]).then_inc(C["ah"], 1)
                if liveq(i, k - 2):
                    u = k - 2
                    waitq(act, C["gr"], i, u, 1)
                    waitq(act, C["t1"], i, u, -1)
                    nc.scalar.activation(q_r[:, u % 2], PS[2][:], ACT.Sigmoid, bias=brz[:, 0:1]).then_inc(C["r"], 1)
                    waitq(act, C["gz"], i, u, 1)
                    waitq(act, C["zd"], i, u, -1)
                    nc.scalar.activation(q_z[:, u % 2], PS[3][:], ACT.Sigmoid, bias=brz[:, 1:2]).then_inc(C["z"], 1)
                if liveq(i, k - 3) and (k - 3) % UNITS < UNITS - 4:
                    u = k - 3
                    waitq(act, C["h"], i, u, 1)
                    waitq(act, C["gn"], i, u, 1)
                    nc.scalar.copy(q_hh[:, u % 4], q_h[:, u % 4]).then_inc(C["hh"], 1)

            act.wait_ge(s_var, 3)
            nc.scalar.activation(NT[:, 1], NT[:, 1], ACT.Sqrt).then_inc(s_sqrt, 1)
            unit_rounds(act, 5, gru)
            for k in (4, 5):
                act.wait_ge(s_var, k)
                nc.scalar.activation(NT[:, 1], NT[:, 1], ACT.Sqrt).then_inc(s_sqrt, 1)
            router(1)
            ffn(1)

        @block.vector
        def _(dve):
            nc.vector.memset(padr[:], 0.0).then_inc(s_padc, 1)
            dve.wait_ge(s_padc, 1)
            nc.vector.memset(padr[:, C_ID:C_ID + 1], NOPAIR).then_inc(s_padc, 1)
            for t in range(TILES):
                if t % 16 == 0:
                    dve.wait_ge(s_x[t // 16], 16)
                ins = nc.vector.bn_stats(ST[:, t], X[:, t])
            ins.then_inc(a_stat, 1)
            dve.wait_ge(s_prepv, 3)
            nc.vector.tensor_scalar(wdst[:], ones[:], WE[:, D + 1:D + 2], None, ALU.mult).then_inc(s_lo, 1)
            dve.wait_ge(s_hi, 1)
            nc.vector.tensor_tensor(WGL[:, 9 * P:], PS[4][:, 0:3 * P], WGH[:, 9 * P:].bitcast(F32), ALU.subtract).then_inc(s_lo, 1)
            for i in range(LAYERS):
                dve.wait_ge(s_hi, 2 + i)
                nc.vector.tensor_tensor(WGL[:, 3 * i * P:3 * (i + 1) * P], PS[5 + i][:, 0:3 * P],
                                        WGH[:, 3 * i * P:3 * (i + 1) * P].bitcast(F32), ALU.subtract).then_inc(s_lo, 1)
            nc.vector.tensor_tensor(brz[:], COLS[:, R_IH:R_IH + 2], COLS[:, R_HH:R_HH + 2], ALU.add).then_inc(s_lo, 1)
            dve.wait_ge(s_hi, 2 + LAYERS)
            nc.vector.tensor_tensor(wgl[:], wg[:], wgh[:].bitcast(F32), ALU.subtract).then_inc(s_lo, 1)

            def finish_stats(k, mean, rstd):
                m0, v0, m1, v1 = (ST[:, :, i] for i in (1, 2, 4, 5))
                own(dve, nc.vector.tensor_tensor(NT[:, 1], m0, m1, ALU.subtract))
                own(dve, nc.vector.scalar_tensor_tensor(out=NT[:, 1], in0=NT[:, 1], scalar=0.25, in1=NT[:, 1], op0=ALU.mult, op1=ALU.mult))
                own(dve, nc.vector.tensor_tensor(NT[:, 0], v0, v1, ALU.add))
                own(dve, nc.vector.scalar_tensor_tensor(out=NT[:, 0], in0=NT[:, 0], scalar=1.0 / D, in1=NT[:, 1], op0=ALU.mult, op1=ALU.add))
                own(dve, nc.vector.tensor_tensor(mean[:], m0, m1, ALU.add))
                own(dve, nc.vector.tensor_scalar(mean[:], mean[:], 0.5, None, ALU.mult))
                own(dve, nc.vector.tensor_copy(RS2[:], NT[:, 0]))
                own(dve, nc.vector.tensor_scalar(NT[:, 0], NT[:, 0], EPS, None, ALU.add))
                inverse_root(k, rstd)

            def inverse_root(k, out_):
                nc.vector.tensor_scalar(NT[:, 1], NT[:, 0], 1.0, None, ALU.mult).then_inc(s_var, 1)
                dve.wait_ge(s_sqrt, k)
                own(dve, nc.vector.reciprocal(out_[:], NT[:, 1]))
                own(dve, nc.vector.tensor_tensor(NT[:, 1], out_[:], out_[:], ALU.mult))
                own(dve, nc.vector.tensor_tensor(NT[:, 1], NT[:, 1], NT[:, 0], ALU.mult))
                own(dve, nc.vector.tensor_scalar(NT[:, 1], NT[:, 1], -0.5, 1.5, ALU.mult, ALU.add))
                own(dve, nc.vector.tensor_tensor(out_[:], out_[:], NT[:, 1], ALU.mult))

            nc.vector.tensor_copy(BX0[:, :, 0:2], COLS[:, R_B1A:R_B1A + 16].rearrange("p (e b) -> p e b", e=E))
            nc.vector.tensor_copy(BX0[:, :, 2], COLS[:, R_B2A:R_B2A + E]).then_inc(s_bx, 1)
            dve.wait_ge(s_const, 7)
            nc.vector.tensor_copy(TRIR[:], TRI[:])
            nc.vector.tensor_copy(ONER[:], ones[:]).then_inc(s_lo, 1)
            dve.wait_ge(a_stat, 1)
            finish_stats(1, MEAN, RSTD)

            def att_round(base, off):
                if live(base, off, B):
                    g = off
                    wait(dve, a_tr, base, g - 1)
                    for r in range(HALVES):
                        t = tile(base + g, r)
                        ins = nc.vector.tensor_scalar(a_xn[:, g % 2, r][:, None], X[:, t, :], MEAN[:, t], RSTD[:, t],
                                                      ALU.subtract, ALU.mult)
                    ins.then_inc(a_norm, 1)
                if isinstance(base, int) and base == 0 and off == 10:
                    dve.wait_ge(s_wlo, len(PIECES))
                if live(base, off - 2, B):
                    g = off - 2
                    if not pool_fills(base, off):
                        wait(dve, a_exp, base, g - 1)
                        nc.vector.memset(a_em[:, g % 2], NEG_INF).then_inc(a_fill, 1)
                    wait(dve, a_e, base, g + 1)
                    nc.vector.scalar_tensor_tensor(out=a_t[:, g % 2], in0=a_t[:, g % 2], scalar=SLOPE, in1=a_t[:, g % 2],
                                                   op0=ALU.mult, op1=ALU.max).then_inc(a_lk, 1)
                    if isinstance(base, int):
                        dve.wait_ge(s_adj[g % U], 16 * ((base + g) // U + 1))
                    else:
                        dve.wait_ge(s_adj[g % U], base * (16 // U) + 16 * (g // U + 1))
                    nc.vector.tensor_scalar(ADJ[:, bass.ds((base + g) * HALVES, HALVES), :],
                                            adjst[:, g % U, :].rearrange("p (r n) -> p r n", r=HALVES), 0, None, ALU.not_equal)
                    carried(dve)
                    wait(dve, a_fill, base, g + 1)
                    wait(dve, a_lk, base, g + 1)
                    nc.vector.copy_predicated(a_em[:, g % 2], mask=adjst[:, g % U, :].rearrange("p (r n) -> p r n", r=HALVES),
                                              data=a_t[:, g % 2]).then_inc(a_sel, 1)
                    wait(dve, a_sel, base, g + 1)
                    nc.vector.tensor_reduce(out=a_mx[:, g % 2], in_=a_em[:, g % 2], op=ALU.max, axis=AX.X,
                                            negate=True).then_inc(a_max, 1)
                if live(base, off - 3, B):
                    g = off - 3
                    wait(dve, a_ptr, base, g + 1)
                    wait(dve, a_out, base, g - 1)
                    nc.vector.tensor_copy(a_pT[:, g % 2], PS[4 + g % 2][:].rearrange("p (r n) -> p r n", r=HALVES)).then_inc(a_ptc, 1)
                if isinstance(base, int) and base == 0 and 3 <= off < 5:
                    j = off - 3
                    dve.wait_ge(s_whi, j + 1)
                    for e in range(4):
                        c = PIECES[j][0] + e * HID1
                        ins = nc.vector.scalar_tensor_tensor(out=WLO[:, c:c + HID1], in0=raw(j)[:, e * HID1:(e + 1) * HID1],
                                                             scalar=COLS[:, R_G + 4 * j + e:R_G + 4 * j + e + 1],
                                                             in1=WHI[:, c:c + HID1].bitcast(F32), op0=ALU.mult, op1=ALU.subtract)
                    ins.then_inc(s_wlo, 1)
                if isinstance(base, int) and base == 0 and off == 4:
                    dve.wait_ge(s_bias, 2)
                    nc.vector.tensor_tensor(BX1[:, :, 0:4], PS[7][:, 0:E * HID1 // P].rearrange("p (e b) -> p e b", e=E),
                                            COLS[:, R_B1B:R_B1B + E * HID1 // P].rearrange("p (e b) -> p e b", e=E), ALU.add)
                    nc.vector.tensor_copy(BX1[:, :, 4], COLS[:, R_B2B:R_B2B + E]).then_inc(s_bx, 1)
                if live(base, off - 4, B):
                    g = off - 4
                    wait(dve, a_out, base, g + 1)
                    o = PS[6 + g % 2][:, 0:2 * (D + 1)].rearrange("p (r c) -> p r c", r=HALVES)
                    nc.vector.reciprocal(a_rc[:, g % 2], o[:, :, D]).then_inc(a_rec, 1)
                    wait(dve, a_rec, base, g + 1)
                    for r in range(HALVES):
                        t = tile(base + g, r)
                        ins = nc.vector.scalar_tensor_tensor(out=X[:, t, :], in0=o[:, r, 0:D][:, None], scalar=a_rc[:, g % 2, r:r + 1],
                                                             in1=X[:, t, :], op0=ALU.mult, op1=ALU.add)
                    ins.then_inc(a_res, 1)
                    wait(dve, a_res, base, g + 1)
                    for r in range(HALVES):
                        t = tile(base + g, r)
                        ins = nc.vector.bn_stats(ST[:, t, :].rearrange("p a s -> p (a s)"), X[:, t, :].rearrange("p a d -> p (a d)"))
                    ins.then_inc(a_stat, 1)
            rounds(dve, B, 4, 12, att_round)

            def normalise(out_, t, mean, rstd, src):
                return nc.vector.tensor_scalar(out_, src, mean[:, t], rstd[:, t], ALU.subtract, ALU.mult)

            def token_stats(t, src):
                return nc.vector.bn_stats(ST[:, t, :].rearrange("p a s -> p (a s)"), src)

            def chain(sem_, base, c, count):
                done = [0]

                def link(ins):
                    done[0] += 1
                    ins.then_inc(sem_, 1)
                    wait(dve, sem_, base, c, count, done[0])
                return link

            def router(l):
                r = R[l]
                own(dve, nc.vector.tensor_scalar(RUN[:], iota8[:], float(REGION), None, ALU.mult))
                own(dve, nc.vector.memset(XR[:, :, :, :, D:RW], 1.0))
                if l == 0:
                    own(dve, nc.vector.memset(OHR[:], 0.0))

                def chunk(base, off):
                    if live(base, off, CHUNKS):
                        wait(dve, r["tr"], base, off - 3)
                        wait(dve, r["rows"], base, off - 3)
                        for i in range(CT):
                            t = tile(base + off, i, CT)
                            ins = normalise(f_y[:, off % 4, i][:, None], t, MEAN, RSTD, X[:, t, :])
                        ins.then_inc(r["norm"], 1)
                    if live(base, off - 1, CHUNKS):
                        c = off - 1
                        wait(dve, r["hi"], base, c + 1)
                        nc.vector.tensor_tensor(xTl[:, c % 2], PS[c % 2][:], xTh[:, c % 2].bitcast(F32), ALU.subtract).then_inc(r["lo"], 1)
                    if live(base, off - 2, CHUNKS):
                        c = off - 2
                        wait(dve, r["log"], base, c + 1)
                        nc.vector.tensor_tensor(L8[:, c % 2], PS[2 + c % 2][:, 0:CT * E].rearrange("p (t e) -> p t e", e=E),
                                                bg[:, l][:, None, :].to_broadcast([P, CT, E]), ALU.add).then_inc(r["lg"], 1)
                        carried(dve)
                        wait(dve, r["lg"], base, c + 1)
                        for i in range(CT):
                            ins = nc.vector.max(M8[:, c % 2, i], L8[:, c % 2, i])
                        ins.then_inc(r["max"], 1)
                        carried(dve)
                        wait(dve, r["max"], base, c + 1)
                        for i in range(CT):
                            ins = nc.vector.max_index(I8[:, c % 2, i], M8[:, c % 2, i], L8[:, c % 2, i])
                        ins.then_inc(r["s2"], 1)
                        if l == 1:
                            nc.vector.tensor_tensor(D8[:, c % 4], L8[:, c % 2], M8[:, c % 2, :, 0:1].to_broadcast([P, CT, E]),
                                                    ALU.subtract).then_inc(r["ex"], 1)
                        wait(dve, r["s2"], base, c, 3, 1)
                        nc.vector.tensor_copy(IF[:, c % 2], I8[:, c % 2, :, 0:2]).then_inc(r["s2"], 1)
                        wait(dve, r["s2"], base, c, 3, 2)
                        for k in range(2):
                            ins = nc.vector.tensor_tensor(OH[:, c % 4, k * CT:(k + 1) * CT], iota8[:, None, :].to_broadcast([P, CT, E]),
                                                          IF[:, c % 2, :, k:k + 1].to_broadcast([P, CT, E]), ALU.is_equal)
                        ins.then_inc(r["s2"], 1)
                        wait(dve, r["s2"], base, c, 3, 3)
                        wait(dve, r["pre"], base, c - 1)
                        nc.vector.tensor_copy(OHR[:, c % 2, 2 * CT * E:4 * CT * E], OH[:, c % 4].rearrange("p j e -> p (j e)")).then_inc(r["ohr"], 1)
                    if live(base, off - 3, CHUNKS):
                        c = off - 3
                        wait(dve, r["pre"], base, c + 1)
                        pre = PS[4 + c % 2]
                        link = chain(r["s4"], base, c, 10 if l else 3)
                        t = T64[:, c % 2]
                        wait(dve, r["pos"], base, c)
                        link(nc.vector.tensor_tensor(t, pre[:, 0:8 * E].rearrange("p (j e) -> p j e", e=E),
                                                     RUN[:][:, None, :].to_broadcast([P, 2 * CT, E]), ALU.add))
                        link(nc.vector.tensor_tensor(t, t, OH[:, c % 4], ALU.mult))
                        link(nc.vector.tensor_reduce(out=PF[:, c % 2], in_=t, op=ALU.add, axis=AX.X))
                        nc.vector.tensor_tensor(RUN[:], pre[:, 8 * E:9 * E], RUN[:], ALU.add).then_inc(r["pos"], 1)
                        if l:
                            wait(dve, r["exd"], base, c + 1)
                            n4, d, q, w = N4[:, c % 2], D8[:, c % 4], Q8[:, c % 2], W2[:, c % 2]
                            link(nc.vector.tensor_reduce(out=n4[:, 0], in_=d, op=ALU.add, axis=AX.X))
                            link(nc.vector.reciprocal(n4[:, 1], n4[:, 0]))
                            link(nc.vector.tensor_tensor(q, d, n4[:, 1][:, :, None].to_broadcast([P, CT, E]), ALU.mult))
                            for k in range(2):
                                ins = nc.vector.tensor_tensor(t[:, k * CT:(k + 1) * CT], OH[:, c % 4, k * CT:(k + 1) * CT], q, ALU.mult)
                            link(ins)
                            link(nc.vector.tensor_reduce(out=w.rearrange("p k t -> p (k t)"), in_=t, op=ALU.add, axis=AX.X))
                            link(nc.vector.tensor_tensor(n4[:, 0], w[:, 0], w[:, 1], ALU.add))
                            link(nc.vector.reciprocal(n4[:, 1], n4[:, 0]))
                        wait2(dve, d_xs[c % 2], base, c, 16 * 2 * CT, l * XS_L)
                        wait(dve, r["posu"], base, c - 1)
                        nc.vector.tensor_copy(PU[:, c % 2], PF[:, c % 2])
                        ts = bass.ds((base + c) * CT, CT)
                        if l == 0:
                            ins = nc.vector.tensor_copy(XR[:, c % 2, 0, :, 0:D], f_y[:, c % 4])
                        else:
                            for j in range(CT):
                                ins = nc.vector.tensor_scalar(XR[:, c % 2, 0, j, 0:D][:, None], f_y[:, c % 4, j][:, None],
                                                              RS2[:, tile(base + c, j, CT)], None, ALU.mult)
                        ins.then_inc(r["x0"], 1)
                        for k in range(2):
                            xr = XR[:, c % 2, k]
                            if l:
                                nc.vector.tensor_tensor(xr[:, :, C_W], w[:, k], n4[:, 1], ALU.mult)
                            ins = nc.vector.tensor_scalar(xr[:, :, C_ID], TID[:, ts], float(k * TILES * P), None, ALU.add)
                        ins.then_inc(r["rows"], 1)
                rounds(dve, CHUNKS, 3, 8, chunk)
                dve.wait_ge(r["pos"], CHUNKS)
                nc.vector.tensor_copy(RUNU[:], RUN[:]).then_inc(s_run, 1)
                cnt, nbf, cum, gap = (t8[:, i] for i in range(4))
                own(dve, nc.vector.scalar_tensor_tensor(out=cnt, in0=iota8[:], scalar=-float(REGION), in1=RUN[:], op0=ALU.mult, op1=ALU.add))
                own(dve, nc.vector.tensor_scalar(t8i[:, 0], cnt, float(CH - 1), None, ALU.add))
                own(dve, nc.vector.tensor_scalar(t8i[:, 1], t8i[:, 0], CH.bit_length() - 1, None, ALU.logical_shift_right))
                own(dve, nc.vector.tensor_copy(nbf, t8i[:, 1]))
                own(dve, nc.vector.tensor_copy(cum, nbf))
                for e in range(1, E):
                    own(dve, nc.vector.tensor_tensor(cum[:, e:e + 1], cum[:, e - 1:e], cum[:, e:e + 1], ALU.add))
                own(dve, nc.vector.tensor_scalar(gap, nbf, -float(CH), float(REGION), ALU.mult, ALU.add))
                own(dve, nc.vector.tensor_tensor(tge, bidx[:, None, :].to_broadcast([P, E, NBLK]),
                                                 cum[:, :, None].to_broadcast([P, E, NBLK]), ALU.is_ge))
                own(dve, nc.vector.tensor_tensor(tgr, tge, gap[:, :, None].to_broadcast([P, E, NBLK]), ALU.mult))
                nc.vector.tensor_reduce(out=tb[:, 0], in_=tge.rearrange("p e b -> p b e"), op=ALU.add, axis=AX.X)
                own(dve, nc.vector.tensor_reduce(out=tb[:, 1], in_=tgr.rearrange("p e b -> p b e"), op=ALU.add, axis=AX.X))
                nc.vector.tensor_scalar(tb[:, 2], tb[:, 0], float(E - 1), None, ALU.min)
                own(dve, nc.vector.scalar_tensor_tensor(out=tb[:, 3], in0=bidx[:], scalar=float(CH), in1=tb[:, 1], op0=ALU.mult, op1=ALU.add))
                nc.vector.memset(tb[:, 4, 0:V], 1.0)
                own(dve, nc.vector.tensor_tensor(tb[:, 4, V:NBLK], tb[:, 2, V:NBLK], tb[:, 2, 0:NBLK - V], ALU.not_equal))
                for j, src in enumerate((3, 2, 4)):
                    ins = nc.vector.tensor_copy(TBU[:, j], tb[:, src])
                ins.then_inc(s_tab, 1)

            def ffn(l):
                f, nb = F[l], NBS[l]

                def block_round(i, off):
                    base = i * V
                    for n in range(nb):
                        if n == 0 and live(base, off, NBLK):
                            wait(dve, f["xhi"], base, off + 1)
                            nc.vector.tensor_tensor(xTl[:, off % V], PS[6][:], xTh[:, off % V].bitcast(F32), ALU.subtract).then_inc(f["xlo"], 1)
                        if live(base, off - 1, NBLK):
                            b = off - 1
                            wait(dve, f["gelu"], base, b, nb, n + 1)
                            wait(dve, f["yb"], base, b, nb, n - 1)
                            nc.vector.tensor_copy(Gh[:, n % 2], f_G[:, n % 2]).then_inc(f["g"], 1)
                            wait(dve, f["g"], base, b, 2 * nb, 2 * n + 1)
                            nc.vector.tensor_tensor(Gl[:, n % 2], f_G[:, n % 2], Gh[:, n % 2].bitcast(F32), ALU.subtract).then_inc(f["g"], 1)
                        if n == 0 and live(base, off - 1, NBLK):
                            b = off - 1
                            waits(dve, d_xb[b % V], i, b, 16, 16 + l * XB_L)
                            wait(dve, f["ixu"], base, b - V + 1)
                            nc.vector.tensor_copy(IDF[:, b % V], XB[:, b % V, :, C_ID])
                            nc.vector.tensor_copy(WR[:, b % V], XB[:, b % V, :, C_W]).then_inc(f["ix"], 1)
                        if n == 0 and live(base, off - 3, NBLK):
                            b = off - 3
                            wait(dve, f["yt"], base, b + 1)
                            waits(dve, d_ys[b % V], i, b, 16 * CT, l * YS_L)
                            nc.vector.tensor_tensor(YB[:, b % V], PS[7][:].rearrange("p (t d) -> p t d", d=D),
                                                    WR[:, b % V][:, :, None].to_broadcast([P, CT, D]), ALU.mult).then_inc(f["wsc"], 1)
                block_rounds(dve, 3, block_round)

                def chunk(base, off):
                    wait(dve, f["ysum"], base, off + 1)
                    ts = bass.ds((base + off) * CT, CT)
                    nc.vector.tensor_tensor(X[:, ts, :], YL[:, off % U, 0], X[:, ts, :], ALU.add).then_inc(f["res"], 1)
                    if l == 0:
                        wait(dve, f["res"], base, off + 1)
                        for i in range(CT):
                            t = tile(base + off, i, CT)
                            ins = token_stats(t, X[:, t, :].rearrange("p a d -> p (a d)"))
                        ins.then_inc(f["st"], 1)
                rounds(dve, CHUNKS, 0, 4, chunk)

            dve.wait_ge(a_stat, 1 + B)
            finish_stats(2, MEAN, RSTD)
            router(0)
            ffn(0)

            def gru(i, k):
                if liveq(i, k) and k == 0:
                    start_pair(i, k)
                if liveq(i, k - 3):
                    u = k - 3
                    waitq(dve, C["n"], i, u, 1)
                    waitq(dve, C["h"], i, u, -1)
                    nc.vector.tensor_tensor(q_d[:, u % 2], q_h[:, u % 4], q_n[:, u % 2], ALU.subtract).then_inc(C["d"], 1)
                    waitq(dve, C["d"], i, u, 1)
                    nc.vector.tensor_tensor(q_d[:, u % 2], q_d[:, u % 2], q_z[:, u % 2], ALU.mult).then_inc(C["zd"], 1)
                if liveq(i, k):
                    T = PS[7 * (k % 2)]
                    if k // 4 == 0:
                        waitq(dve, C["hh"], i, k, 1)
                        nc.vector.tensor_tensor(q_hl[:, k % 4], T[:], q_hh[:, k % 4].bitcast(F32), ALU.subtract).then_inc(C["hl"], 1)
                        T = q_xn[:, k % 2].rearrange("p t d -> p (t d)")
                    waitq(dve, C["mh"], i, k, 1)
                    nc.vector.tensor_tensor(q_ml[:, k % 2], T[:], q_mh[:, k % 2].bitcast(F32), ALU.subtract).then_inc(C["ml"], 1)
                if liveq(i, k - 1):
                    u = k - 1
                    waitq(dve, C["ah"], i, u, 1)
                    nc.vector.tensor_tensor(q_al[:, u % 2], PS[1][:], q_ah[:, u % 2].bitcast(F32), ALU.subtract).then_inc(C["al"], 1)
                if liveq(i, k - 4) and (k - 4) % UNITS >= UNITS - 4:
                    u = k - 4
                    waitp(dve, C["ft"], i, u, 1)
                    pair = i * 4 + (u // UNITS * 4 + u % 4)
                    ts = bass.ds(pair * CT, CT)
                    nc.vector.tensor_tensor(X[:, ts, :], PS[6][:].rearrange("p (t d) -> p t d", d=D), X[:, ts, :], ALU.add).then_inc(C["res"], 1)
                    waitp(dve, C["res"], i, u, 1)
                    for j in range(CT):
                        t = bass.ds(pair * CT + j, 1)
                        ins = token_stats(t, X[:, t, :].rearrange("p a d -> p (a d)"))
                    ins.then_inc(a_stat, 1)
                if liveq(i, k) and k < 3:
                    start_pair(i, k + 1)
                if liveq(i, k - 2):
                    u = k - 2
                    waitq(dve, C["gn"], i, u, 1)
                    waitq(dve, C["r"], i, u, 1)
                    waitq(dve, C["n"], i, u, -1)
                    nc.vector.scalar_tensor_tensor(out=q_t[:, u % 2], in0=PS[4][:], scalar=COLS[:, R_HH + 2:R_HH + 3], in1=q_r[:, u % 2],
                                                   op0=ALU.add, op1=ALU.mult).then_inc(C["t1"], 1)
                    waitq(dve, C["t1"], i, u, 1)
                    nc.vector.tensor_tensor(q_t[:, u % 2], PS[5][:], q_t[:, u % 2], ALU.add).then_inc(C["t2"], 1)
                if liveq(i, k - 3) and (k - 3) % UNITS < UNITS - 4:
                    u = k - 3
                    waitq(dve, C["hh"], i, u + 4, 1)
                    nc.vector.tensor_tensor(q_hl[:, u % 4], q_h[:, u % 4], q_hh[:, u % 4].bitcast(F32), ALU.subtract).then_inc(C["hl"], 1)

            def start_pair(i, u):
                pair = i * 4 + (u // UNITS * 4 + u % 4)
                back = 1 if u % 4 >= 2 else 9
                waitq(dve, C["tr"], i, u, -back)
                waitq(dve, C["mh"], i, u, -back)
                for j in range(CT):
                    t = bass.ds(pair * CT + j, 1)
                    ins = normalise(q_xn[:, u % 2, j][:, None], t, MEAN, RSTD, X[:, t, :])
                ins.then_inc(C["xn"], 1)

            dve.wait_ge(F[0]["st"], CHUNKS)
            finish_stats(3, MEAN, RSTD)
            unit_rounds(dve, 5, gru)
            dve.wait_ge(a_stat, 1 + B + B // 2)
            finish_stats(4, MEAN, RSTD)
            own(dve, nc.vector.tensor_tensor(NT[:, 1], RSTD[:], RSTD[:], ALU.mult))
            own(dve, nc.vector.tensor_tensor(RS2[:], RS2[:], NT[:, 1], ALU.mult))
            own(dve, nc.vector.tensor_scalar(NT[:, 0], RS2[:], EPS, None, ALU.add))
            inverse_root(5, RS2)
            router(1)
            ffn(1)

        @block.tensor
        def _(pe):
            pe.wait_ge(s_ident, 2)
            pe.wait_ge(s_vec, 176)
            nc.tensor.transpose(PS[0][:, 0:R_END], ROWS[:], ident[0:R_END, 0:R_END])
            nc.tensor.transpose(PS[1][:, 0:P], gWr[:], ident[:]).then_inc(s_prep, 1)
            pe.wait_ge(s_prepv, 2)
            nc.tensor.matmul(PS[0][:, 128:130], gWr[:], COLS[:, 0:2], start=True, stop=True).then_inc(s_prep, 1)
            pe.wait_ge(s_gru, 48)
            for i in range(3):
                nc.tensor.transpose(PS[2][:, i * P:(i + 1) * P], rgw[:, i], ident[:])
                nc.tensor.transpose(PS[3][:, i * P:(i + 1) * P], rih[:, i], ident[:])
                ins = nc.tensor.transpose(PS[4][:, i * P:(i + 1) * P], rhh[:, i], ident[:])
            ins.then_inc(s_prep, 1)
            pe.wait_ge(s_prepv, 5)
            for i in range(LAYERS):
                nc.tensor.matmul(PS[5 + i][:, 0:3 * P], gwT[:, i], ihT, start=True, stop=True).then_inc(s_prep, 1)
            pe.wait_ge(s_lo, 7)
            pe.wait_ge(s_const, 11)

            def att_round(base, off):
                if isinstance(base, int) and base == 0 and 2 <= off < 4:
                    j, nb = off - 2, HID1 // P
                    pe.wait_ge(s_raw[j], 16)
                    for n in range(4 * nb):
                        e, k = 4 * j + n // nb, n % nb
                        ins = nc.tensor.matmul(PS[7][:, e * nb + k:e * nb + k + 1], raw(j)[:, n * P:(n + 1) * P],
                                               COLS[:, R_B + e:R_B + e + 1], start=True, stop=True)
                    ins.then_inc(s_bias, 1)
                if isinstance(base, int) and base == 0 and off == 5:
                    pe.wait_ge(s_bx, 2)
                if live(base, off - 1, B):
                    g = off - 1
                    wait(pe, a_norm, base, g + 1)
                    wait(pe, a_e, base, g - 1)
                    for r in range(HALVES):
                        ins = nc.tensor.transpose(PS[g % 2][:, r * P:(r + 1) * P], a_xn[:, g % 2, r], ident[:])
                    ins.then_inc(a_tr, 1)
                if live(base, off - 3, B):
                    g = off - 3
                    wait(pe, a_exp, base, g + 1)
                    wait(pe, a_ptc, base, g - 1)
                    for j in range(HALVES):
                        for r in range(HALVES):
                            ins = nc.tensor.transpose(PS[4 + g % 2][:, j * N + r * P:j * N + (r + 1) * P],
                                                      a_p[:, g % 2, r, j * P:(j + 1) * P], ident[:])
                    ins.then_inc(a_ptr, 1)
                if live(base, off - 4, B):
                    g = off - 4
                    wait(pe, a_ptc, base, g + 1)
                    wait(pe, a_res, base, g - 1)
                    for r in range(HALVES):
                        for j in range(HALVES):
                            ins = nc.tensor.matmul(PS[6 + g % 2][:, r * (D + 1):(r + 1) * (D + 1)],
                                                   a_pT[:, g % 2, j, r * P:(r + 1) * P], a_h[:, g % 4, j],
                                                   start=(j == 0), stop=(j == HALVES - 1))
                    ins.then_inc(a_out, 1)
                if live(base, off - 1, B):
                    g = off - 1
                    wait(pe, a_trc, base, g + 1)
                    wait(pe, a_hc, base, g, 2, -2)
                    for r in range(HALVES):
                        nc.tensor.matmul(PS[2 + g % 2][:, r * (D + 1):(r + 1) * (D + 1)],
                                         a_xT[:, g % 2, r * P:(r + 1) * P], WE[:, 0:D + 1], start=True, stop=True)
                    nc.tensor.matmul(PS[g % 2][:, N:2 * N], wdst[:], a_xT[:, g % 2], start=True, stop=True).then_inc(a_prod, 1)
            rounds(pe, B, 4, 12, att_round)

            def mm3(o, lh, ll, rh, rl, start=True, stop=True):
                nc.tensor.matmul(o, lh, rh, start=start, stop=False)
                nc.tensor.matmul(o, lh, rl, start=False, stop=False)
                return nc.tensor.matmul(o, ll, rh, start=False, stop=stop)

            def router(l):
                r = R[l]

                def chunk(base, off):
                    if live(base, off - 1, CHUNKS):
                        c = off - 1
                        wait(pe, r["norm"], base, c + 1)
                        wait(pe, r["lo"], base, c - 1)
                        for i in range(CT):
                            ins = nc.tensor.transpose(PS[c % 2][:, i * P:(i + 1) * P], f_y[:, c % 4, i], ident[:])
                        ins.then_inc(r["tr"], 1)
                    if live(base, off - 2, CHUNKS):
                        c = off - 2
                        wait(pe, r["lo"], base, c + 1)
                        wait(pe, r["lg"], base, c - 1)
                        for i in range(CT):
                            ins = mm3(PS[2 + c % 2][:, i * E:(i + 1) * E], xTh[:, c % 2, i * P:(i + 1) * P],
                                      xTl[:, c % 2, i * P:(i + 1) * P], wgh[:, l * E:(l + 1) * E], wgl[:, l * E:(l + 1) * E])
                        ins.then_inc(r["log"], 1)
                    if live(base, off - 3, CHUNKS):
                        c = off - 3
                        wait(pe, r["ohr"], base, c + 1)
                        wait(pe, r["pos"], base, c - 1)
                        cols = 2 * CT
                        for j in range(cols + 1):
                            ins = nc.tensor.matmul(PS[4 + c % 2][:, 0:(cols + 1) * E], (ONER if j else TRIR)[:],
                                                   OHR[:, c % 2, (cols - j) * E:(2 * cols - j + 1) * E], start=j == 0, stop=j == cols)
                        ins.then_inc(r["pre"], 1)
                rounds(pe, CHUNKS, 3, 8, chunk)

            def ffn(l):
                f, nb = F[l], NBS[l]
                hid = nb * P

                def block_round(i, off):
                    base = i * V
                    for n in range(nb):
                        if n == 0 and live(base, off, NBLK):
                            waits(pe, d_xb[off % V], i, off, 16, 16 + l * XB_L)
                            wait(pe, f["xlo"], base, off)
                            for j in range(CT):
                                ins = nc.tensor.transpose(PS[6][:, j * P:(j + 1) * P], XB[:, off % V, j, 0:D], ident[:])
                            ins.then_inc(f["tr"], 1)
                        if live(base, off - 1, NBLK):
                            b = off - 1
                            if n == 0:
                                wait(pe, f["xlo"], base, b + 1)
                                waits(pe, d_ws[b % V], i, b, 32, 32 + l * WS_L)
                            wait(pe, f["gelu"], base, b, nb, n - 2)
                            w = WS[:, b % V]
                            mm3(PS[(b * nb + n) % 3][:], w[:, n * P:(n + 1) * P], w[:, 2 * hid + n * P:2 * hid + (n + 1) * P],
                                xTh[:, b % V], xTl[:, b % V]).then_inc(f["h"], 1)
                        if n == 0 and live(base, off - 3, NBLK):
                            b = off - 3
                            wait(pe, f["yev"], base, b + 1)
                            wait(pe, f["wsc"], base, b)
                            for j in range(CT):
                                ins = nc.tensor.transpose(PS[7][:, j * P:(j + 1) * P], f_ye[:, b % V, j * P:(j + 1) * P], ident[:])
                            ins.then_inc(f["yt"], 1)
                        b, m = off - 1 + (n - 2) // nb, (n - 2) % nb
                        if live(base, b, NBLK):
                            wait(pe, f["g"], base, b, 2 * nb, 2 * (m + 1))
                            if m == 0:
                                wait(pe, f["yev"], base, b - V + 1)
                            w = WS[:, b % V]
                            mm3(PS[3 + b % V][:], w[:, hid + m * P:hid + (m + 1) * P], w[:, 3 * hid + m * P:3 * hid + (m + 1) * P],
                                Gh[:, m % 2], Gl[:, m % 2], start=m == 0, stop=m == nb - 1).then_inc(f["yb"], 1)
                block_rounds(pe, 3, block_round)

            router(0)
            ffn(0)

            def gru(i, k):
                w = k % 4
                if liveq(i, k):
                    T = PS[7 * (k % 2)]
                    if k // 4 == 0:
                        waitp(pe, C["xn"], i, k, 1)
                    else:
                        waitq(pe, C["h"], i, k, -3)
                    waitq(pe, C["ml"], i, k, -1)
                    waitq(pe, C["hl"], i, k, -1)
                    for j in range(CT):
                        src = q_xn[:, k % 2, j] if k // 4 == 0 else q_h[:, w, j * P:(j + 1) * P]
                        ins = nc.tensor.transpose(T[:, j * P:(j + 1) * P], src, ident[:])
                    ins.then_inc(C["tr"], 1)
                if liveq(i, k - 4) and (k - 4) % UNITS >= UNITS - 4:
                    u = k - 4
                    waitq(pe, C["h"], i, u, 1)
                    waitp(pe, C["res"], i, u)
                    for j in range(CT):
                        ins = nc.tensor.transpose(PS[6][:, j * P:(j + 1) * P], q_h[:, u % 4, j * P:(j + 1) * P], ident[:])
                    ins.then_inc(C["ft"], 1)
                if liveq(i, k - 1):
                    u = k - 1
                    waitq(pe, C["ml"], i, u, 1)
                    if u // 4 % 3 == 0:
                        waitp(pe, C["adj"], i, u, 1)
                    waitq(pe, C["al"], i, u)
                    for g in range(2):
                        for j in range(HALVES):
                            t = g * HALVES + j
                            for m in (q_mh, q_ml):
                                ins = nc.tensor.matmul(PS[1][:, g * N:(g + 1) * N], m[:, u % 2, t * P:(t + 1) * P], q_A[:, u % 4, t],
                                                       start=j == 0 and m is q_mh, stop=j == 1 and m is q_ml)
                    ins.then_inc(C["ag"], 1)
                if liveq(i, k - 2):
                    u = k - 2
                    lay = u // 4 % LAYERS
                    ai, hi = (q_ah[:, u % 2], q_al[:, u % 2]), (q_hh[:, u % 4], q_hl[:, u % 4])

                    def part(bank, row, rhs, start, stop):
                        return mm3(PS[bank][:], WGH[:, row * P:(row + 1) * P], WGL[:, row * P:(row + 1) * P], *rhs, start, stop)
                    waitq(pe, C["hl"], i, u, 1)
                    waitq(pe, C["r"], i, u)
                    part(2, 9, hi, True, False)
                    waitq(pe, C["al"], i, u, 1)
                    part(2, 3 * lay, ai, False, True).then_inc(C["gr"], 1)
                    waitq(pe, C["z"], i, u)
                    part(3, 10, hi, True, False)
                    part(3, 3 * lay + 1, ai, False, True).then_inc(C["gz"], 1)
                    waitq(pe, C["t2"], i, u)
                    part(4, 11, hi, True, True)
                    part(5, 3 * lay + 2, ai, True, True).then_inc(C["gn"], 1)

            unit_rounds(pe, 5, gru)
            router(1)
            ffn(1)


_INS = ['x', 'adj', 'L0_gnn_W', 'L0_gnn_a_src', 'L0_gnn_a_dst', 'L0_ffn_Wg', 'L0_ffn_bg', 'L0_ffn_W1', 'L0_ffn_b1',
        'L0_ffn_W2', 'L0_ffn_b2', 'L1_gnn_weight', 'L1_gnn_w_ih', 'L1_gnn_w_hh', 'L1_gnn_b_ih', 'L1_gnn_b_hh',
        'L1_ffn_Wr', 'L1_ffn_br', 'L1_ffn_ln_g', 'L1_ffn_ln_b', 'L1_ffn_W1', 'L1_ffn_b1', 'L1_ffn_W2', 'L1_ffn_b2']


def kernel(**inputs):
    import numpy as np
    import concourse.bacc as bacc
    from concourse.bass_utils import run_bass_kernel_spmd

    nc = bacc.Bacc("TRN2", target_bir_lowering=False, num_devices=1)
    arrays, args = {}, []
    for name in _INS:
        a = np.ascontiguousarray(inputs[name])
        arrays[f"in_{name}"] = a
        args.append(nc.dram_tensor(f"in_{name}", a.shape, mybir.dt.from_np(a.dtype), kind="ExternalInput").ap())
    args.append(nc.dram_tensor("out_x", (B, N, D), F32, kind="ExternalOutput").ap())
    build(nc, *args)
    r = run_bass_kernel_spmd(nc, [arrays], core_ids=[0])
    return r.results[0]["out_x"]
```
